# Optimizing a Trainium2 kernel written in Bass

```python
import numpy as np
import jax
import jax.numpy as jnp

def _softmax(x, axis=-1):
    return jax.nn.softmax(x, axis=axis)

def _gelu(x):
    return jax.nn.gelu(x, approximate=True)

def _silu(x):
    return jax.nn.silu(x)

def _sigmoid(x):
    return jax.nn.sigmoid(x)

def _layernorm(x, axis=-1, eps=1e-05):
    m = jnp.mean(x, axis=axis, keepdims=True)
    v = jnp.var(x, axis=axis, keepdims=True)
    return (x - m) / jnp.sqrt(v + eps)

def _scatter_add(tgt, idx, src, axis=0):
    return tgt.at[idx].add(src)

def _segment_sum(src, seg, n):
    return jax.ops.segment_sum(src, seg, n)
kernel_name = 'mk_lm_tower_d1_tok_ids1024_r4_afb59c'

def setup_inputs(seed: int=0):
    np.random.seed(seed)
    _w = jnp.asarray

    def _rec_inputs():
        import jax
        import jax.numpy as jnp
        _rk = jax.random.key(seed)
        x = jax.random.randint(jax.random.fold_in(_rk, 1), (8, 512), 0, 31993, jnp.int32)
        return x
    x = _rec_inputs()

    def _L0_tok_setup():
        import jax, jax.numpy as jnp
        import numpy as np
        VOCAB_SIZE = 8000
        EMBED_DIM = 256

        def _trunc_normal(key, shape, lo=-3.0, hi=3.0):
            return jax.random.truncated_normal(key, lo, hi, shape, dtype=jnp.float32)
        key = jax.random.key(seed)
        k_x, k_w = jax.random.split(key)
        x = jax.random.randint(k_x, (4, 512), 0, VOCAB_SIZE, dtype=jnp.int64 if jax.config.read('jax_enable_x64') else jnp.int32)
        embeddings = _trunc_normal(k_w, (VOCAB_SIZE, EMBED_DIM))
        return {'x': x, 'embeddings': embeddings}
    _L0_tok_all = _L0_tok_setup()
    _L0_tok_in = {k: v for k, v in _L0_tok_all.items() if k in ('embeddings',)}
    del _L0_tok_all

    def _L0_attn_setup():
        import jax, jax.numpy as jnp
        from jax import lax
        import numpy as np
        CHUNK = 64

        def short_conv(x, w):
            L = x.shape[1]
            K = w.shape[1]
            xp = jnp.pad(x, ((0, 0), (K - 1, 0), (0, 0)))
            return sum((xp[:, j:j + L, :] * w[:, j] for j in range(K)))

        def o2b_weighted_delta_rule(k, q, v, b):
            B, L, H, D = k.shape
            C = CHUNK
            Nc = L // C

            def to_chunks(t):
                return t.transpose(0, 2, 1, 3).reshape(B, H, Nc, C, D).transpose(2, 0, 1, 3, 4)
            Kc, Qc, Vc, Bc = map(to_chunks, (k, q, v, b))
            eyeC = jnp.eye(C, dtype=jnp.float32)
            W0 = jnp.zeros((B, H, D, D), jnp.float32)
            Cf = float(C)

            def step(carry, xs):
                W_t, W_avg = carry
                i, Ki, Qi, Vi, Bi = xs
                KiT = jnp.swapaxes(Ki, -1, -2)
                T = jnp.tril(Bi @ KiT, k=-1)
                inv = jnp.linalg.inv(eyeC + T)
                Ui = inv @ (Vi - Bi @ W_t)
                W_new = W_t + KiT @ Ui
                ts = (i * C).astype(jnp.float32)
                idx = jnp.arange(1, C + 1, dtype=jnp.float32) + ts
                cs = jnp.cumsum(idx)
                weighted_idx = idx + idx.sum() - cs
                w_i = (weighted_idx / ((1 + ts + Cf) * (ts + Cf) / 2))[:, None]
                coef1 = ts / (ts + Cf) * ((1 + ts) / (1 + ts + Cf))
                coef2 = Cf / (ts + Cf) * ((ts * 2 + 1 + Cf) / (1 + ts + Cf))
                W_avg_new = coef1 * W_avg + coef2 * W_t + KiT @ (Ui * w_i)
                tri0 = (1 + ts) * ts / 2
                a = (tri0 / (tri0 + cs))[:, None]
                c = 1.0 - a
                r = cs[:, None]
                j_idx = (cs - idx)[None, :]
                T_mat = jnp.where(r >= j_idx, (r - j_idx) / (tri0 + r), 0.0)
                O_i = Qi @ W_avg * a + Qi @ W_t * c + T_mat * (Qi @ KiT) @ Ui
                return ((W_new, W_avg_new), O_i)
            (_, _), O = lax.scan(step, (W0, W0), (jnp.arange(Nc), Kc, Qc, Vc, Bc))
            return O.transpose(1, 2, 0, 3, 4).reshape(B, H, L, D).transpose(0, 2, 1, 3)
        key = jax.random.key(seed)
        ks = jax.random.split(key, 9)
        B, L, Dm, H = (4, 512, 256, 16)
        Dh, K = (Dm // H, 4)
        s = 0.02
        return {'x': jax.random.normal(ks[0], (B, L, Dm), jnp.float32), 'Wk': s * jax.random.normal(ks[1], (Dm, Dm), jnp.float32), 'bk': jnp.zeros((Dm,), jnp.float32), 'Wq': s * jax.random.normal(ks[2], (Dm, Dm), jnp.float32), 'bq': jnp.zeros((Dm,), jnp.float32), 'Wv': s * jax.random.normal(ks[3], (Dm, Dm), jnp.float32), 'bv': jnp.zeros((Dm,), jnp.float32), 'Wbeta': s * jax.random.normal(ks[4], (H, Dm), jnp.float32), 'bbeta': jnp.zeros((H,), jnp.float32), 'conv_k': 0.1 * jax.random.normal(ks[5], (Dm, K), jnp.float32), 'conv_q': 0.1 * jax.random.normal(ks[6], (Dm, K), jnp.float32), 'conv_v': 0.1 * jax.random.normal(ks[7], (Dm, K), jnp.float32), 'rms_w': jnp.ones((Dh,), jnp.float32), 'Wout': s * jax.random.normal(ks[8], (Dm, Dm), jnp.float32), 'bout': jnp.zeros((Dm,), jnp.float32)}
    _L0_attn_all = _L0_attn_setup()
    _L0_attn_in = {k: v for k, v in _L0_attn_all.items() if k in ('Wk', 'bk', 'Wq', 'bq', 'Wv', 'bv', 'Wbeta', 'bbeta', 'conv_k', 'conv_q', 'conv_v', 'rms_w', 'Wout', 'bout')}
    del _L0_attn_all

    def _L0_ffn_setup():
        import jax, jax.numpy as jnp
        import numpy as np
        TOP_K = 2
        E = 8
        D = 256
        F = 512
        B, S = (2, 256)
        key = jax.random.key(seed)
        ks = jax.random.split(key, 8)
        sc = 0.02
        return {'x_bsD': jax.random.normal(ks[0], (B, S, D), dtype=jnp.float32), 'router_DE': jax.random.normal(ks[1], (D, E), dtype=jnp.float32) * sc, 'w_in_shared_FD': jax.random.normal(ks[2], (F, D), dtype=jnp.float32) * sc, 'w_out_shared_DF': jax.random.normal(ks[3], (D, F), dtype=jnp.float32) * sc, 'w_swiglu_FD': jax.random.normal(ks[4], (F, D), dtype=jnp.float32) * sc, 'w_in_eDF': jax.random.normal(ks[5], (E, D, F), dtype=jnp.float32) * sc, 'w_swiglu_eDF': jax.random.normal(ks[6], (E, D, F), dtype=jnp.float32) * sc, 'w_out_eFD': jax.random.normal(ks[7], (E, F, D), dtype=jnp.float32) * sc}
    _L0_ffn_all = _L0_ffn_setup()
    _L0_ffn_in = {k: v for k, v in _L0_ffn_all.items() if k in ('router_DE', 'w_in_shared_FD', 'w_out_shared_DF', 'w_swiglu_FD', 'w_in_eDF', 'w_swiglu_eDF', 'w_out_eFD')}
    del _L0_ffn_all
    return {'x': x, 'L0_tok_embeddings': _L0_tok_in['embeddings'], 'L0_attn_Wk': _L0_attn_in['Wk'], 'L0_attn_bk': _L0_attn_in['bk'], 'L0_attn_Wq': _L0_attn_in['Wq'], 'L0_attn_bq': _L0_attn_in['bq'], 'L0_attn_Wv': _L0_attn_in['Wv'], 'L0_attn_bv': _L0_attn_in['bv'], 'L0_attn_Wbeta': _L0_attn_in['Wbeta'], 'L0_attn_bbeta': _L0_attn_in['bbeta'], 'L0_attn_conv_k': _L0_attn_in['conv_k'], 'L0_attn_conv_q': _L0_attn_in['conv_q'], 'L0_attn_conv_v': _L0_attn_in['conv_v'], 'L0_attn_rms_w': _L0_attn_in['rms_w'], 'L0_attn_Wout': _L0_attn_in['Wout'], 'L0_attn_bout': _L0_attn_in['bout'], 'L0_ffn_router_DE': _L0_ffn_in['router_DE'], 'L0_ffn_w_in_shared_FD': _L0_ffn_in['w_in_shared_FD'], 'L0_ffn_w_out_shared_DF': _L0_ffn_in['w_out_shared_DF'], 'L0_ffn_w_swiglu_FD': _L0_ffn_in['w_swiglu_FD'], 'L0_ffn_w_in_eDF': _L0_ffn_in['w_in_eDF'], 'L0_ffn_w_swiglu_eDF': _L0_ffn_in['w_swiglu_eDF'], 'L0_ffn_w_out_eFD': _L0_ffn_in['w_out_eFD']}

def reference(x, L0_tok_embeddings, L0_attn_Wk, L0_attn_bk, L0_attn_Wq, L0_attn_bq, L0_attn_Wv, L0_attn_bv, L0_attn_Wbeta, L0_attn_bbeta, L0_attn_conv_k, L0_attn_conv_q, L0_attn_conv_v, L0_attn_rms_w, L0_attn_Wout, L0_attn_bout, L0_ffn_router_DE, L0_ffn_w_in_shared_FD, L0_ffn_w_out_shared_DF, L0_ffn_w_swiglu_FD, L0_ffn_w_in_eDF, L0_ffn_w_swiglu_eDF, L0_ffn_w_out_eFD):
    import jax
    import jax.numpy as jnp

    def _L0_tok_ref(x, embeddings):
        import jax, jax.numpy as jnp
        import numpy as np
        VOCAB_SIZE = 8000
        EMBED_DIM = 256

        def _trunc_normal(key, shape, lo=-3.0, hi=3.0):
            return jax.random.truncated_normal(key, lo, hi, shape, dtype=jnp.float32)
        vocab_size = embeddings.shape[0]
        onehot = (x[..., None] == jnp.arange(vocab_size)).astype(embeddings.dtype)
        return jnp.einsum('...v,vd->...d', onehot, embeddings)

    def _L0_attn_ref(x, Wk, bk, Wq, bq, Wv, bv, Wbeta, bbeta, conv_k, conv_q, conv_v, rms_w, Wout, bout):
        import jax, jax.numpy as jnp
        from jax import lax
        import numpy as np
        CHUNK = 64

        def short_conv(x, w):
            L = x.shape[1]
            K = w.shape[1]
            xp = jnp.pad(x, ((0, 0), (K - 1, 0), (0, 0)))
            return sum((xp[:, j:j + L, :] * w[:, j] for j in range(K)))

        def o2b_weighted_delta_rule(k, q, v, b):
            B, L, H, D = k.shape
            C = CHUNK
            Nc = L // C

            def to_chunks(t):
                return t.transpose(0, 2, 1, 3).reshape(B, H, Nc, C, D).transpose(2, 0, 1, 3, 4)
            Kc, Qc, Vc, Bc = map(to_chunks, (k, q, v, b))
            eyeC = jnp.eye(C, dtype=jnp.float32)
            W0 = jnp.zeros((B, H, D, D), jnp.float32)
            Cf = float(C)

            def step(carry, xs):
                W_t, W_avg = carry
                i, Ki, Qi, Vi, Bi = xs
                KiT = jnp.swapaxes(Ki, -1, -2)
                T = jnp.tril(Bi @ KiT, k=-1)
                inv = jnp.linalg.inv(eyeC + T)
                Ui = inv @ (Vi - Bi @ W_t)
                W_new = W_t + KiT @ Ui
                ts = (i * C).astype(jnp.float32)
                idx = jnp.arange(1, C + 1, dtype=jnp.float32) + ts
                cs = jnp.cumsum(idx)
                weighted_idx = idx + idx.sum() - cs
                w_i = (weighted_idx / ((1 + ts + Cf) * (ts + Cf) / 2))[:, None]
                coef1 = ts / (ts + Cf) * ((1 + ts) / (1 + ts + Cf))
                coef2 = Cf / (ts + Cf) * ((ts * 2 + 1 + Cf) / (1 + ts + Cf))
                W_avg_new = coef1 * W_avg + coef2 * W_t + KiT @ (Ui * w_i)
                tri0 = (1 + ts) * ts / 2
                a = (tri0 / (tri0 + cs))[:, None]
                c = 1.0 - a
                r = cs[:, None]
                j_idx = (cs - idx)[None, :]
                T_mat = jnp.where(r >= j_idx, (r - j_idx) / (tri0 + r), 0.0)
                O_i = Qi @ W_avg * a + Qi @ W_t * c + T_mat * (Qi @ KiT) @ Ui
                return ((W_new, W_avg_new), O_i)
            (_, _), O = lax.scan(step, (W0, W0), (jnp.arange(Nc), Kc, Qc, Vc, Bc))
            return O.transpose(1, 2, 0, 3, 4).reshape(B, H, L, D).transpose(0, 2, 1, 3)
        B, L, Dm = x.shape
        H = Wbeta.shape[0]
        Dh = Dm // H
        k = short_conv(x @ Wk.T + bk, conv_k)
        q = short_conv(x @ Wq.T + bq, conv_q)
        v = short_conv(x @ Wv.T + bv, conv_v)
        beta = jax.nn.sigmoid(x @ Wbeta.T + bbeta)
        k = k.reshape(B, L, H, Dh)
        q = q.reshape(B, L, H, Dh)
        v = jax.nn.silu(v.reshape(B, L, H, Dh))
        knorm = jnp.linalg.norm(k, axis=-1, keepdims=True)
        qnorm = jnp.linalg.norm(q, axis=-1, keepdims=True)
        k = k / (knorm + 1e-06)
        q = q / (qnorm + 1e-06)
        eta = beta
        b = eta[..., None] * k
        v = eta[..., None] * v
        o = o2b_weighted_delta_rule(k, q, v, b)
        o = o * jax.lax.rsqrt(jnp.mean(o * o, axis=-1, keepdims=True) + 1e-06) * rms_w
        o = o.reshape(B, L, Dm)
        return o @ Wout.T + bout

    def _L0_ffn_ref(x_bsD, router_DE, w_in_shared_FD, w_out_shared_DF, w_swiglu_FD, w_in_eDF, w_swiglu_eDF, w_out_eFD):
        import jax, jax.numpy as jnp
        import numpy as np
        TOP_K = 2
        E = 8
        D = 256
        F = 512
        B, S = (2, 256)
        b, s, d = x_bsD.shape
        x_aD = x_bsD.reshape(-1, d)
        a = x_aD.shape[0]
        scores_aE = x_aD @ router_DE
        topv_aK, topi_aK = jax.lax.top_k(scores_aE, TOP_K)
        masked_aE = jnp.full_like(scores_aE, -jnp.inf)
        masked_aE = masked_aE.at[jnp.arange(a)[:, None], topi_aK].set(topv_aK)
        gates_Ea = jax.nn.sigmoid(masked_aE.astype(jnp.float32)).astype(x_aD.dtype).T
        routed_in_EaD = x_aD[None, :, :] * gates_Ea[:, :, None]
        routed_in_EaD = jax.lax.stop_gradient(routed_in_EaD)
        mid_EaF = jnp.einsum('ead,edf->eaf', routed_in_EaD, w_in_eDF)
        sw_EaF = jnp.einsum('ead,edf->eaf', routed_in_EaD, w_swiglu_eDF)
        h_EaF = jax.nn.silu(mid_EaF) * sw_EaF
        out_EaD = jnp.einsum('eaf,efd->ead', h_EaF, w_out_eFD)
        shared_aF = jax.nn.silu(x_aD @ w_in_shared_FD.T) * (x_aD @ w_swiglu_FD.T)
        shared_out_aD = jax.lax.stop_gradient(shared_aF @ w_out_shared_DF.T)
        out_aD = shared_out_aD + jnp.sum(out_EaD, axis=0)
        return out_aD.reshape(b, s, d)
    h = _L0_tok_ref(x, L0_tok_embeddings)
    h = h + _L0_attn_ref(_layernorm(h, axis=-1), L0_attn_Wk, L0_attn_bk, L0_attn_Wq, L0_attn_bq, L0_attn_Wv, L0_attn_bv, L0_attn_Wbeta, L0_attn_bbeta, L0_attn_conv_k, L0_attn_conv_q, L0_attn_conv_v, L0_attn_rms_w, L0_attn_Wout, L0_attn_bout)
    h = h + _L0_ffn_ref(_layernorm(h, axis=-1), L0_ffn_router_DE, L0_ffn_w_in_shared_FD, L0_ffn_w_out_shared_DF, L0_ffn_w_swiglu_FD, L0_ffn_w_in_eDF, L0_ffn_w_swiglu_eDF, L0_ffn_w_out_eFD)
    return h

_drawn_inputs = setup_inputs


def setup_inputs(seed=0):
    import zlib

    import numpy as np

    out = dict(_drawn_inputs(seed))
    spreads = {'L0_attn_bk': (0.0, 0.1),
     'L0_attn_bq': (0.0, 0.1),
     'L0_attn_bv': (0.0, 0.1),
     'L0_attn_bbeta': (0.0, 0.651),
     'L0_attn_rms_w': (1.0, 0.2),
     'L0_attn_bout': (0.0, 0.1)}
    factors = {'L0_ffn_router_DE': 3.234,
     'L0_ffn_w_in_eDF': 2.78,
     'L0_ffn_w_swiglu_eDF': 2.81,
     'L0_ffn_w_out_eFD': 2.784}
    for name, (base, spread) in spreads.items():
        noise = np.random.default_rng([zlib.crc32(name.encode()), seed]).standard_normal(out[name].shape)
        drawn = base * np.exp(spread * noise) if base else spread * noise
        out[name] = jnp.asarray(drawn.astype(out[name].dtype))
    for name, factor in factors.items():
        out[name] = (out[name] * factor).astype(out[name].dtype)
    return out
```

```python
from contextlib import ExitStack

import numpy as np
import concourse.bass as bass
from concourse import mybir

P = 128
B, L, D = 8, 512, 256
H, DH = 16, 16
C = 32
TILES = L // P
NT = B * TILES
CH = P // C
KH = D // P
VOCAB = 8000
E, F = 8, 512
FK = F // P
TAPS = 4
HP = H // 2
NC_BATCH = L // C
ROW = 2 * C

F32 = mybir.dt.float32
I32 = mybir.dt.int32
U32 = mybir.dt.uint32
ALU = mybir.AluOpType
ACT = mybir.ActivationFunctionType
AX = mybir.AxisListType.X


class Chain:

    def __init__(self, eng, sem, base=0):
        self.eng, self.sem, self.base, self.n = eng, sem, base, 0

    def did(self, ins):
        ins.then_inc(self.sem, 1)
        self.n += 1
        return self.n

    def wait(self, n=None):
        self.eng.wait_ge(self.sem, self.base + (self.n if n is None else n) + 1)


def wait_apart(dve, tick, sem, value):
    dve.wait_ge(sem, value + 1)
    dve.memset(tick, 0.0)


def consts():
    tri = lambda n: n * (n + 1) / 2.0
    p = np.arange(P)
    where, parts, at = {}, [], 0

    def add(name, a):
        nonlocal at
        a = np.asarray(a, np.float64).reshape(P, -1)
        where[name] = (at, a.shape[1])
        parts.append(a)
        at += a.shape[1]

    add("ident", np.eye(P))
    add("headblock", (p[:, None] // DH) == (p[None, :] // DH))
    add("parity", np.stack([(p // DH) % 2 == k for k in range(2)], 1))
    m = np.zeros((P, TILES, P))
    for t in range(TILES):
        i = t * P + p[None, :] + 1.0
        j = t * P + p[:, None] + 1.0
        m[:, t, :] = np.where(j <= i, (tri(i) - tri(j - 1)) / tri(i), 0.0)
    add("average", m)
    n = np.arange(TILES)[None, :] * P + p[:, None] + 1.0
    add("tri_before", tri(n - 1))
    add("minus_tri_inverse", -1.0 / tri(n))
    row = np.arange(32)
    fwd = np.zeros((P, 2, KH, 32))
    back = np.zeros((P, TILES, 2, KH, P))
    for u in range(2):
        for m in range(KH):
            fwd[:, u, m, :] = row[None, :] == (H * u + (m * P + p[:, None]) // DH)
            for t in range(TILES):
                back[:, t, u, m, :] = p[:, None] == (32 * t + H * u + (m * P + p[None, :]) // DH)
    add("to_heads", fwd)
    add("to_channels", back)
    k = np.arange(C)
    add("unit", np.broadcast_to((k[:, None, None] == k[None, None, :]) * np.ones((1, 2, 1)), (P, C, 2, C)))
    add("experts", np.broadcast_to(np.arange(E), (P, E)))
    return np.concatenate(parts, 1).astype(np.float32), where


def build(nc, ids, emb, wqkv, wbeta, wout, router, conv_w, qkv_b, bbeta, bout, rms, const, w_in, w_sw, w_out, out,
          where):
    n_dram = nc.dram_tensor("chunk_gram_dram", [B, HP, L, ROW], F32, kind="Internal").ap()
    x_dram = nc.dram_tensor("chunk_inverse_dram", [B, HP, L, ROW], F32, kind="Internal").ap()
    kT_dram = nc.dram_tensor("k_channels_dram", [B, P, KH * L], F32, kind="Internal").ap()
    qT_dram = nc.dram_tensor("q_channels_dram", [B, P, KH * L], F32, kind="Internal").ap()
    k_dram = nc.dram_tensor("k_tokens_dram", [B, P, TILES * D], F32, kind="Internal").ap()
    bv_dram = nc.dram_tensor("beta_kv_dram", [B, P, TILES * 2 * D], F32, kind="Internal").ap()
    xn_dram = nc.dram_tensor("ffn_input_dram", [NT, P, D], F32, kind="Internal").ap()

    made = []
    with ExitStack() as top:
        def sb(ctx, name, shape, dt=F32):
            return ctx.enter_context(nc.sbuf_tensor(name, shape, dt))

        def ps(ctx, name, shape):
            return ctx.enter_context(nc.psum_tensor(name, shape, F32))

        def sem(ctx, name):
            made.append(ctx.enter_context(nc.semaphore(name)))
            return made[-1]

        def start_at_one():
            with nc.Block() as block:
                @block.sync
                def _(sp):
                    for s in made:
                        sp.sem_inc(s, 1)
            made.clear()

        h = sb(top, "h", [P, NT, D])
        gates = sb(top, "gates", [P, NT, E])
        cst = sb(top, "cst", [P, const.shape[1]])

        def table(name):
            a, n = where[name]
            return cst[:, a:a + n]

        ident = table("ident")
        headblock = table("headblock")

        with ExitStack() as ctx:
            ids_sb = sb(ctx, "ids_sb", [P, NT], I32)
            wqkv_sb = sb(ctx, "wqkv_sb", [P, KH, 3, D])
            wbeta_sb = sb(ctx, "wbeta_sb", [P, KH, H])
            conv_sb = sb(ctx, "conv_sb", [P, 3, KH, TAPS])
            qkvb_sb = sb(ctx, "qkvb_sb", [P, 3, KH])
            bbeta_sb = sb(ctx, "bbeta_sb", [P, H])
            xhat = sb(ctx, "xhat", [P, TILES, D])
            stats = sb(ctx, "stats", [P, NT, 6])
            mv = sb(ctx, "mv", [P, NT, 2])
            std = sb(ctx, "std", [P, NT])
            rstd = sb(ctx, "rstd", [P, NT])
            xT = sb(ctx, "xT", [P, KH, L])
            raw = sb(ctx, "raw", [P, 3, KH, L + TAPS - 1])
            cv = sb(ctx, "cv", [P, 3, KH, L])
            sq = sb(ctx, "sq", [P, 2, KH, L])
            norm = sb(ctx, "norm", [P, P])
            rnorm = sb(ctx, "rnorm", [P, P])
            th = sb(ctx, "th", [P, TILES, H])
            kT = sb(ctx, "kT", [P, KH, L])
            qT = sb(ctx, "qT", [P, KH, L])
            kM = sb(ctx, "kM", [P, KH, 2, L])
            lin = sb(ctx, "lin", [P, TILES, H])
            eta = sb(ctx, "eta", [P, TILES, H])
            neta = sb(ctx, "neta", [P, TILES, H])
            k_tok = sb(ctx, "k_tok", [P, TILES, D])
            v_tok = sb(ctx, "v_tok", [P, TILES, D])
            bv = sb(ctx, "bv", [P, TILES, H, 2, DH])
            ng = sb(ctx, "ng", [P, TILES, HP, ROW])
            nx = sb(ctx, "nx", [P, C, 2, C])
            xt = sb(ctx, "xt", [P, C, 2, C])
            prod = sb(ctx, "prod", [P, (C - 1) * 2 * (C - 1)])

            p_t = [ps(ctx, f"p_t{i}", [P, L]) for i in range(2)]
            p_p = [ps(ctx, f"p_p{i}", [P, L]) for i in range(2)]
            p_g = [ps(ctx, f"p_g{i}", [P, TILES, 2, ROW]) for i in range(4)]
            p_n = [p_g[i][:].rearrange("p t g x -> p (t g x)") for i in range(2)]

            s_ids, s_w, s_zero = (sem(ctx, n) for n in ("ids_in", "weights_in", "h_zeroed"))
            s_emb = ctx.enter_context(nc.semaphore("embedded"))
            s_pad = sem(ctx, "pad_zeroed")
            s_chain = sem(ctx, "vector_chain_a")
            s_xhat = sem(ctx, "xhat_ready")
            s_xtr = sem(ctx, "x_transposed")
            s_xT = sem(ctx, "xT_ready")
            s_bps = sem(ctx, "beta_summed")
            s_lin = sem(ctx, "beta_biased")
            s_eta = sem(ctx, "eta_ready")
            s_proj = sem(ctx, "projected")
            s_raw = sem(ctx, "raw_ready")
            s_cv = sem(ctx, "convolved")
            s_sq = sem(ctx, "squared")
            s_nsum = sem(ctx, "norms_summed")
            s_var = sem(ctx, "variance_ready")
            s_std = sem(ctx, "std_ready")
            s_norm = sem(ctx, "norms_ready")
            s_rn = sem(ctx, "inverse_norms_ready")
            s_nb = sem(ctx, "inverse_norms_spread")
            s_pre = sem(ctx, "vector_chain_setup")
            to_heads = table("to_heads").rearrange("p (n r) -> p n r", r=32)
            to_channels = table("to_channels").rearrange("p (t n r) -> p t n r", t=TILES, r=P)
            s_nrm = sem(ctx, "normalized")
            s_km = sem(ctx, "k_masked")
            s_ttr = sem(ctx, "kv_transposed")
            s_kt = sem(ctx, "k_tokens_ready")
            s_vt = sem(ctx, "v_tokens_ready")
            s_bv = sem(ctx, "beta_kv_ready")
            s_gram = sem(ctx, "gram_summed")
            s_ng = sem(ctx, "gram_scaled")
            s_ngst = sem(ctx, "gram_stored")
            s_st = sem(ctx, "kv_stored")
            s_nx = sem(ctx, "gram_loaded")
            s_xst = sem(ctx, "inverse_stored")
            s_inv = sem(ctx, "inverse_ready")

            CHAIN_A = 6 * (TAPS - 1) + 1 + 2 + 1 + 2 * (C - 1) - 1

            start_at_one()
            with nc.Block() as block:
                @block.sync
                def _(sp):
                    sp.dma_start(ids_sb[:], ids).then_inc(s_ids, 16)
                    for dst, src in ((cst[:], const), (wqkv_sb[:], wqkv), (wbeta_sb[:], wbeta), (conv_sb[:], conv_w),
                                     (qkvb_sb[:], qkv_b), (bbeta_sb[:], bbeta)):
                        sp.dma_start(dst, src).then_inc(s_w, 16)
                    with sp.Fori(0, B) as b:
                        sp.wait_ge(s_nrm, b * 4 + 5)
                        sp.dma_start(kT_dram[b], kT[:].rearrange("p k l -> p (k l)")).then_inc(s_st, 16)
                        sp.dma_start(qT_dram[b], qT[:].rearrange("p k l -> p (k l)")).then_inc(s_st, 16)
                        sp.wait_ge(s_kt, b * 2 + 3)
                        sp.dma_start(k_dram[b], k_tok[:].rearrange("p t d -> p (t d)")).then_inc(s_st, 16)
                        sp.wait_ge(s_bv, b * 4 + 5)
                        sp.dma_start(bv_dram[b], bv[:].rearrange("p t h u d -> p (t h u d)")).then_inc(s_st, 16)
                        sp.wait_ge(s_inv, b + 1)
                        sp.wait_ge(s_ng, b * 8 + 9)
                        for t in range(TILES):
                            sp.dma_start(n_dram[b, :, t * P:(t + 1) * P, :].rearrange("g p x -> p g x"),
                                         ng[:, t]).then_inc(s_ngst, 16)
                        sp.wait_ge(s_ngst, b * 64 + 65)
                        sp.dma_start(nx[:].rearrange("p i g j -> p (i g j)"),
                                     n_dram[b].rearrange("g (c i) x -> (g c) (i x)", i=C)).then_inc(s_nx, 16)
                        sp.wait_ge(s_inv, b + 2)
                        sp.dma_start(x_dram[b].rearrange("g (c i) x -> (g c) (i x)", i=C),
                                     xt[:].rearrange("p i g j -> p (i g j)")).then_inc(s_xst, 16)
                    sp.wait_ge(s_st, 64 * B + 1)
                    sp.wait_ge(s_xst, 16 * B + 1)

                @block.gpsimd
                def _(pool):
                    pool.memset(h[:], 0.0).then_inc(s_zero, 1)
                    pool.wait_ge(s_zero, 1 + 1)
                    pool.wait_ge(s_ids, 16 + 1)
                    for t in range(NT):
                        pool.indirect_dma_start(h[:, t, :], None, emb, bass.IndirectOffsetOnAxis(ids_sb[:, t:t + 1].bitcast(U32), 0),
                                                bounds_check=VOCAB - 1, oob_is_err=False).then_inc(s_emb, 16)
                    pool.wait_ge(s_emb, 16 * NT)

                @block.tensor
                def _(pe):
                    pe.wait_ge(s_w, 16 * 6 + 1)
                    with pe.Fori(0, B) as b:
                        for k in range(KH):
                            if k == 0:
                                pe.wait_ge(s_vt, b * 2 + 1)
                            for t in range(TILES):
                                pe.wait_ge(s_xhat, b * TILES + t + 2)
                                ins = pe.transpose(p_t[k][:, t * P:(t + 1) * P], xhat[:, t, k * P:(k + 1) * P], ident)
                            ins.then_inc(s_xtr, 1)
                        pe.wait_ge(s_xT, b * KH + KH + 1)
                        pe.wait_ge(s_ng, b * 8 + 1)
                        for t in range(TILES):
                            for k in range(KH):
                                ins = pe.matmul(p_n[0][:, t * H:(t + 1) * H], xT[:, k, t * P:(t + 1) * P],
                                                wbeta_sb[:, k, :], start=(k == 0), stop=(k == KH - 1))
                        ins.then_inc(s_bps, 1)
                        for p in range(3):
                            for m in range(KH):
                                n = p * KH + m
                                pe.wait_ge(s_raw, b * 6 + max(n - 1, 0) + 1)
                                for k in range(KH):
                                    ins = pe.matmul(p_p[n % 2][:], wqkv_sb[:, k, p, m * P:(m + 1) * P], xT[:, k, :],
                                                    start=(k == 0), stop=(k == KH - 1))
                                ins.then_inc(s_proj, 1)
                        pe.wait_ge(s_lin, b + 2)
                        pe.wait_ge(s_sq, b * 4 + 5)
                        for t in range(TILES):
                            for n in range(4):
                                ins = pe.matmul(p_n[0][32 * t:32 * t + 32, 0:P], to_heads[:, n, :],
                                                sq[:, n // KH, n % KH, t * P:(t + 1) * P], start=(n == 0), stop=(n == 3))
                        ins.then_inc(s_nsum, 1)
                        pe.wait_ge(s_rn, b + 2)
                        for n in range(4):
                            if n >= 2:
                                pe.wait_ge(s_nrm, b * 4 + n - 1 + 1)
                            for t in range(TILES):
                                ins = pe.matmul(p_n[(n + 1) % 2][:, t * P:(t + 1) * P], to_channels[:, t, n, :], rnorm[:],
                                                start=True, stop=True)
                            ins.then_inc(s_nb, 1)
                        pe.wait_ge(s_nrm, b * 4 + 3)
                        for u in range(4):
                            if u >= 2:
                                pe.wait_ge(s_cv, b * 6 + 7)
                                pe.wait_ge(s_nrm, b * 4 + 5)
                                pe.wait_ge(s_km, b * KH * 2 + KH * 2 + 1)
                                pe.wait_ge(s_kt, b * 2 + u - 1 + 1)
                                pe.wait_ge(s_bv, b * 4 + u - 1 + 1)
                            for s in range(4):
                                t, k = 2 * (u % 2) + s // 2, s % 2
                                src = kT[:, k, t * P:(t + 1) * P] if u < 2 else cv[:, 2, k, t * P:(t + 1) * P]
                                ins = pe.transpose(p_t[u % 2][:, s * P:(s + 1) * P], src, ident)
                            ins.then_inc(s_ttr, 1)
                        for t in range(TILES):
                            for c in range(CH):
                                tok = slice(t * P + c * C, t * P + (c + 1) * C)
                                for g in range(HP):
                                    r = slice(32 * (g % 4), 32 * (g % 4) + 32)
                                    ins = pe.matmul(p_g[g % 4][c * C:(c + 1) * C, t, g // 4, :],
                                                    kT[r, g // 4, tok], kM[r, g // 4, :, tok], start=True, stop=True)
                        ins.then_inc(s_gram, 1)

                @block.scalar
                def _(act):
                    act.wait_ge(s_w, 16 * 6 + 1)
                    act.wait_ge(s_var, 1 + 1)
                    act.activation(std[:], std[:], ACT.Sqrt).then_inc(s_std, 1)
                    with act.Fori(0, B) as b:
                        for k in range(KH):
                            act.wait_ge(s_xtr, b * KH + k + 2)
                            act.copy(xT[:, k, :], p_t[k][:]).then_inc(s_xT, 1)
                        for n in range(6):
                            act.wait_ge(s_proj, b * 6 + n + 2)
                            act.wait_ge(s_cv, b * 6 + 1)
                            act.activation(raw[:, n // KH, n % KH, TAPS - 1:], p_p[n % 2][:], ACT.Identity,
                                           bias=qkvb_sb[:, n // KH, n % KH:n % KH + 1]).then_inc(s_raw, 1)
                        for n in range(4):
                            act.wait_ge(s_cv, b * 6 + n + 2)
                            act.activation(sq[:, n // KH, n % KH, :], cv[:, n // KH, n % KH, :],
                                           ACT.Square).then_inc(s_sq, 1)
                        act.wait_ge(s_nsum, b + 2)
                        act.activation(norm[:], p_n[0][:, 0:P], ACT.Sqrt).then_inc(s_norm, 1)
                        act.wait_ge(s_lin, b + 2)
                        act.activation(th[:], lin[:], ACT.Tanh, scale=0.5).then_inc(s_eta, 1)
                        act.wait_ge(s_nrm, b * 4 + 3)
                        act.wait_ge(s_gram, b + 1)
                        for k in range(KH):
                            for e in range(2):
                                a, _n = where["parity"]
                                act.activation(kM[:, k, e, :], kT[:, k, :], ACT.Copy,
                                               scale=cst[:, a + e:a + e + 1]).then_inc(s_km, 1)
                        act.wait_ge(s_st, b * 64 + 1)
                        for u in range(2):
                            act.wait_ge(s_ttr, b * 4 + u + 2)
                            act.copy(k_tok[:, 2 * u:2 * u + 2, :].rearrange("p t d -> p (t d)"),
                                     p_t[u][:]).then_inc(s_kt, 1)
                        for u in range(2):
                            act.wait_ge(s_ttr, b * 4 + u + 4)
                            act.activation(v_tok[:, 2 * u:2 * u + 2, :].rearrange("p t d -> p (t d)"), p_t[u][:],
                                           ACT.Silu).then_inc(s_vt, 1)

                @block.vector
                def _(dve):
                    dve.memset(raw[:, :, :, 0:TAPS - 1], 0.0).then_inc(s_pad, 1)
                    dve.wait_ge(s_w, 16 * 6 + 1)
                    pre = Chain(dve, s_pre)
                    dve.wait_ge(s_emb, 16 * NT)
                    for t in range(NT):
                        pre.did(dve.bn_stats(stats[:, t, :], h[:, t, :]))
                    for t in range(NT):
                        pre.wait(t + 1)
                        pre.did(dve.bn_aggr(mv[:, t, :], stats[:, t, :]))
                    pre.wait()
                    dve.tensor_scalar(std[:], mv[:, :, 1], 1e-5, None, ALU.add).then_inc(s_var, 1)
                    dve.wait_ge(s_std, 1 + 1)
                    pre.did(dve.reciprocal(rstd[:], std[:]))
                    pre.wait()
                    with dve.Fori(0, B) as b:
                        link = Chain(dve, s_chain, b * CHAIN_A)
                        dve.wait_ge(s_xtr, b * KH + 1)
                        for t in range(TILES):
                            dve.tensor_scalar(xhat[:, t, :], h[:, b * TILES + t, :], mv[:, b * TILES + t, 0:1],
                                              rstd[:, bass.ds(b * TILES + t, 1)],
                                              ALU.subtract, ALU.mult).then_inc(s_xhat, 1)
                        dve.wait_ge(s_bps, b + 2)
                        dve.tensor_tensor(lin[:], p_n[0][:, 0:TILES * H].rearrange("p (t h) -> p t h", t=TILES),
                                          bbeta_sb[:].unsqueeze(1).to_broadcast([P, TILES, H]), ALU.add).then_inc(s_lin, 1)
                        for n in range(6):
                            p, m = n // KH, n % KH
                            if n == 0:
                                dve.wait_ge(s_ttr, b * 4 + 1)
                            dve.wait_ge(s_raw, b * 6 + n + 2)
                            for j in range(TAPS):
                                w = conv_sb[:, p, m, j:j + 1]
                                x = raw[:, p, m, j:j + L]
                                if j == 0:
                                    ins = dve.tensor_scalar(cv[:, p, m, :], x, w, None, ALU.mult)
                                else:
                                    link.wait()
                                    ins = dve.scalar_tensor_tensor(cv[:, p, m, :], x, w, cv[:, p, m, :], ALU.mult, ALU.add)
                                if j < TAPS - 1:
                                    link.did(ins)
                                else:
                                    ins.then_inc(s_cv, 1)
                        dve.wait_ge(s_norm, b + 2)
                        link.did(dve.tensor_scalar(norm[:], norm[:], 1e-6, None, ALU.add))
                        link.wait()
                        dve.reciprocal(rnorm[:], norm[:]).then_inc(s_rn, 1)
                        dve.wait_ge(s_eta, b + 2)
                        link.did(dve.tensor_scalar(eta[:], th[:], 0.5, 0.5, ALU.mult, ALU.add))
                        link.did(dve.tensor_scalar(neta[:], th[:], -0.5, -0.5, ALU.mult, ALU.add))
                        dve.wait_ge(s_st, b * 64 + 1)
                        dve.wait_ge(s_gram, b + 1)
                        for n in range(4):
                            dst = (kT, qT)[n // KH]
                            dve.wait_ge(s_nb, b * 4 + n + 2)
                            dve.tensor_tensor(dst[:, n % KH, :], cv[:, n // KH, n % KH, :], p_n[(n + 1) % 2],
                                              ALU.mult).then_inc(s_nrm, 1)
                        link.wait()
                        for u in range(4):
                            t = slice(2 * (u % 2), 2 * (u % 2) + 2)
                            dve.wait_ge(s_kt if u < 2 else s_vt, b * 2 + u % 2 + 2)
                            src = (k_tok if u < 2 else v_tok)[:, t, :].rearrange("p t (h d) -> p t h d", d=DH)
                            dve.tensor_tensor(bv[:, t, :, u // 2, :].rearrange("p t h d -> p (t h) d"),
                                              src.rearrange("p t h d -> p (t h) d"),
                                              eta[:, t, :].rearrange("p t h -> p (t h)").unsqueeze(2).to_broadcast([P, 2 * H, DH]),
                                              ALU.mult).then_inc(s_bv, 1)
                        dve.wait_ge(s_ngst, b * 64 + 1)
                        dve.wait_ge(s_gram, b + 2)
                        for g in range(HP):
                            dve.tensor_tensor(ng[:, :, g, :].rearrange("p t (e j) -> p t e j", e=2),
                                              p_g[g % 4][:, :, g // 4, :].rearrange("p t (e j) -> p t e j", e=2),
                                              neta[:, :, 2 * g:2 * g + 2].unsqueeze(3).to_broadcast([P, TILES, 2, C]),
                                              ALU.mult).then_inc(s_ng, 1)
                        dve.wait_ge(s_xst, b * 16 + 1)
                        link.did(dve.tensor_copy(xt[:].rearrange("p k e i -> p (k e i)"), table("unit")))
                        dve.wait_ge(s_nx, b * 16 + 17)
                        for i in range(1, C):
                            link.wait()
                            pr = prod[:, 0:i * 2 * i].rearrange("p (k e j) -> p k e j", e=2, j=i)
                            link.did(dve.tensor_tensor(pr, nx[:, i, :, 0:i].unsqueeze(1).to_broadcast([P, i, 2, i]),
                                                       xt[:, 0:i, :, 0:i], ALU.mult))
                            link.wait()
                            ins = dve.tensor_reduce(xt[:, 0:i, :, i], pr, AX, ALU.add)
                            if i < C - 1:
                                link.did(ins)
                            else:
                                ins.then_inc(s_inv, 1)
                        assert link.n == CHAIN_A, link.n

        with ExitStack() as ctx:
            wout_sb = sb(ctx, "wout_sb", [P, KH, D])
            router_sb = sb(ctx, "router_sb", [P, KH, E])
            bout_sb = sb(ctx, "bout_sb", [P, D])
            rms_sb = sb(ctx, "rms_sb", [P, 1])
            kT = sb(ctx, "kTb", [P, KH, L])
            qT = sb(ctx, "qTb", [P, KH, L])
            qM = sb(ctx, "qM", [P, KH, 2, L])
            k_tok = sb(ctx, "k_tok_b", [P, TILES, D])
            bv = sb(ctx, "bv_b", [P, TILES, H, 2 * DH])
            xbd = [sb(ctx, f"xbd{i}", [P, HP, 2, P]) for i in range(2)]
            st = [sb(ctx, f"st{i}", [P, H, P]) for i in range(2)]
            y_tok = sb(ctx, "y_tok", [P, D])
            z_tok = [sb(ctx, f"z_tok{i}", [P, D]) for i in range(2)]
            yT = [sb(ctx, f"yT{i}", [P, KH, P]) for i in range(2)]
            u = sb(ctx, "u", [P, D])
            uw = sb(ctx, "uw", [P, D])
            w_bd = sb(ctx, "w_bd", [P, KH, P])
            d_bd = sb(ctx, "d_bd", [P, KH, P])
            od = sb(ctx, "od", [P, D])
            o = sb(ctx, "o", [P, D])
            osq = sb(ctx, "osq", [P, D])
            oms = sb(ctx, "oms", [P, H])
            orms = sb(ctx, "orms", [P, H])
            on = sb(ctx, "on", [P, D])
            oT = sb(ctx, "oT", [P, KH, P])
            hb = sb(ctx, "hb", [P, D])
            stats = sb(ctx, "stats_b", [P, 6])
            mv = sb(ctx, "mv_b", [P, 2])
            std = sb(ctx, "std_b", [P, 1])
            rstd = sb(ctx, "rstd_b", [P, 1])
            xn = sb(ctx, "xn", [P, D])
            xnT = sb(ctx, "xnT", [P, KH, P])
            score = sb(ctx, "score", [P, E])
            best = sb(ctx, "best", [P, 8])
            best_at = sb(ctx, "best_at", [P, 8], U32)
            best_f = sb(ctx, "best_f", [P, 2])
            pick = sb(ctx, "pick", [P, E])
            tick = sb(ctx, "tick", [P, 1])

            p_yz = ps(ctx, "p_yz", [P, H, 2 * DH])
            p_tr = ps(ctx, "p_tr", [P, L])
            p_r = ps(ctx, "p_r", [P, L])
            p_acc = ps(ctx, "p_acc", [P, 2, KH, P])
            p_st = [ps(ctx, f"p_st{i}", [P, KH, 2, P]) for i in range(2)]
            p_o = ps(ctx, "p_o", [P, 2, KH, P])
            p_out = ps(ctx, "p_out", [P, L])

            names = ("b_weights", "batch_loaded", "xbd_zeroed", "xbd_loaded0", "xbd_loaded1", "q_masked", "yz_summed", "yz_out",
                     "y_transposed", "yT_ready", "weights_summed", "weights_masked", "state_cleared", "old_reads",
                     "od_ready", "r_summed", "u_ready", "w_summed", "w_ready", "uw_ready", "d_summed", "d_ready",
                     "o_summed", "o_ready", "o_squared", "on_ready", "o_transposed", "oT_ready", "out_projected",
                     "hb_ready", "xn_ready", "xn_stored", "xn_transposed", "xnT_ready", "scored", "score_copied",
                     "oms_ready", "orms_ready", "var_ready", "std_ready", "all_scored", "all_sigmoid", "picked", "vector_chain_b")
            S = {n: sem(ctx, "b_" + n) for n in names}
            CHAIN_B = TILES * (2 + 4 + 5)
            scores = sb(ctx, 'scores', [P, NT, E])

            start_at_one()
            with nc.Block() as block:
                @block.sync
                def _(sp):
                    for dst, src in ((wout_sb[:], wout), (router_sb[:], router), (bout_sb[:], bout), (rms_sb[:], rms)):
                        sp.dma_start(dst, src).then_inc(S["b_weights"], 16)
                    sp.wait_ge(S["xbd_zeroed"], 2 + 1)
                    with sp.Fori(0, B) as b:
                        sp.wait_ge(S["o_summed"], b * TILES + 1)
                        sp.wait_ge(S["d_summed"], b * TILES + 1)
                        sp.wait_ge(S["q_masked"], b * 4 + 1)
                        for dst, src in ((kT[:].rearrange("p k l -> p (k l)"), kT_dram[b]),
                                         (qT[:].rearrange("p k l -> p (k l)"), qT_dram[b]),
                                         (k_tok[:].rearrange("p t d -> p (t d)"), k_dram[b]),
                                         (bv[:].rearrange("p t h d -> p (t h d)"), bv_dram[b])):
                            sp.dma_start(dst, src).then_inc(S["batch_loaded"], 16)
                        for t in range(TILES):
                            sp.wait_ge(S["yz_summed"], b * TILES + max(t - 1, 0) + 1)
                            for c in range(CH):
                                for g in range(HP):
                                    sp.dma_start(xbd[t % 2][c * C:(c + 1) * C, g, :, c * C:(c + 1) * C],
                                                 x_dram[b, g, t * P + c * C:t * P + (c + 1) * C, :].rearrange(
                                                     "p (e i) -> p e i", e=2)).then_inc(S[f"xbd_loaded{t % 2}"], 16)

                @block.gpsimd
                def _(pool):
                    for i in range(2):
                        pool.memset(xbd[i][:], 0.0).then_inc(S["xbd_zeroed"], 1)
                    pool.wait_ge(S["b_weights"], 64 + 1)
                    with pool.Fori(0, B) as b:
                        def residual(t):
                            pool.wait_ge(S["xn_ready"], b * TILES + t + 1)
                            pool.tensor_tensor(hb[:], h[:, b * TILES + t, :], bout_sb[:], ALU.add).then_inc(S["hb_ready"], 1)

                        for t in range(TILES):
                            if t:
                                residual(t - 1)
                            pool.wait_ge(S["u_ready"], b * NC_BATCH + (t + 1) * CH + 1)
                            pool.wait_ge(S["d_summed"], b * TILES + t + 1)
                            a, _n = where["tri_before"]
                            pool.tensor_tensor(uw[:], u[:], cst[:, a + t:a + t + 1].to_broadcast([P, D]),
                                               ALU.mult).then_inc(S["uw_ready"], 1)
                        residual(TILES - 1)

                @block.tensor
                def _(pe):
                    pe.wait_ge(S["b_weights"], 64 + 1)
                    with pe.Fori(0, B) as b:
                        def tile0(t):
                            return b * TILES + t

                        def yz(t):
                            pe.wait_ge(S[f"xbd_loaded{t % 2}"], (b * (TILES // 2) + t // 2 + 1) * 16 * CH * HP + 1)
                            pe.wait_ge(S["yz_out"], tile0(t) * 2 + 1)
                            for hd in range(H):
                                ins = pe.matmul(p_yz[:, hd, :], xbd[t % 2][:, hd // 2, hd % 2, :], bv[:, t, hd, :],
                                                start=True, stop=True)
                            ins.then_inc(S["yz_summed"], 1)

                        def y_transpose(t):
                            pe.wait_ge(S["yz_out"], tile0(t) * 2 + 3)
                            pe.wait_ge(S["yT_ready"], b * TILES + t + 1)
                            pe.wait_ge(S["xnT_ready"], b * TILES + max(t - 2, 0) + 1)
                            for k in range(KH):
                                ins = pe.transpose(p_tr[:, k * P:(k + 1) * P], y_tok[:, k * P:(k + 1) * P], ident)
                            ins.then_inc(S["y_transposed"], 1)

                        def weights(t, n):
                            pe.wait_ge(S["weights_masked"], tile0(t) * 4 + n if t or n else b * TILES * 4 + 1)
                            r = slice(32 * n, 32 * n + 32)
                            for k in range(KH):
                                ins = pe.matmul(p_st[n % 2][:, k, :, :], kT[r, k, t * P:(t + 1) * P],
                                                qM[r, k, :, t * P:(t + 1) * P], start=True, stop=True)
                            ins.then_inc(S["weights_summed"], 1)

                        def old_reads(t):
                            pe.wait_ge(S["o_ready"], tile0(t) + 1)
                            pe.wait_ge(S["w_ready"], b * NC_BATCH + t * CH + 1)
                            pe.wait_ge(S["d_ready"], tile0(t) + 1)
                            pe.wait_ge(S["state_cleared"], b + 2)
                            for n, state in enumerate((w_bd, d_bd)):
                                for k in range(KH):
                                    ins = pe.matmul(p_o[:, n, k, :], qT[:, k, t * P:(t + 1) * P], state[:, k, :],
                                                    start=(n == 0 and k == 0), stop=False, skip_group_check=True)
                            ins.then_inc(S["old_reads"], 1)

                        def recur_r(t, c):
                            n = b * NC_BATCH + t * CH + c
                            pe.wait_ge(S["w_ready"], n + 1)
                            pe.wait_ge(S["u_ready"], n + 1)
                            if c == 0:
                                pe.wait_ge(S["yT_ready"], tile0(t) + 2)
                            for k in range(KH):
                                ins = pe.matmul(p_r[c * C:(c + 1) * C, k * P:(k + 1) * P], yT[t % 2][:, k, c * C:(c + 1) * C],
                                                w_bd[:, k, :], start=True, stop=True)
                            ins.then_inc(S["r_summed"], 1)

                        def recur_w(t, c):
                            pe.wait_ge(S["u_ready"], b * NC_BATCH + t * CH + c + 2)
                            if c == 0:
                                pe.wait_ge(S["d_ready"], tile0(t) + 1)
                            for k in range(KH):
                                ins = pe.matmul(p_acc[:, 0, k, :], k_tok[c * C:(c + 1) * C, t, k * P:(k + 1) * P],
                                                u[c * C:(c + 1) * C, k * P:(k + 1) * P],
                                                start=(t == 0 and c == 0 and k == 0), stop=False, skip_group_check=True)
                            ins.then_inc(S["w_summed"], 1)

                        def average(t):
                            pe.wait_ge(S["uw_ready"], tile0(t) + 2)
                            pe.wait_ge(S["w_ready"], b * NC_BATCH + (t + 1) * CH + 1)
                            for k in range(KH):
                                ins = pe.matmul(p_acc[:, 1, k, :], k_tok[:, t, k * P:(k + 1) * P], uw[:, k * P:(k + 1) * P],
                                                start=False, stop=False, skip_group_check=True)
                            ins.then_inc(S["d_summed"], 1)

                        def new_reads(t):
                            pe.wait_ge(S["od_ready"], tile0(t) + 2)
                            pe.wait_ge(S["weights_masked"], tile0(t) * 4 + 5)
                            for hd in range(H):
                                ins = pe.matmul(p_o[:, 0, hd // 8, (hd % 8) * DH:(hd % 8 + 1) * DH], st[t % 2][:, hd, :],
                                                u[:, hd * DH:(hd + 1) * DH], start=False, stop=(hd == H - 1),
                                                skip_group_check=True)
                            ins.then_inc(S["o_summed"], 1)

                        def o_transpose(t):
                            pe.wait_ge(S["on_ready"], tile0(t) + 2)
                            pe.wait_ge(S["yT_ready"], b * TILES + min(t + 3, TILES) + 1)
                            pe.wait_ge(S["xnT_ready"], b * TILES + t + 1)
                            for k in range(KH):
                                ins = pe.transpose(p_tr[:, k * P:(k + 1) * P], on[:, k * P:(k + 1) * P], ident)
                            ins.then_inc(S["o_transposed"], 1)

                        def project(t):
                            pe.wait_ge(S["oT_ready"], tile0(t) + 2)
                            pe.wait_ge(S["score_copied"], tile0(t) + 1)
                            for k in range(KH):
                                ins = pe.matmul(p_out[:, 0:D], oT[:, k, :], wout_sb[:, k, :], start=(k == 0), stop=(k == KH - 1))
                            ins.then_inc(S["out_projected"], 1)

                        def xn_transpose(t):
                            pe.wait_ge(S["xn_ready"], tile0(t) + 2)
                            for k in range(KH):
                                ins = pe.transpose(p_tr[:, k * P:(k + 1) * P], xn[:, k * P:(k + 1) * P], ident)
                            ins.then_inc(S["xn_transposed"], 1)

                        def route(t):
                            pe.wait_ge(S["xnT_ready"], tile0(t) + 2)
                            for k in range(KH):
                                ins = pe.matmul(p_out[:, D:D + E], xnT[:, k, :], router_sb[:, k, :], start=(k == 0), stop=(k == KH - 1))
                            ins.then_inc(S["scored"], 1)

                        pe.wait_ge(S["batch_loaded"], b * 64 + 65)
                        yz(0)
                        y_transpose(0)
                        pe.wait_ge(S["q_masked"], b * 4 + 5)
                        for n in range(4):
                            weights(0, n)
                        for t in range(TILES):
                            nxt, last = t + 1 < TILES, t > 0
                            old_reads(t)
                            recur_r(t, 0)
                            if nxt:
                                yz(t + 1)
                            recur_w(t, 0)
                            recur_r(t, 1)
                            if nxt:
                                y_transpose(t + 1)
                                weights(t + 1, 0)
                            recur_w(t, 1)
                            recur_r(t, 2)
                            if nxt:
                                weights(t + 1, 1)
                            if last:
                                o_transpose(t - 1)
                            recur_w(t, 2)
                            recur_r(t, 3)
                            if nxt:
                                weights(t + 1, 2)
                            if last:
                                project(t - 1)
                            recur_w(t, 3)
                            if nxt:
                                weights(t + 1, 3)
                            average(t)
                            new_reads(t)
                            if last:
                                xn_transpose(t - 1)
                                route(t - 1)
                        o_transpose(TILES - 1)
                        project(TILES - 1)
                        xn_transpose(TILES - 1)
                        route(TILES - 1)

                @block.scalar
                def _(act):
                    act.wait_ge(S["b_weights"], 64 + 1)
                    with act.Fori(0, B) as b:
                        def tile0(t):
                            return b * TILES + t

                        def yz_out(t):
                            act.wait_ge(S["yz_summed"], tile0(t) + 2)
                            act.wait_ge(S["y_transposed"], tile0(t) + 1)
                            act.copy(y_tok[:].rearrange("p (h d) -> p h d", d=DH), p_yz[:, :, 0:DH]).then_inc(S["yz_out"], 1)
                            act.wait_ge(S["u_ready"], b * NC_BATCH + max(t - 1, 0) * CH + 1)
                            act.copy(z_tok[t % 2][:].rearrange("p (h d) -> p h d", d=DH),
                                     p_yz[:, :, DH:2 * DH]).then_inc(S["yz_out"], 1)

                        def yT_out(t):
                            act.wait_ge(S["y_transposed"], tile0(t) + 2)
                            act.wait_ge(S["r_summed"], b * NC_BATCH + max(t - 1, 0) * CH + 1)
                            act.copy(yT[t % 2][:].rearrange("p k l -> p (k l)"), p_tr[:, 0:D]).then_inc(S["yT_ready"], 1)

                        def od_out(t):
                            act.wait_ge(S["old_reads"], tile0(t) + 2)
                            act.wait_ge(S["o_ready"], tile0(t) + 1)
                            a, _n = where["minus_tri_inverse"]
                            act.activation(od[:], p_o[:, 1, :, :].rearrange("p k l -> p (k l)"), ACT.Copy,
                                           scale=cst[:, a + t:a + t + 1]).then_inc(S["od_ready"], 1)

                        def square(t):
                            act.wait_ge(S["o_ready"], tile0(t) + 2)
                            act.activation(osq[:], o[:], ACT.Square).then_inc(S["o_squared"], 1)

                        def head_sqrt(t):
                            act.wait_ge(S["oms_ready"], tile0(t) + 2)
                            act.activation(orms[:], oms[:], ACT.Sqrt).then_inc(S["orms_ready"], 1)

                        def row_sqrt(t):
                            act.wait_ge(S["var_ready"], tile0(t) + 2)
                            act.activation(std[:], rstd[:], ACT.Sqrt).then_inc(S["std_ready"], 1)

                        def oT_out(t):
                            act.wait_ge(S["o_transposed"], tile0(t) + 2)
                            act.activation(oT[:].rearrange("p k l -> p (k l)"), p_tr[:, 0:D], ACT.Copy,
                                           scale=rms_sb[:, 0:1]).then_inc(S["oT_ready"], 1)

                        def xnT_out(t):
                            act.wait_ge(S["xn_ready"], tile0(t) + 2)
                            act.dma_start(xn_dram[b * TILES + t], xn[:]).then_inc(S["xn_stored"], 16)
                            act.wait_ge(S["xn_transposed"], tile0(t) + 2)
                            act.copy(xnT[:].rearrange("p k l -> p (k l)"), p_tr[:, 0:D]).then_inc(S["xnT_ready"], 1)

                        act.wait_ge(S["batch_loaded"], b * 64 + 65)
                        yz_out(0)
                        yT_out(0)
                        for k in range(KH):
                            for e in range(2):
                                a, _n = where["parity"]
                                act.activation(qM[:, k, e, :], qT[:, k, :], ACT.Copy,
                                               scale=cst[:, a + e:a + e + 1]).then_inc(S["q_masked"], 1)
                        for t in range(TILES):
                            od_out(t)
                            if t:
                                head_sqrt(t - 1)
                            if t + 1 < TILES:
                                yz_out(t + 1)
                                yT_out(t + 1)
                            if t:
                                oT_out(t - 1)
                                row_sqrt(t - 1)
                            square(t)
                            if t:
                                xnT_out(t - 1)
                        head_sqrt(TILES - 1)
                        oT_out(TILES - 1)
                        row_sqrt(TILES - 1)
                        xnT_out(TILES - 1)
                    act.wait_ge(S["xn_stored"], 16 * NT + 1)
                    act.wait_ge(S["all_scored"], NT + 1)
                    act.activation(scores[:], scores[:], ACT.Sigmoid).then_inc(S["all_sigmoid"], 1)

                @block.vector
                def _(dve):
                    dve.wait_ge(S["b_weights"], 64 + 1)
                    with dve.Fori(0, B) as b:
                        link = Chain(dve, S["vector_chain_b"], b * CHAIN_B)

                        def tile0(t):
                            return b * TILES + t

                        def update(t, c):
                            r = slice(c * C, (c + 1) * C)
                            n = b * NC_BATCH + t * CH + c
                            dve.wait_ge(S["r_summed"], n + 2)
                            if c == 0:
                                dve.wait_ge(S["yz_out"], tile0(t) * 2 + 3)
                                dve.wait_ge(S["o_summed"], tile0(t) + 1)
                                dve.wait_ge(S["uw_ready"], tile0(t) + 1)
                            dve.tensor_tensor(u[r, :], z_tok[t % 2][r, :], p_r[r, 0:D], ALU.subtract).then_inc(S["u_ready"], 1)
                            dve.wait_ge(S["w_summed"], n + 2)
                            dve.tensor_tensor(w_bd[:], p_acc[:, 0], headblock.unsqueeze(1).to_broadcast([P, KH, P]),
                                              ALU.mult).then_inc(S["w_ready"], 1)

                        def mask(t, n):
                            dve.wait_ge(S["weights_summed"], tile0(t) * 4 + n + 2)
                            if n == 0:
                                dve.wait_ge(S["o_summed"], b * TILES + max(t - 1, 0) + 1)
                            a, _n = where["average"]
                            dve.tensor_tensor(st[t % 2][:].rearrange("p (k h) i -> p k h i", k=KH)[:, :, 2 * n:2 * n + 2, :],
                                              p_st[n % 2][:],
                                              cst[:, a + t * P:a + (t + 1) * P].unsqueeze(1).unsqueeze(1).to_broadcast(
                                                  [P, KH, 2, P]),
                                              ALU.mult).then_inc(S["weights_masked"], 1)

                        def read_out(t):
                            dve.wait_ge(S["o_summed"], tile0(t) + 2)
                            dve.wait_ge(S["od_ready"], tile0(t) + 2)
                            dve.tensor_tensor(o[:], p_o[:, 0, :, :].rearrange("p k l -> p (k l)"), od[:],
                                              ALU.add).then_inc(S["o_ready"], 1)

                        def head_norm(t):
                            dve.wait_ge(S["o_squared"], tile0(t) + 2)
                            link.did(dve.tensor_reduce(oms[:], osq[:].rearrange("p (h d) -> p h d", d=DH), AX, ALU.add))
                            link.wait()
                            dve.tensor_scalar(oms[:], oms[:], 1.0 / DH, 1e-6, ALU.mult, ALU.add).then_inc(S["oms_ready"], 1)
                            dve.wait_ge(S["orms_ready"], tile0(t) + 2)
                            link.did(dve.reciprocal(oms[:], orms[:]))
                            link.wait()
                            dve.tensor_tensor(on[:].rearrange("p (h d) -> p h d", d=DH), o[:].rearrange("p (h d) -> p h d", d=DH),
                                              oms[:].unsqueeze(2).to_broadcast([P, H, DH]), ALU.mult).then_inc(S["on_ready"], 1)

                        def residual_norm(t):
                            dve.wait_ge(S["out_projected"], tile0(t) + 2)
                            dve.wait_ge(S["hb_ready"], tile0(t) + 2)
                            dve.wait_ge(S["xn_stored"], tile0(t) * 16 + 1)
                            hh = h[:, b * TILES + t, :]
                            link.did(dve.tensor_tensor(hh, p_out[:, 0:D], hb[:], ALU.add))
                            wait_apart(dve, tick[:], link.sem, link.base + link.n)
                            link.did(dve.bn_stats(stats[:], hh))
                            wait_apart(dve, tick[:], link.sem, link.base + link.n)
                            link.did(dve.bn_aggr(mv[:], stats[:]))
                            link.wait()
                            dve.tensor_scalar(rstd[:], mv[:, 1:2], 1e-5, None, ALU.add).then_inc(S["var_ready"], 1)
                            dve.wait_ge(S["std_ready"], tile0(t) + 2)
                            link.did(dve.reciprocal(rstd[:], std[:]))
                            link.wait()
                            dve.tensor_scalar(xn[:], hh, mv[:, 0:1], rstd[:, 0:1], ALU.subtract, ALU.mult).then_inc(S["xn_ready"], 1)

                        def copy_score(t):
                            dve.wait_ge(S["scored"], tile0(t) + 2)
                            dve.tensor_copy(score[:], p_out[:, D:D + E]).then_inc(S["score_copied"], 1)
                            dve.wait_ge(S["score_copied"], tile0(t) + 2)
                            dve.tensor_copy(scores[:, b * TILES + t, :], score[:]).then_inc(S["all_scored"], 1)

                        def gate(t):
                            wait_apart(dve, tick[:], S["score_copied"], tile0(t) + 1)
                            link.did(dve.max(best[:], score[:]))
                            wait_apart(dve, tick[:], link.sem, link.base + link.n)
                            link.did(dve.max_index(best_at[:], best[:], score[:]))
                            link.wait()
                            link.did(dve.tensor_copy(best_f[:], best_at[:, 0:2]))
                            link.wait()
                            link.did(dve.tensor_scalar(pick[:], table("experts"), best_f[:, 0:1], None, ALU.is_equal))
                            link.wait()
                            link.did(dve.scalar_tensor_tensor(gates[:, b * TILES + t, :], table("experts"), best_f[:, 1:2],
                                                              pick[:], ALU.is_equal, ALU.add))

                        dve.wait_ge(S["old_reads"], b * TILES + 1)
                        dve.wait_ge(S["r_summed"], b * NC_BATCH + 1)
                        dve.memset(w_bd[:], 0.0)
                        dve.memset(d_bd[:], 0.0).then_inc(S["state_cleared"], 1)
                        for n in range(4):
                            mask(0, n)
                        for t in range(TILES):
                            nxt, last = t + 1 < TILES, t > 0
                            update(t, 0)
                            if last:
                                head_norm(t - 1)
                            update(t, 1)
                            if nxt:
                                mask(t + 1, 0)
                            update(t, 2)
                            if nxt:
                                mask(t + 1, 1)
                            update(t, 3)
                            if nxt:
                                mask(t + 1, 2)
                            if last:
                                residual_norm(t - 1)
                            dve.wait_ge(S["d_summed"], tile0(t) + 2)
                            dve.tensor_tensor(d_bd[:], p_acc[:, 1], headblock.unsqueeze(1).to_broadcast([P, KH, P]),
                                              ALU.mult).then_inc(S["d_ready"], 1)
                            if nxt:
                                mask(t + 1, 3)
                            read_out(t)
                            if last:
                                copy_score(t - 1)
                                gate(t - 1)
                        head_norm(TILES - 1)
                        residual_norm(TILES - 1)
                        copy_score(TILES - 1)
                        gate(TILES - 1)
                        assert link.n == CHAIN_B, link.n
                    dve.wait_ge(S["all_sigmoid"], 1 + 1)
                    dve.wait_ge(S["vector_chain_b"], B * CHAIN_B + 1)
                    dve.tensor_tensor(gates[:], gates[:], scores[:], ALU.mult).then_inc(S["picked"], 1)
                    dve.wait_ge(S["picked"], 1 + 1)

        with ExitStack() as ctx:
            NE = E + 1
            wi = sb(ctx, "wi", [P, NE, KH, F])
            ws = sb(ctx, "ws", [P, NE, KH, F])
            wo = sb(ctx, "wo", [P, NE, FK, D])
            xn = sb(ctx, "xn_c", [P, D])
            xnT = sb(ctx, "xnT_c", [P, KH, P])
            act_sb = [sb(ctx, f"act{i}", [P, F]) for i in range(2)]
            hid = [sb(ctx, f"hid{i}", [P, F]) for i in range(2)]
            hidT = [sb(ctx, f"hidT{i}", [P, FK, P]) for i in range(2)]
            gate1 = sb(ctx, "gate1", [P, NE])
            res = sb(ctx, "res", [P, D])

            p_i = [ps(ctx, f"p_i{i}", [P, F]) for i in range(2)]
            p_s = [ps(ctx, f"p_s{i}", [P, F]) for i in range(2)]
            p_h = [ps(ctx, f"p_h{i}", [P, FK, P]) for i in range(2)]
            p_x = ps(ctx, "p_x", [P, KH, P])
            p_y = ps(ctx, "p_y", [P, D])

            names = ("w", "x", "xtr", "xT", "up", "silu", "hid", "htr", "hidT", "down", "gate", "res", "out", "one")
            S = {n: sem(ctx, "c_" + n) for n in names}

            start_at_one()
            with nc.Block() as block:
                @block.sync
                def _(sp):
                    for dst, src in ((wi, w_in), (ws, w_sw), (wo, w_out)):
                        for e in range(NE):
                            sp.dma_start(dst[:, e], src[e]).then_inc(S["w"], 16)
                    with sp.Fori(0, NT) as t:
                        sp.wait_ge(S["xtr"], t + 1)
                        sp.dma_start(xn[:], xn_dram[t]).then_inc(S["x"], 16)
                        sp.wait_ge(S["res"], t + 2)
                        sp.dma_start(out[t], res[:]).then_inc(S["out"], 16)
                    sp.wait_ge(S["out"], 16 * NT + 1)

                @block.tensor
                def _(pe):
                    pe.wait_ge(S["w"], 16 * 3 * NE + 1)
                    with pe.Fori(0, NT) as t:
                        pe.wait_ge(S["x"], t * 16 + 17)
                        for k in range(KH):
                            ins = pe.transpose(p_x[:, k, :], xn[:, k * P:(k + 1) * P], ident)
                        ins.then_inc(S["xtr"], 1)
                        pe.wait_ge(S["xT"], t + 2)
                        for s in range(NE + 2):
                            if s < NE:
                                if s >= 2:
                                    pe.wait_ge(S["silu"], t * NE + s - 1 + 1)
                                    pe.wait_ge(S["hid"], t * NE + s - 1 + 1)
                                else:
                                    pe.wait_ge(S["hid"], t * NE + 1)
                                for w, p in ((wi, p_i), (ws, p_s)):
                                    for k in range(KH):
                                        ins = pe.matmul(p[s % 2][:], xnT[:, k, :], w[:, s, k, :], start=(k == 0), stop=(k == KH - 1))
                                    ins.then_inc(S["up"], 1)
                            if 1 <= s <= NE:
                                e = s - 1
                                pe.wait_ge(S["hid"], t * NE + e + 2)
                                pe.wait_ge(S["hidT"], t * NE + max(e - 1, 0) + 1)
                                for f in range(FK):
                                    ins = pe.transpose(p_h[e % 2][:, f, :], hid[e % 2][:, f * P:(f + 1) * P], ident)
                                ins.then_inc(S["htr"], 1)
                            if s >= 2:
                                e = s - 2
                                if e == 0:
                                    pe.wait_ge(S["res"], t + 1)
                                pe.wait_ge(S["hidT"], t * NE + e + 2)
                                for f in range(FK):
                                    ins = pe.matmul(p_y[:], hidT[e % 2][:, f, :], wo[:, e, f, :], start=(e == 0 and f == 0),
                                                    stop=(e == NE - 1 and f == FK - 1))
                                ins.then_inc(S["down"], 1)

                @block.scalar
                def _(act):
                    with act.Fori(0, NT) as t:
                        act.wait_ge(S["gate"], t + 2)
                        act.wait_ge(S["xtr"], t + 2)
                        act.wait_ge(S["down"], t * NE + 1)
                        act.copy(xnT[:], p_x[:]).then_inc(S["xT"], 1)
                        for s in range(NE + 1):
                            if s < NE:
                                act.wait_ge(S["up"], (t * NE + s) * 2 + 2)
                                act.wait_ge(S["hid"], t * NE + max(s - 1, 0) + 1)
                                act.activation(act_sb[s % 2][:], p_i[s % 2][:], ACT.Silu,
                                               scale=gate1[:, s:s + 1]).then_inc(S["silu"], 1)
                            if s >= 1:
                                e = s - 1
                                act.wait_ge(S["htr"], t * NE + e + 2)
                                act.wait_ge(S["down"], t * NE + max(e - 1, 0) + 1)
                                act.copy(hidT[e % 2][:], p_h[e % 2][:]).then_inc(S["hidT"], 1)

                @block.vector
                def _(dve):
                    dve.memset(gate1[:, E:NE], 1.0).then_inc(S["one"], 1)
                    dve.wait_ge(S["one"], 1 + 1)
                    with dve.Fori(0, NT) as t:
                        dve.wait_ge(S["silu"], t * NE + 1)
                        dve.tensor_copy(gate1[:, 0:E], gates[:, t, :]).then_inc(S["gate"], 1)
                        dve.wait_ge(S["gate"], t + 2)
                        for e in range(NE):
                            dve.wait_ge(S["silu"], t * NE + e + 2)
                            dve.wait_ge(S["up"], (t * NE + e) * 2 + 3)
                            dve.wait_ge(S["htr"], t * NE + max(e - 1, 0) + 1)
                            dve.scalar_tensor_tensor(hid[e % 2][:], p_s[e % 2][:], gate1[:, e:e + 1], act_sb[e % 2][:],
                                                     ALU.mult, ALU.mult).then_inc(S["hid"], 1)
                        dve.wait_ge(S["down"], t * NE + NE + 1)
                        dve.wait_ge(S["out"], t * 16 + 1)
                        dve.tensor_tensor(res[:], p_y[:], h[:, t, :], ALU.add).then_inc(S["res"], 1)


def lay_out(a):
    k, n = a.shape
    return np.ascontiguousarray(a.reshape(k // P, P, n).transpose(1, 0, 2))


def kernel(**inputs):
    import concourse.bacc as _bacc
    from concourse.bass_utils import run_bass_kernel_spmd as _run

    x = {k: np.asarray(v) for k, v in inputs.items()}
    a, f = "L0_attn_", "L0_ffn_"
    const, where = consts()
    qkv = ("k", "q", "v")
    arrays = {
        "ids": np.ascontiguousarray(x["x"].reshape(NT, P).T),
        "emb": x["L0_tok_embeddings"],
        "wqkv": np.stack([lay_out(x[f"{a}W{n}"].T) for n in qkv], 2),
        "wbeta": lay_out(x[a + "Wbeta"].T),
        "wout": lay_out(x[a + "Wout"].T),
        "router": lay_out(x[f + "router_DE"]),
        "conv_w": np.stack([lay_out(x[f"{a}conv_{n}"]) for n in qkv], 1),
        "qkv_b": np.stack([x[f"{a}b{n}"].reshape(KH, P).T for n in qkv], 1),
        "bbeta": np.broadcast_to(x[a + "bbeta"], (P, H)),
        "bout": np.broadcast_to(x[a + "bout"], (P, D)),
        "rms": np.tile(x[a + "rms_w"], P // DH).reshape(P, 1),
        "const": const,
        "w_in": np.stack([lay_out(w) for w in (*x[f + "w_in_eDF"], x[f + "w_in_shared_FD"].T)]),
        "w_sw": np.stack([lay_out(w) for w in (*x[f + "w_swiglu_eDF"], x[f + "w_swiglu_FD"].T)]),
        "w_out": np.stack([lay_out(w) for w in (*x[f + "w_out_eFD"], x[f + "w_out_shared_DF"].T)]),
    }
    arrays = {n: np.ascontiguousarray(v) for n, v in arrays.items()}
    nc = _bacc.Bacc("TRN2", target_bir_lowering=False, num_devices=1)
    args = [nc.dram_tensor(f"in_{n}", v.shape, mybir.dt.from_np(v.dtype), kind="ExternalInput").ap()
            for n, v in arrays.items()]
    out = nc.dram_tensor("out_h", [NT, P, D], F32, kind="ExternalOutput").ap()
    build(nc, *args, out, where)
    r = _run(nc, [{f"in_{n}": v for n, v in arrays.items()}], core_ids=[0])
    return r.results[0]["out_h"].reshape(B, L, D)
```

```python
from contextlib import ExitStack

import numpy as np
import concourse.bass as bass
from concourse import mybir

P = 128
B, L, D = 8, 512, 256
H, DH = 16, 16
C = 32
TILES = L // P
NT = B * TILES
CH = P // C
KH = D // P
VOCAB = 8000
E, F = 8, 512
FK = F // P
TAPS = 4
HP = H // 2
NC_BATCH = L // C
TOP = 2
SLOTS = TOP * B * L // P + E - 1
ROW = 2 * C

F32 = mybir.dt.float32
I32 = mybir.dt.int32
U32 = mybir.dt.uint32
ALU = mybir.AluOpType
ACT = mybir.ActivationFunctionType
AX = mybir.AxisListType.X


class Chain:

    def __init__(self, eng, sem, base=0):
        self.eng, self.sem, self.base, self.n = eng, sem, base, 0

    def did(self, ins):
        ins.then_inc(self.sem, 1)
        self.n += 1
        return self.n

    def wait(self, n=None):
        self.eng.wait_ge(self.sem, self.base + (self.n if n is None else n) + 1)


def wait_apart(dve, tick, sem, value):
    dve.wait_ge(sem, value + 1)
    dve.memset(tick, 0.0)


def consts():
    tri = lambda n: n * (n + 1) / 2.0
    p = np.arange(P)
    where, parts, at = {}, [], 0

    def add(name, a):
        nonlocal at
        a = np.asarray(a, np.float64).reshape(P, -1)
        where[name] = (at, a.shape[1])
        parts.append(a)
        at += a.shape[1]

    add("ident", np.eye(P))
    add("headblock", (p[:, None] // DH) == (p[None, :] // DH))
    add("parity", np.stack([(p // DH) % 2 == k for k in range(2)], 1))
    m = np.zeros((P, TILES, P))
    for t in range(TILES):
        i = t * P + p[None, :] + 1.0
        j = t * P + p[:, None] + 1.0
        m[:, t, :] = np.where(j <= i, (tri(i) - tri(j - 1)) / tri(i), 0.0)
    add("average", m)
    n = np.arange(TILES)[None, :] * P + p[:, None] + 1.0
    add("tri_before", tri(n - 1))
    add("minus_tri_inverse", -1.0 / tri(n))
    row = np.arange(32)
    fwd = np.zeros((P, 2, KH, 32))
    back = np.zeros((P, TILES, 2, KH, P))
    for u in range(2):
        for m in range(KH):
            fwd[:, u, m, :] = row[None, :] == (H * u + (m * P + p[:, None]) // DH)
            for t in range(TILES):
                back[:, t, u, m, :] = p[:, None] == (32 * t + H * u + (m * P + p[None, :]) // DH)
    add("to_heads", fwd)
    add("to_channels", back)
    k = np.arange(C)
    add("unit", np.broadcast_to((k[:, None, None] == k[None, None, :]) * np.ones((1, 2, 1)), (P, C, 2, C)))
    add("before", p[:, None] < p[None, :])
    add("ones", np.ones((P, P)))
    add("slot", np.broadcast_to(np.arange(SLOTS) * P, (P, SLOTS)))
    add("zeros_nt", np.zeros((P, NT)))
    add("experts", np.broadcast_to(np.arange(E), (P, E)))
    return np.concatenate(parts, 1).astype(np.float32), where


def build(nc, ids, emb, wqkv, wbeta, wout, router, conv_w, qkv_b, bbeta, bout, rms, const, w_in, w_sw, w_out, out,
          where):
    n_dram = nc.dram_tensor("chunk_gram_dram", [B, HP, L, ROW], F32, kind="Internal").ap()
    x_dram = nc.dram_tensor("chunk_inverse_dram", [B, L, H * C], F32, kind="Internal").ap()
    kT_dram = nc.dram_tensor("k_channels_dram", [B, P, KH * L], F32, kind="Internal").ap()
    qT_dram = nc.dram_tensor("q_channels_dram", [B, P, KH * L], F32, kind="Internal").ap()
    k_dram = nc.dram_tensor("k_tokens_dram", [B, P, TILES * D], F32, kind="Internal").ap()
    bv_dram = nc.dram_tensor("beta_kv_dram", [B, P, TILES * 2 * D], F32, kind="Internal").ap()
    xs_dram = nc.dram_tensor("slots_in_dram", [(SLOTS + 1) * P, D], F32, kind="Internal").ap()
    ys_dram = nc.dram_tensor("slots_out_dram", [SLOTS * P, D], F32, kind="Internal").ap()
    xn_dram = nc.dram_tensor("ffn_input_dram", [NT, P, D], F32, kind="Internal").ap()

    made = []
    with ExitStack() as top:
        def sb(ctx, name, shape, dt=F32):
            return ctx.enter_context(nc.sbuf_tensor(name, shape, dt))

        def ps(ctx, name, shape):
            return ctx.enter_context(nc.psum_tensor(name, shape, F32))

        def sem(ctx, name):
            made.append(ctx.enter_context(nc.semaphore(name)))
            return made[-1]

        def start_at_one():
            with nc.Block() as block:
                @block.sync
                def _(sp):
                    for s in made:
                        sp.sem_inc(s, 1)
            made.clear()

        h = sb(top, "h", [P, NT, D])
        picks = sb(top, "picks", [P, NT, TOP, E])
        best_score = sb(top, "best_score", [P, NT, TOP])
        cst = sb(top, "cst", [P, const.shape[1]])

        def table(name):
            a, n = where[name]
            return cst[:, a:a + n]

        ident = table("ident")
        headblock = table("headblock")

        with ExitStack() as ctx:
            ids_sb = sb(ctx, "ids_sb", [P, NT], I32)
            wqkv_sb = sb(ctx, "wqkv_sb", [P, KH, 3, D])
            wbeta_sb = sb(ctx, "wbeta_sb", [P, KH, H])
            conv_sb = sb(ctx, "conv_sb", [P, 3, KH, TAPS])
            qkvb_sb = sb(ctx, "qkvb_sb", [P, 3, KH])
            bbeta_sb = sb(ctx, "bbeta_sb", [P, H])
            xhat = sb(ctx, "xhat", [P, TILES, D])
            stats = sb(ctx, "stats", [P, NT, 6])
            mv = sb(ctx, "mv", [P, NT, 2])
            std = sb(ctx, "std", [P, NT])
            rstd = sb(ctx, "rstd", [P, NT])
            xT = sb(ctx, "xT", [P, KH, L])
            raw = sb(ctx, "raw", [P, 3, KH, L + TAPS - 1])
            cv = sb(ctx, "cv", [P, 3, KH, L])
            sq = sb(ctx, "sq", [P, 2, KH, L])
            norm = sb(ctx, "norm", [P, P])
            rnorm = sb(ctx, "rnorm", [P, P])
            th = sb(ctx, "th", [P, TILES, H])
            kT = sb(ctx, "kT", [P, KH, L])
            qT = sb(ctx, "qT", [P, KH, L])
            kM = sb(ctx, "kM", [P, KH, 2, L])
            lin = sb(ctx, "lin", [P, TILES, H])
            eta = sb(ctx, "eta", [P, TILES, H])
            neta = sb(ctx, "neta", [P, TILES, H])
            k_tok = sb(ctx, "k_tok", [P, TILES, D])
            v_tok = sb(ctx, "v_tok", [P, TILES, D])
            bv = sb(ctx, "bv", [P, TILES, H, 2, DH])
            ng = sb(ctx, "ng", [P, TILES, HP, ROW])
            nx = sb(ctx, "nx", [P, C, 2, C])
            zero = sb(ctx, "zero", [P, 8, D])
            xt = sb(ctx, "xt", [P, C, 2, C])
            prod = sb(ctx, "prod", [P, C // 2 * 2 * C // 2])

            p_t = [ps(ctx, f"p_t{i}", [P, L]) for i in range(2)]
            p_p = [ps(ctx, f"p_p{i}", [P, L]) for i in range(2)]
            p_g = [ps(ctx, f"p_g{i}", [P, TILES, 2, ROW]) for i in range(4)]
            p_n = [p_g[i][:].rearrange("p t g x -> p (t g x)") for i in range(2)]

            s_ids, s_w, s_zero = (sem(ctx, n) for n in ("ids_in", "weights_in", "h_zeroed"))
            s_emb = ctx.enter_context(nc.semaphore("embedded"))
            s_pad = sem(ctx, "pad_zeroed")
            s_zero0 = sem(ctx, "zero_ready")
            s_slots = sem(ctx, "slots_zeroed")
            s_chain = sem(ctx, "vector_chain_a")
            s_xhat = sem(ctx, "xhat_ready")
            s_xtr = sem(ctx, "x_transposed")
            s_xT = sem(ctx, "xT_ready")
            s_bps = sem(ctx, "beta_summed")
            s_lin = sem(ctx, "beta_biased")
            s_eta = sem(ctx, "eta_ready")
            s_proj = sem(ctx, "projected")
            s_raw = sem(ctx, "raw_ready")
            s_cv = sem(ctx, "convolved")
            s_sq = sem(ctx, "squared")
            s_nsum = sem(ctx, "norms_summed")
            s_var = sem(ctx, "variance_ready")
            s_std = sem(ctx, "std_ready")
            s_norm = sem(ctx, "norms_ready")
            s_rn = sem(ctx, "inverse_norms_ready")
            s_nb = sem(ctx, "inverse_norms_spread")
            s_pre = sem(ctx, "vector_chain_setup")
            to_heads = table("to_heads").rearrange("p (n r) -> p n r", r=32)
            to_channels = table("to_channels").rearrange("p (t n r) -> p t n r", t=TILES, r=P)
            s_nrm = sem(ctx, "normalized")
            s_km = sem(ctx, "k_masked")
            s_ttr = sem(ctx, "kv_transposed")
            s_kt = sem(ctx, "k_tokens_ready")
            s_vt = sem(ctx, "v_tokens_ready")
            s_bv = sem(ctx, "beta_kv_ready")
            s_gram = sem(ctx, "gram_summed")
            s_ng = sem(ctx, "gram_scaled")
            s_ngst = sem(ctx, "gram_stored")
            s_st = sem(ctx, "kv_stored")
            s_nx = sem(ctx, "gram_loaded")
            s_xst = sem(ctx, "inverse_stored")
            s_inv = sem(ctx, "inverse_ready")

            CHAIN_A = 6 * (TAPS - 1) + 1 + 2 + 1 + 2 * (C - 1) - 1

            start_at_one()
            with nc.Block() as block:
                @block.sync
                def _(sp):
                    sp.dma_start(ids_sb[:], ids).then_inc(s_ids, 16)
                    for dst, src in ((cst[:], const), (wqkv_sb[:], wqkv), (wbeta_sb[:], wbeta), (conv_sb[:], conv_w),
                                     (qkvb_sb[:], qkv_b), (bbeta_sb[:], bbeta)):
                        sp.dma_start(dst, src).then_inc(s_w, 16)
                    sp.wait_ge(s_zero0, 2)
                    with sp.Fori(0, (SLOTS + 1) // 8) as n:
                        sp.dma_start(xs_dram[bass.ds(n * (8 * P), 8 * P), :].rearrange("(p g) d -> p g d", g=8),
                                     zero[:]).then_inc(s_slots, 16)
                    with sp.Fori(0, B) as b:
                        sp.wait_ge(s_nrm, b * 4 + 5)
                        sp.dma_start(kT_dram[b], kT[:].rearrange("p k l -> p (k l)")).then_inc(s_st, 16)
                        sp.dma_start(qT_dram[b], qT[:].rearrange("p k l -> p (k l)")).then_inc(s_st, 16)
                        sp.wait_ge(s_kt, b * 2 + 3)
                        sp.dma_start(k_dram[b], k_tok[:].rearrange("p t d -> p (t d)")).then_inc(s_st, 16)
                        sp.wait_ge(s_bv, b * 4 + 5)
                        sp.dma_start(bv_dram[b], bv[:].rearrange("p t h u d -> p (t h u d)")).then_inc(s_st, 16)
                        sp.wait_ge(s_inv, b + 1)
                        sp.wait_ge(s_ng, b * 8 + 9)
                        for t in range(TILES):
                            sp.dma_start(n_dram[b, :, t * P:(t + 1) * P, :].rearrange("g p x -> p g x"),
                                         ng[:, t]).then_inc(s_ngst, 16)
                        sp.wait_ge(s_ngst, b * 64 + 65)
                        sp.dma_start(nx[:].rearrange("p i g j -> p (i g j)"),
                                     n_dram[b].rearrange("g (c i) x -> (g c) (i x)", i=C)).then_inc(s_nx, 16)
                        sp.wait_ge(s_inv, b + 2)
                        for g in range(HP):
                            sp.dma_start(x_dram[b, :, g * ROW:(g + 1) * ROW].rearrange("(c k) x -> c k x", k=C),
                                         xt[g * NC_BATCH:(g + 1) * NC_BATCH].rearrange("p k e i -> p k (e i)")
                                         ).then_inc(s_xst, 16)
                    sp.wait_ge(s_slots, 16 * ((SLOTS + 1) // 8) + 1)
                    sp.wait_ge(s_st, 64 * B + 1)
                    sp.wait_ge(s_xst, 16 * HP * B + 1)

                @block.gpsimd
                def _(pool):
                    pool.memset(zero[:], 0.0).then_inc(s_zero0, 1)
                    pool.memset(h[:], 0.0).then_inc(s_zero, 1)
                    pool.wait_ge(s_zero, 1 + 1)
                    pool.wait_ge(s_ids, 16 + 1)
                    for t in range(NT):
                        pool.indirect_dma_start(h[:, t, :], None, emb, bass.IndirectOffsetOnAxis(ids_sb[:, t:t + 1].bitcast(U32), 0),
                                                bounds_check=VOCAB - 1, oob_is_err=False).then_inc(s_emb, 16)
                    pool.wait_ge(s_emb, 16 * NT)

                @block.tensor
                def _(pe):
                    pe.wait_ge(s_w, 16 * 6 + 1)
                    with pe.Fori(0, B) as b:
                        for k in range(KH):
                            if k == 0:
                                pe.wait_ge(s_vt, b * 2 + 1)
                            for t in range(TILES):
                                pe.wait_ge(s_xhat, b * TILES + t + 2)
                                ins = pe.transpose(p_t[k][:, t * P:(t + 1) * P], xhat[:, t, k * P:(k + 1) * P], ident)
                            ins.then_inc(s_xtr, 1)
                        pe.wait_ge(s_xT, b * KH + KH + 1)
                        pe.wait_ge(s_ng, b * 8 + 1)
                        for t in range(TILES):
                            for k in range(KH):
                                ins = pe.matmul(p_n[0][:, t * H:(t + 1) * H], xT[:, k, t * P:(t + 1) * P],
                                                wbeta_sb[:, k, :], start=(k == 0), stop=(k == KH - 1))
                        ins.then_inc(s_bps, 1)
                        for p in range(3):
                            for m in range(KH):
                                n = p * KH + m
                                pe.wait_ge(s_raw, b * 6 + max(n - 1, 0) + 1)
                                for k in range(KH):
                                    ins = pe.matmul(p_p[n % 2][:], wqkv_sb[:, k, p, m * P:(m + 1) * P], xT[:, k, :],
                                                    start=(k == 0), stop=(k == KH - 1))
                                ins.then_inc(s_proj, 1)
                        pe.wait_ge(s_lin, b + 2)
                        pe.wait_ge(s_sq, b * 4 + 5)
                        for t in range(TILES):
                            for n in range(4):
                                ins = pe.matmul(p_n[0][32 * t:32 * t + 32, 0:P], to_heads[:, n, :],
                                                sq[:, n // KH, n % KH, t * P:(t + 1) * P], start=(n == 0), stop=(n == 3))
                        ins.then_inc(s_nsum, 1)
                        pe.wait_ge(s_rn, b + 2)
                        for n in range(4):
                            if n >= 2:
                                pe.wait_ge(s_nrm, b * 4 + n - 1 + 1)
                            for t in range(TILES):
                                ins = pe.matmul(p_n[(n + 1) % 2][:, t * P:(t + 1) * P], to_channels[:, t, n, :], rnorm[:],
                                                start=True, stop=True)
                            ins.then_inc(s_nb, 1)
                        pe.wait_ge(s_nrm, b * 4 + 3)
                        for u in range(4):
                            if u >= 2:
                                pe.wait_ge(s_cv, b * 6 + 7)
                                pe.wait_ge(s_nrm, b * 4 + 5)
                                pe.wait_ge(s_km, b * KH * 2 + KH * 2 + 1)
                                pe.wait_ge(s_kt, b * 2 + u - 1 + 1)
                                pe.wait_ge(s_bv, b * 4 + u - 1 + 1)
                            for s in range(4):
                                t, k = 2 * (u % 2) + s // 2, s % 2
                                src = kT[:, k, t * P:(t + 1) * P] if u < 2 else cv[:, 2, k, t * P:(t + 1) * P]
                                ins = pe.transpose(p_t[u % 2][:, s * P:(s + 1) * P], src, ident)
                            ins.then_inc(s_ttr, 1)
                        for t in range(TILES):
                            for c in range(CH):
                                tok = slice(t * P + c * C, t * P + (c + 1) * C)
                                for g in range(HP):
                                    r = slice(32 * (g % 4), 32 * (g % 4) + 32)
                                    ins = pe.matmul(p_g[g % 4][c * C:(c + 1) * C, t, g // 4, :],
                                                    kT[r, g // 4, tok], kM[r, g // 4, :, tok], start=True, stop=True)
                        ins.then_inc(s_gram, 1)

                @block.scalar
                def _(act):
                    act.wait_ge(s_w, 16 * 6 + 1)
                    act.wait_ge(s_var, 1 + 1)
                    act.activation(std[:], std[:], ACT.Sqrt).then_inc(s_std, 1)
                    with act.Fori(0, B) as b:
                        for k in range(KH):
                            act.wait_ge(s_xtr, b * KH + k + 2)
                            act.copy(xT[:, k, :], p_t[k][:]).then_inc(s_xT, 1)
                        for n in range(6):
                            act.wait_ge(s_proj, b * 6 + n + 2)
                            act.wait_ge(s_cv, b * 6 + 1)
                            act.activation(raw[:, n // KH, n % KH, TAPS - 1:], p_p[n % 2][:], ACT.Identity,
                                           bias=qkvb_sb[:, n // KH, n % KH:n % KH + 1]).then_inc(s_raw, 1)
                        for n in range(4):
                            act.wait_ge(s_cv, b * 6 + n + 2)
                            act.activation(sq[:, n // KH, n % KH, :], cv[:, n // KH, n % KH, :],
                                           ACT.Square).then_inc(s_sq, 1)
                        act.wait_ge(s_nsum, b + 2)
                        act.activation(norm[:], p_n[0][:, 0:P], ACT.Sqrt).then_inc(s_norm, 1)
                        act.wait_ge(s_lin, b + 2)
                        act.activation(th[:], lin[:], ACT.Tanh, scale=0.5).then_inc(s_eta, 1)
                        act.wait_ge(s_nrm, b * 4 + 3)
                        act.wait_ge(s_gram, b + 1)
                        for k in range(KH):
                            for e in range(2):
                                a, _n = where["parity"]
                                act.activation(kM[:, k, e, :], kT[:, k, :], ACT.Copy,
                                               scale=cst[:, a + e:a + e + 1]).then_inc(s_km, 1)
                        act.wait_ge(s_st, b * 64 + 1)
                        for u in range(2):
                            act.wait_ge(s_ttr, b * 4 + u + 2)
                            act.copy(k_tok[:, 2 * u:2 * u + 2, :].rearrange("p t d -> p (t d)"),
                                     p_t[u][:]).then_inc(s_kt, 1)
                        for u in range(2):
                            act.wait_ge(s_ttr, b * 4 + u + 4)
                            act.activation(v_tok[:, 2 * u:2 * u + 2, :].rearrange("p t d -> p (t d)"), p_t[u][:],
                                           ACT.Silu).then_inc(s_vt, 1)

                @block.vector
                def _(dve):
                    dve.memset(raw[:, :, :, 0:TAPS - 1], 0.0).then_inc(s_pad, 1)
                    dve.wait_ge(s_w, 16 * 6 + 1)
                    pre = Chain(dve, s_pre)
                    dve.wait_ge(s_emb, 16 * NT)
                    for t in range(NT):
                        pre.did(dve.bn_stats(stats[:, t, :], h[:, t, :]))
                    for t in range(NT):
                        pre.wait(t + 1)
                        pre.did(dve.bn_aggr(mv[:, t, :], stats[:, t, :]))
                    pre.wait()
                    dve.tensor_scalar(std[:], mv[:, :, 1], 1e-5, None, ALU.add).then_inc(s_var, 1)
                    dve.wait_ge(s_std, 1 + 1)
                    pre.did(dve.reciprocal(rstd[:], std[:]))
                    pre.wait()
                    with dve.Fori(0, B) as b:
                        link = Chain(dve, s_chain, b * CHAIN_A)
                        dve.wait_ge(s_xtr, b * KH + 1)
                        for t in range(TILES):
                            dve.tensor_scalar(xhat[:, t, :], h[:, b * TILES + t, :], mv[:, b * TILES + t, 0:1],
                                              rstd[:, bass.ds(b * TILES + t, 1)],
                                              ALU.subtract, ALU.mult).then_inc(s_xhat, 1)
                        dve.wait_ge(s_bps, b + 2)
                        dve.tensor_tensor(lin[:], p_n[0][:, 0:TILES * H].rearrange("p (t h) -> p t h", t=TILES),
                                          bbeta_sb[:].unsqueeze(1).to_broadcast([P, TILES, H]), ALU.add).then_inc(s_lin, 1)
                        for n in range(6):
                            p, m = n // KH, n % KH
                            if n == 0:
                                dve.wait_ge(s_ttr, b * 4 + 1)
                            dve.wait_ge(s_raw, b * 6 + n + 2)
                            for j in range(TAPS):
                                w = conv_sb[:, p, m, j:j + 1]
                                x = raw[:, p, m, j:j + L]
                                if j == 0:
                                    ins = dve.tensor_scalar(cv[:, p, m, :], x, w, None, ALU.mult)
                                else:
                                    link.wait()
                                    ins = dve.scalar_tensor_tensor(cv[:, p, m, :], x, w, cv[:, p, m, :], ALU.mult, ALU.add)
                                if j < TAPS - 1:
                                    link.did(ins)
                                else:
                                    ins.then_inc(s_cv, 1)
                        dve.wait_ge(s_norm, b + 2)
                        link.did(dve.tensor_scalar(norm[:], norm[:], 1e-6, None, ALU.add))
                        link.wait()
                        dve.reciprocal(rnorm[:], norm[:]).then_inc(s_rn, 1)
                        dve.wait_ge(s_eta, b + 2)
                        link.did(dve.tensor_scalar(eta[:], th[:], 0.5, 0.5, ALU.mult, ALU.add))
                        link.did(dve.tensor_scalar(neta[:], th[:], -0.5, -0.5, ALU.mult, ALU.add))
                        dve.wait_ge(s_st, b * 64 + 1)
                        dve.wait_ge(s_gram, b + 1)
                        for n in range(4):
                            dst = (kT, qT)[n // KH]
                            dve.wait_ge(s_nb, b * 4 + n + 2)
                            dve.tensor_tensor(dst[:, n % KH, :], cv[:, n // KH, n % KH, :], p_n[(n + 1) % 2],
                                              ALU.mult).then_inc(s_nrm, 1)
                        link.wait()
                        for u in range(4):
                            t = slice(2 * (u % 2), 2 * (u % 2) + 2)
                            dve.wait_ge(s_kt if u < 2 else s_vt, b * 2 + u % 2 + 2)
                            src = (k_tok if u < 2 else v_tok)[:, t, :].rearrange("p t (h d) -> p t h d", d=DH)
                            dve.tensor_tensor(bv[:, t, :, u // 2, :].rearrange("p t h d -> p (t h) d"),
                                              src.rearrange("p t h d -> p (t h) d"),
                                              eta[:, t, :].rearrange("p t h -> p (t h)").unsqueeze(2).to_broadcast([P, 2 * H, DH]),
                                              ALU.mult).then_inc(s_bv, 1)
                        dve.wait_ge(s_ngst, b * 64 + 1)
                        dve.wait_ge(s_gram, b + 2)
                        for g in range(HP):
                            dve.tensor_tensor(ng[:, :, g, :].rearrange("p t (e j) -> p t e j", e=2),
                                              p_g[g % 4][:, :, g // 4, :].rearrange("p t (e j) -> p t e j", e=2),
                                              neta[:, :, 2 * g:2 * g + 2].unsqueeze(3).to_broadcast([P, TILES, 2, C]),
                                              ALU.mult).then_inc(s_ng, 1)
                        dve.wait_ge(s_xst, b * 16 * HP + 1)
                        link.did(dve.tensor_copy(xt[:].rearrange("p k e i -> p (k e i)"), table("unit")))
                        dve.wait_ge(s_nx, b * 16 + 17)
                        for i in range(C - 1):
                            k, m = i + 1, C - 1 - i
                            link.wait()
                            pr = prod[:, 0:k * 2 * m].rearrange("p (k e j) -> p k e j", e=2, j=m)
                            link.did(dve.tensor_tensor(
                                pr, nx[:, k:C, :, i].rearrange("p j e -> p e j").unsqueeze(1).to_broadcast([P, k, 2, m]),
                                xt[:, 0:k, :, i:i + 1].to_broadcast([P, k, 2, m]), ALU.mult))
                            link.wait()
                            ins = dve.tensor_tensor(xt[:, 0:k, :, k:C], xt[:, 0:k, :, k:C], pr, ALU.add)
                            if i < C - 2:
                                link.did(ins)
                            else:
                                ins.then_inc(s_inv, 1)
                        assert link.n == CHAIN_A, link.n

        with ExitStack() as ctx:
            wout_sb = sb(ctx, "wout_sb", [P, KH, D])
            router_sb = sb(ctx, "router_sb", [P, KH, E])
            bout_sb = sb(ctx, "bout_sb", [P, D])
            rms_sb = sb(ctx, "rms_sb", [P, 1])
            kT = sb(ctx, "kTb", [P, KH, L])
            qT = sb(ctx, "qTb", [P, KH, L])
            qM = sb(ctx, "qM", [P, KH, 2, L])
            k_tok = sb(ctx, "k_tok_b", [P, TILES, D])
            bv = sb(ctx, "bv_b", [P, TILES, H, 2 * DH])
            xbd = [sb(ctx, f"xbd{i}", [P, HP, 2, P]) for i in range(2)]
            st = [sb(ctx, f"st{i}", [P, H, P]) for i in range(2)]
            y_tok = sb(ctx, "y_tok", [P, D])
            z_tok = [sb(ctx, f"z_tok{i}", [P, D]) for i in range(2)]
            yT = [sb(ctx, f"yT{i}", [P, KH, P]) for i in range(2)]
            u = sb(ctx, "u", [P, D])
            uw = sb(ctx, "uw", [P, D])
            w_bd = sb(ctx, "w_bd", [P, KH, P])
            d_bd = sb(ctx, "d_bd", [P, KH, P])
            od = sb(ctx, "od", [P, D])
            o = sb(ctx, "o", [P, D])
            osq = sb(ctx, "osq", [P, D])
            oms = sb(ctx, "oms", [P, H])
            orms = sb(ctx, "orms", [P, H])
            on = sb(ctx, "on", [P, D])
            oT = sb(ctx, "oT", [P, KH, P])
            hb = sb(ctx, "hb", [P, D])
            stats = sb(ctx, "stats_b", [P, 6])
            mv = sb(ctx, "mv_b", [P, 2])
            std = sb(ctx, "std_b", [P, 1])
            rstd = sb(ctx, "rstd_b", [P, 1])
            xn = sb(ctx, "xn", [P, D])
            xnT = sb(ctx, "xnT", [P, KH, P])
            score = sb(ctx, "score", [P, E])
            best = sb(ctx, "best", [P, 8])
            best_at = sb(ctx, "best_at", [P, 8], U32)
            best_f = sb(ctx, "best_f", [P, 2])
            tick = sb(ctx, "tick", [P, 1])

            p_yz = ps(ctx, "p_yz", [P, H, 2 * DH])
            p_tr = ps(ctx, "p_tr", [P, L])
            p_r = ps(ctx, "p_r", [P, L])
            p_acc = ps(ctx, "p_acc", [P, 2, KH, P])
            p_st = [ps(ctx, f"p_st{i}", [P, KH, 2, P]) for i in range(2)]
            p_o = ps(ctx, "p_o", [P, 2, KH, P])
            p_out = ps(ctx, "p_out", [P, L])

            names = ("b_weights", "batch_loaded", "xbd_zeroed", "xbd_loaded0", "xbd_loaded1", "q_masked", "yz_summed", "yz_out",
                     "y_transposed", "yT_ready", "weights_summed", "weights_masked", "state_cleared", "old_reads",
                     "od_ready", "r_summed", "u_ready", "w_summed", "w_ready", "uw_ready", "d_summed", "d_ready",
                     "o_summed", "o_ready", "o_squared", "on_ready", "o_transposed", "oT_ready", "out_projected",
                     "hb_ready", "xn_ready", "xn_stored", "xn_transposed", "xnT_ready", "scored", "score_copied",
                     "oms_ready", "orms_ready", "var_ready", "std_ready", "vector_chain_b")
            S = {n: sem(ctx, "b_" + n) for n in names}
            CHAIN_B = TILES * (2 + 4 + 5)

            start_at_one()
            with nc.Block() as block:
                @block.sync
                def _(sp):
                    for dst, src in ((wout_sb[:], wout), (router_sb[:], router), (bout_sb[:], bout), (rms_sb[:], rms)):
                        sp.dma_start(dst, src).then_inc(S["b_weights"], 16)
                    sp.wait_ge(S["xbd_zeroed"], 2 + 1)
                    with sp.Fori(0, B) as b:
                        sp.wait_ge(S["o_summed"], b * TILES + 1)
                        sp.wait_ge(S["d_summed"], b * TILES + 1)
                        sp.wait_ge(S["q_masked"], b * 4 + 1)
                        for dst, src in ((kT[:].rearrange("p k l -> p (k l)"), kT_dram[b]),
                                         (qT[:].rearrange("p k l -> p (k l)"), qT_dram[b]),
                                         (k_tok[:].rearrange("p t d -> p (t d)"), k_dram[b]),
                                         (bv[:].rearrange("p t h d -> p (t h d)"), bv_dram[b])):
                            sp.dma_start(dst, src).then_inc(S["batch_loaded"], 16)
                        for t in range(TILES):
                            sp.wait_ge(S["yz_summed"], b * TILES + max(t - 1, 0) + 1)
                            for c in range(CH):
                                sp.dma_start(xbd[t % 2][c * C:(c + 1) * C, :, :, c * C:(c + 1) * C].rearrange("p g e i -> p (g e) i"),
                                             x_dram[b, t * P + c * C:t * P + (c + 1) * C, :].rearrange(
                                                 "p (g i) -> p g i", i=C)).then_inc(S[f"xbd_loaded{t % 2}"], 16)

                @block.gpsimd
                def _(pool):
                    for i in range(2):
                        pool.memset(xbd[i][:], 0.0).then_inc(S["xbd_zeroed"], 1)
                    pool.wait_ge(S["b_weights"], 64 + 1)
                    with pool.Fori(0, B) as b:
                        def residual(t):
                            pool.wait_ge(S["xn_ready"], b * TILES + t + 1)
                            pool.tensor_tensor(hb[:], h[:, b * TILES + t, :], bout_sb[:], ALU.add).then_inc(S["hb_ready"], 1)

                        for t in range(TILES):
                            if t:
                                residual(t - 1)
                            pool.wait_ge(S["u_ready"], b * NC_BATCH + (t + 1) * CH + 1)
                            pool.wait_ge(S["d_summed"], b * TILES + t + 1)
                            a, _n = where["tri_before"]
                            pool.tensor_tensor(uw[:], u[:], cst[:, a + t:a + t + 1].to_broadcast([P, D]),
                                               ALU.mult).then_inc(S["uw_ready"], 1)
                        residual(TILES - 1)

                @block.tensor
                def _(pe):
                    pe.wait_ge(S["b_weights"], 64 + 1)
                    with pe.Fori(0, B) as b:
                        def tile0(t):
                            return b * TILES + t

                        def yz(t):
                            pe.wait_ge(S[f"xbd_loaded{t % 2}"], (b * (TILES // 2) + t // 2 + 1) * 16 * CH + 1)
                            pe.wait_ge(S["yz_out"], tile0(t) * 2 + 1)
                            for hd in range(H):
                                ins = pe.matmul(p_yz[:, hd, :], xbd[t % 2][:, hd // 2, hd % 2, :], bv[:, t, hd, :],
                                                start=True, stop=True)
                            ins.then_inc(S["yz_summed"], 1)

                        def y_transpose(t):
                            pe.wait_ge(S["yz_out"], tile0(t) * 2 + 3)
                            pe.wait_ge(S["yT_ready"], b * TILES + t + 1)
                            pe.wait_ge(S["xnT_ready"], b * TILES + max(t - 2, 0) + 1)
                            for k in range(KH):
                                ins = pe.transpose(p_tr[:, k * P:(k + 1) * P], y_tok[:, k * P:(k + 1) * P], ident)
                            ins.then_inc(S["y_transposed"], 1)

                        def weights(t, n):
                            pe.wait_ge(S["weights_masked"], tile0(t) * 4 + n if t or n else b * TILES * 4 + 1)
                            r = slice(32 * n, 32 * n + 32)
                            for k in range(KH):
                                ins = pe.matmul(p_st[n % 2][:, k, :, :], kT[r, k, t * P:(t + 1) * P],
                                                qM[r, k, :, t * P:(t + 1) * P], start=True, stop=True)
                            ins.then_inc(S["weights_summed"], 1)

                        def old_reads(t):
                            pe.wait_ge(S["o_ready"], tile0(t) + 1)
                            pe.wait_ge(S["w_ready"], b * NC_BATCH + t * CH + 1)
                            pe.wait_ge(S["d_ready"], tile0(t) + 1)
                            pe.wait_ge(S["state_cleared"], b + 2)
                            for n, state in enumerate((w_bd, d_bd)):
                                for k in range(KH):
                                    ins = pe.matmul(p_o[:, n, k, :], qT[:, k, t * P:(t + 1) * P], state[:, k, :],
                                                    start=(n == 0 and k == 0), stop=False, skip_group_check=True)
                            ins.then_inc(S["old_reads"], 1)

                        def recur_r(t, c):
                            n = b * NC_BATCH + t * CH + c
                            pe.wait_ge(S["w_ready"], n + 1)
                            pe.wait_ge(S["u_ready"], n + 1)
                            if c == 0:
                                pe.wait_ge(S["yT_ready"], tile0(t) + 2)
                            for k in range(KH):
                                ins = pe.matmul(p_r[c * C:(c + 1) * C, k * P:(k + 1) * P], yT[t % 2][:, k, c * C:(c + 1) * C],
                                                w_bd[:, k, :], start=True, stop=True)
                            ins.then_inc(S["r_summed"], 1)

                        def recur_w(t, c):
                            pe.wait_ge(S["u_ready"], b * NC_BATCH + t * CH + c + 2)
                            if c == 0:
                                pe.wait_ge(S["d_ready"], tile0(t) + 1)
                            for k in range(KH):
                                ins = pe.matmul(p_acc[:, 0, k, :], k_tok[c * C:(c + 1) * C, t, k * P:(k + 1) * P],
                                                u[c * C:(c + 1) * C, k * P:(k + 1) * P],
                                                start=(t == 0 and c == 0 and k == 0), stop=False, skip_group_check=True)
                            ins.then_inc(S["w_summed"], 1)

                        def average(t):
                            pe.wait_ge(S["uw_ready"], tile0(t) + 2)
                            pe.wait_ge(S["w_ready"], b * NC_BATCH + (t + 1) * CH + 1)
                            for k in range(KH):
                                ins = pe.matmul(p_acc[:, 1, k, :], k_tok[:, t, k * P:(k + 1) * P], uw[:, k * P:(k + 1) * P],
                                                start=False, stop=False, skip_group_check=True)
                            ins.then_inc(S["d_summed"], 1)

                        def new_reads(t):
                            pe.wait_ge(S["od_ready"], tile0(t) + 2)
                            pe.wait_ge(S["weights_masked"], tile0(t) * 4 + 5)
                            for hd in range(H):
                                ins = pe.matmul(p_o[:, 0, hd // 8, (hd % 8) * DH:(hd % 8 + 1) * DH], st[t % 2][:, hd, :],
                                                u[:, hd * DH:(hd + 1) * DH], start=False, stop=(hd == H - 1),
                                                skip_group_check=True)
                            ins.then_inc(S["o_summed"], 1)

                        def o_transpose(t):
                            pe.wait_ge(S["on_ready"], tile0(t) + 2)
                            pe.wait_ge(S["yT_ready"], b * TILES + min(t + 3, TILES) + 1)
                            pe.wait_ge(S["xnT_ready"], b * TILES + t + 1)
                            for k in range(KH):
                                ins = pe.transpose(p_tr[:, k * P:(k + 1) * P], on[:, k * P:(k + 1) * P], ident)
                            ins.then_inc(S["o_transposed"], 1)

                        def project(t):
                            pe.wait_ge(S["oT_ready"], tile0(t) + 2)
                            pe.wait_ge(S["score_copied"], tile0(t) + 1)
                            for k in range(KH):
                                ins = pe.matmul(p_out[:, 0:D], oT[:, k, :], wout_sb[:, k, :], start=(k == 0), stop=(k == KH - 1))
                            ins.then_inc(S["out_projected"], 1)

                        def xn_transpose(t):
                            pe.wait_ge(S["xn_ready"], tile0(t) + 2)
                            for k in range(KH):
                                ins = pe.transpose(p_tr[:, k * P:(k + 1) * P], xn[:, k * P:(k + 1) * P], ident)
                            ins.then_inc(S["xn_transposed"], 1)

                        def route(t):
                            pe.wait_ge(S["xnT_ready"], tile0(t) + 2)
                            for k in range(KH):
                                ins = pe.matmul(p_out[:, D:D + E], xnT[:, k, :], router_sb[:, k, :], start=(k == 0), stop=(k == KH - 1))
                            ins.then_inc(S["scored"], 1)

                        pe.wait_ge(S["batch_loaded"], b * 64 + 65)
                        yz(0)
                        y_transpose(0)
                        pe.wait_ge(S["q_masked"], b * 4 + 5)
                        for n in range(4):
                            weights(0, n)
                        for t in range(TILES):
                            nxt, last = t + 1 < TILES, t > 0
                            old_reads(t)
                            recur_r(t, 0)
                            if nxt:
                                yz(t + 1)
                            recur_w(t, 0)
                            recur_r(t, 1)
                            if nxt:
                                y_transpose(t + 1)
                                weights(t + 1, 0)
                            recur_w(t, 1)
                            recur_r(t, 2)
                            if nxt:
                                weights(t + 1, 1)
                            if last:
                                o_transpose(t - 1)
                            recur_w(t, 2)
                            recur_r(t, 3)
                            if nxt:
                                weights(t + 1, 2)
                            if last:
                                project(t - 1)
                            recur_w(t, 3)
                            if nxt:
                                weights(t + 1, 3)
                            average(t)
                            new_reads(t)
                            if last:
                                xn_transpose(t - 1)
                                route(t - 1)
                        o_transpose(TILES - 1)
                        project(TILES - 1)
                        xn_transpose(TILES - 1)
                        route(TILES - 1)

                @block.scalar
                def _(act):
                    act.wait_ge(S["b_weights"], 64 + 1)
                    with act.Fori(0, B) as b:
                        def tile0(t):
                            return b * TILES + t

                        def yz_out(t):
                            act.wait_ge(S["yz_summed"], tile0(t) + 2)
                            act.wait_ge(S["y_transposed"], tile0(t) + 1)
                            act.copy(y_tok[:].rearrange("p (h d) -> p h d", d=DH), p_yz[:, :, 0:DH]).then_inc(S["yz_out"], 1)
                            act.wait_ge(S["u_ready"], b * NC_BATCH + max(t - 1, 0) * CH + 1)
                            act.copy(z_tok[t % 2][:].rearrange("p (h d) -> p h d", d=DH),
                                     p_yz[:, :, DH:2 * DH]).then_inc(S["yz_out"], 1)

                        def yT_out(t):
                            act.wait_ge(S["y_transposed"], tile0(t) + 2)
                            act.wait_ge(S["r_summed"], b * NC_BATCH + max(t - 1, 0) * CH + 1)
                            act.copy(yT[t % 2][:].rearrange("p k l -> p (k l)"), p_tr[:, 0:D]).then_inc(S["yT_ready"], 1)

                        def od_out(t):
                            act.wait_ge(S["old_reads"], tile0(t) + 2)
                            act.wait_ge(S["o_ready"], tile0(t) + 1)
                            a, _n = where["minus_tri_inverse"]
                            act.activation(od[:], p_o[:, 1, :, :].rearrange("p k l -> p (k l)"), ACT.Copy,
                                           scale=cst[:, a + t:a + t + 1]).then_inc(S["od_ready"], 1)

                        def square(t):
                            act.wait_ge(S["o_ready"], tile0(t) + 2)
                            act.activation(osq[:], o[:], ACT.Square).then_inc(S["o_squared"], 1)

                        def head_sqrt(t):
                            act.wait_ge(S["oms_ready"], tile0(t) + 2)
                            act.activation(orms[:], oms[:], ACT.Sqrt).then_inc(S["orms_ready"], 1)

                        def row_sqrt(t):
                            act.wait_ge(S["var_ready"], tile0(t) + 2)
                            act.activation(std[:], rstd[:], ACT.Sqrt).then_inc(S["std_ready"], 1)

                        def oT_out(t):
                            act.wait_ge(S["o_transposed"], tile0(t) + 2)
                            act.activation(oT[:].rearrange("p k l -> p (k l)"), p_tr[:, 0:D], ACT.Copy,
                                           scale=rms_sb[:, 0:1]).then_inc(S["oT_ready"], 1)

                        def xnT_out(t):
                            act.wait_ge(S["xn_ready"], tile0(t) + 2)
                            act.dma_start(xn_dram[b * TILES + t], xn[:]).then_inc(S["xn_stored"], 16)
                            act.wait_ge(S["xn_transposed"], tile0(t) + 2)
                            act.copy(xnT[:].rearrange("p k l -> p (k l)"), p_tr[:, 0:D]).then_inc(S["xnT_ready"], 1)

                        act.wait_ge(S["batch_loaded"], b * 64 + 65)
                        yz_out(0)
                        yT_out(0)
                        for k in range(KH):
                            for e in range(2):
                                a, _n = where["parity"]
                                act.activation(qM[:, k, e, :], qT[:, k, :], ACT.Copy,
                                               scale=cst[:, a + e:a + e + 1]).then_inc(S["q_masked"], 1)
                        for t in range(TILES):
                            od_out(t)
                            if t:
                                head_sqrt(t - 1)
                            if t + 1 < TILES:
                                yz_out(t + 1)
                                yT_out(t + 1)
                            if t:
                                oT_out(t - 1)
                                row_sqrt(t - 1)
                            square(t)
                            if t:
                                xnT_out(t - 1)
                        head_sqrt(TILES - 1)
                        oT_out(TILES - 1)
                        row_sqrt(TILES - 1)
                        xnT_out(TILES - 1)
                    act.wait_ge(S["xn_stored"], 16 * NT + 1)

                @block.vector
                def _(dve):
                    dve.wait_ge(S["b_weights"], 64 + 1)
                    with dve.Fori(0, B) as b:
                        link = Chain(dve, S["vector_chain_b"], b * CHAIN_B)

                        def tile0(t):
                            return b * TILES + t

                        def update(t, c):
                            r = slice(c * C, (c + 1) * C)
                            n = b * NC_BATCH + t * CH + c
                            dve.wait_ge(S["r_summed"], n + 2)
                            if c == 0:
                                dve.wait_ge(S["yz_out"], tile0(t) * 2 + 3)
                                dve.wait_ge(S["o_summed"], tile0(t) + 1)
                                dve.wait_ge(S["uw_ready"], tile0(t) + 1)
                            dve.tensor_tensor(u[r, :], z_tok[t % 2][r, :], p_r[r, 0:D], ALU.subtract).then_inc(S["u_ready"], 1)
                            dve.wait_ge(S["w_summed"], n + 2)
                            dve.tensor_tensor(w_bd[:], p_acc[:, 0], headblock.unsqueeze(1).to_broadcast([P, KH, P]),
                                              ALU.mult).then_inc(S["w_ready"], 1)

                        def mask(t, n):
                            dve.wait_ge(S["weights_summed"], tile0(t) * 4 + n + 2)
                            if n == 0:
                                dve.wait_ge(S["o_summed"], b * TILES + max(t - 1, 0) + 1)
                            a, _n = where["average"]
                            dve.tensor_tensor(st[t % 2][:].rearrange("p (k h) i -> p k h i", k=KH)[:, :, 2 * n:2 * n + 2, :],
                                              p_st[n % 2][:],
                                              cst[:, a + t * P:a + (t + 1) * P].unsqueeze(1).unsqueeze(1).to_broadcast(
                                                  [P, KH, 2, P]),
                                              ALU.mult).then_inc(S["weights_masked"], 1)

                        def read_out(t):
                            dve.wait_ge(S["o_summed"], tile0(t) + 2)
                            dve.wait_ge(S["od_ready"], tile0(t) + 2)
                            dve.tensor_tensor(o[:], p_o[:, 0, :, :].rearrange("p k l -> p (k l)"), od[:],
                                              ALU.add).then_inc(S["o_ready"], 1)

                        def head_norm(t):
                            dve.wait_ge(S["o_squared"], tile0(t) + 2)
                            link.did(dve.tensor_reduce(oms[:], osq[:].rearrange("p (h d) -> p h d", d=DH), AX, ALU.add))
                            link.wait()
                            dve.tensor_scalar(oms[:], oms[:], 1.0 / DH, 1e-6, ALU.mult, ALU.add).then_inc(S["oms_ready"], 1)
                            dve.wait_ge(S["orms_ready"], tile0(t) + 2)
                            link.did(dve.reciprocal(oms[:], orms[:]))
                            link.wait()
                            dve.tensor_tensor(on[:].rearrange("p (h d) -> p h d", d=DH), o[:].rearrange("p (h d) -> p h d", d=DH),
                                              oms[:].unsqueeze(2).to_broadcast([P, H, DH]), ALU.mult).then_inc(S["on_ready"], 1)

                        def residual_norm(t):
                            dve.wait_ge(S["out_projected"], tile0(t) + 2)
                            dve.wait_ge(S["hb_ready"], tile0(t) + 2)
                            dve.wait_ge(S["xn_stored"], tile0(t) * 16 + 1)
                            hh = h[:, b * TILES + t, :]
                            link.did(dve.tensor_tensor(hh, p_out[:, 0:D], hb[:], ALU.add))
                            wait_apart(dve, tick[:], link.sem, link.base + link.n)
                            link.did(dve.bn_stats(stats[:], hh))
                            wait_apart(dve, tick[:], link.sem, link.base + link.n)
                            link.did(dve.bn_aggr(mv[:], stats[:]))
                            link.wait()
                            dve.tensor_scalar(rstd[:], mv[:, 1:2], 1e-5, None, ALU.add).then_inc(S["var_ready"], 1)
                            dve.wait_ge(S["std_ready"], tile0(t) + 2)
                            link.did(dve.reciprocal(rstd[:], std[:]))
                            link.wait()
                            dve.tensor_scalar(xn[:], hh, mv[:, 0:1], rstd[:, 0:1], ALU.subtract, ALU.mult).then_inc(S["xn_ready"], 1)

                        def copy_score(t):
                            dve.wait_ge(S["scored"], tile0(t) + 2)
                            dve.tensor_copy(score[:], p_out[:, D:D + E]).then_inc(S["score_copied"], 1)

                        def gate(t):
                            wait_apart(dve, tick[:], S["score_copied"], tile0(t) + 1)
                            link.did(dve.max(best[:], score[:]))
                            wait_apart(dve, tick[:], link.sem, link.base + link.n)
                            link.did(dve.max_index(best_at[:], best[:], score[:]))
                            link.wait()
                            link.did(dve.tensor_copy(best_f[:], best_at[:, 0:2]))
                            link.wait()
                            for k in range(TOP):
                                link.did(dve.tensor_scalar(picks[:, b * TILES + t, k, :], table("experts"), best_f[:, k:k + 1],
                                                           None, ALU.is_equal))
                            dve.tensor_copy(best_score[:, b * TILES + t, :], best[:, 0:TOP])

                        dve.wait_ge(S["old_reads"], b * TILES + 1)
                        dve.wait_ge(S["r_summed"], b * NC_BATCH + 1)
                        dve.memset(w_bd[:], 0.0)
                        dve.memset(d_bd[:], 0.0).then_inc(S["state_cleared"], 1)
                        for n in range(4):
                            mask(0, n)
                        for t in range(TILES):
                            nxt, last = t + 1 < TILES, t > 0
                            update(t, 0)
                            if last:
                                head_norm(t - 1)
                            update(t, 1)
                            if nxt:
                                mask(t + 1, 0)
                            update(t, 2)
                            if nxt:
                                mask(t + 1, 1)
                            update(t, 3)
                            if nxt:
                                mask(t + 1, 2)
                            if last:
                                residual_norm(t - 1)
                            dve.wait_ge(S["d_summed"], tile0(t) + 2)
                            dve.tensor_tensor(d_bd[:], p_acc[:, 1], headblock.unsqueeze(1).to_broadcast([P, KH, P]),
                                              ALU.mult).then_inc(S["d_ready"], 1)
                            if nxt:
                                mask(t + 1, 3)
                            read_out(t)
                            if last:
                                copy_score(t - 1)
                                gate(t - 1)
                        head_norm(TILES - 1)
                        residual_norm(TILES - 1)
                        copy_score(TILES - 1)
                        gate(TILES - 1)
                        assert link.n == CHAIN_B, link.n

        with ExitStack() as ctx:
            SHARED = E
            HALF = NT // 2
            wi = sb(ctx, "wi", [P, E + 1, KH, F])
            ws = sb(ctx, "ws", [P, E + 1, KH, F])
            wo = sb(ctx, "wo", [P, E + 1, FK, D])
            x_in = [sb(ctx, f"x_in{i}", [P, D]) for i in range(2)]
            xT = [sb(ctx, f"xT_c{i}", [P, KH, P]) for i in range(2)]
            silu = [sb(ctx, f"silu{i}", [P, F]) for i in range(2)]
            hid = [sb(ctx, f"hid{i}", [P, F]) for i in range(2)]
            hidT = [sb(ctx, f"hidT{i}", [P, FK, P]) for i in range(2)]
            y_sb = [sb(ctx, f"y_sb{i}", [P, D]) for i in range(2)]
            rows = [sb(ctx, f"rows{i}", [P, 2, TOP, D]) for i in range(2)]
            at = [sb(ctx, f"at{i}", [P, 2, TOP], U32) for i in range(2)]
            x_rows = sb(ctx, "x_rows", [P, 4, D])
            gate = sb(ctx, "gate", [P, NT, TOP])
            slot_of = sb(ctx, "slot_of", [P, NT, TOP], U32)
            expert_of = sb(ctx, "expert_of", [P, SLOTS], I32)
            count = sb(ctx, "count", [P, NT, E])
            total = sb(ctx, "total", [P, NT, E])
            upto = sb(ctx, "upto", [P, E, NT])
            place = sb(ctx, "place", [P, NT, E])
            chosen = sb(ctx, "chosen", [P, NT, TOP, E])
            slot_f = sb(ctx, "slot_f", [P, NT, TOP])
            padded_i = sb(ctx, "padded_i", [P, E], I32)
            padded = sb(ctx, "padded", [P, E])
            end = sb(ctx, "end", [P, E])
            base = sb(ctx, "base", [P, E])
            past = sb(ctx, "past", [P, SLOTS, E])
            past_n = sb(ctx, "past_n", [P, SLOTS])
            tick = sb(ctx, "tick_c", [P, 1])

            p_x = ps(ctx, "p_x", [P, KH, P])
            p_i = ps(ctx, "p_i", [P, F])
            p_s = ps(ctx, "p_s", [P, F])
            p_h = ps(ctx, "p_h", [P, FK, P])
            p_y = ps(ctx, "p_y", [P, D])
            p_c = ps(ctx, "p_c", [P, 2, NT * E])

            s_w = sem(ctx, "c_weights")
            s_w_shared = sem(ctx, "c_weights_shared")
            FFN = ("x_loaded0", "x_loaded1", "x_turned", "xT_ready", "mid_summed", "sw_summed", "silu_ready", "hid_ready",
                   "hid_turned", "hidT_ready", "y_summed", "y_out")

            def turn_x(pe, S, c, i, pair):
                pe.wait_ge(S[f"x_loaded{i}"], pair * 16 + 17)
                pe.wait_ge(S["xT_ready"], c + 1)
                for k in range(KH):
                    ins = pe.transpose(p_x[:, k, :], x_in[i][:, k * P:(k + 1) * P], ident)
                ins.then_inc(S["x_turned"], 1)

            def up_mid(pe, S, c, i, e):
                pe.wait_ge(S["xT_ready"], c + 2)
                pe.wait_ge(S["silu_ready"], c + 1)
                for k in range(KH):
                    ins = pe.matmul(p_i[:], xT[i][:, k, :], wi[:, e, k, :], start=(k == 0), stop=(k == KH - 1))
                ins.then_inc(S["mid_summed"], 1)

            def up_sw(pe, S, c, i, e):
                pe.wait_ge(S["hid_ready"], c + 1)
                for k in range(KH):
                    ins = pe.matmul(p_s[:], xT[i][:, k, :], ws[:, e, k, :], start=(k == 0), stop=(k == KH - 1))
                ins.then_inc(S["sw_summed"], 1)

            def turn_hid(pe, S, c, i):
                pe.wait_ge(S["hid_ready"], c + 2)
                pe.wait_ge(S["hidT_ready"], c + 1)
                for f in range(FK):
                    ins = pe.transpose(p_h[:, f, :], hid[i][:, f * P:(f + 1) * P], ident)
                ins.then_inc(S["hid_turned"], 1)

            def down(pe, S, c, i, e):
                pe.wait_ge(S["hidT_ready"], c + 2)
                pe.wait_ge(S["y_out"], c + 1)
                for f in range(FK):
                    ins = pe.matmul(p_y[:], hidT[i][:, f, :], wo[:, e, f, :], start=(f == 0), stop=(f == FK - 1))
                ins.then_inc(S["y_summed"], 1)

            def xT_out(act, S, c, i):
                act.wait_ge(S["x_turned"], c + 2)
                act.copy(xT[i][:], p_x[:]).then_inc(S["xT_ready"], 1)

            def silu_out(act, S, c, i):
                act.wait_ge(S["mid_summed"], c + 2)
                act.activation(silu[i][:], p_i[:], ACT.Silu).then_inc(S["silu_ready"], 1)

            def hidT_out(act, S, c, i):
                act.wait_ge(S["hid_turned"], c + 2)
                act.copy(hidT[i][:], p_h[:]).then_inc(S["hidT_ready"], 1)

            def hid_out(dve, S, c, i):
                dve.wait_ge(S["silu_ready"], c + 2)
                dve.wait_ge(S["sw_summed"], c + 2)
                dve.tensor_tensor(hid[i][:], p_s[:], silu[i][:], ALU.mult).then_inc(S["hid_ready"], 1)

            def shared_pe(pe, S, c):
                turn_x(pe, S, c, 0, c // 2 if isinstance(c, int) else S["pair"])
                turn_x(pe, S, c + 1, 1, S["pair"])
                up_mid(pe, S, c, 0, SHARED)
                up_sw(pe, S, c, 0, SHARED)
                up_mid(pe, S, c + 1, 1, SHARED)
                turn_hid(pe, S, c, 0)
                up_sw(pe, S, c + 1, 1, SHARED)
                down(pe, S, c, 0, SHARED)
                turn_hid(pe, S, c + 1, 1)
                down(pe, S, c + 1, 1, SHARED)

            def shared_act(act, S, c):
                xT_out(act, S, c, 0)
                xT_out(act, S, c + 1, 1)
                silu_out(act, S, c, 0)
                silu_out(act, S, c + 1, 1)
                hidT_out(act, S, c, 0)
                hidT_out(act, S, c + 1, 1)

            def shared_add(dve, S, c, t):
                dve.wait_ge(S["y_summed"], c + 2)
                dve.tensor_tensor(h[:, t, :], p_y[:], h[:, t, :], ALU.add).then_inc(S["y_out"], 1)

            S = {n: sem(ctx, "c1_" + n) for n in FFN + ("counted", "chain", "gates_ready", "rows_in", "rows_ready",
                                                        "routed")}
            s_scat = [ctx.enter_context(nc.semaphore(f"scattered{i}")) for i in range(2)]
            start_at_one()
            with nc.Block() as block:
                @block.sync
                def _(sp):
                    for dst, src in ((wi, w_in), (ws, w_sw), (wo, w_out)):
                        sp.dma_start(dst[:, SHARED], src[SHARED]).then_inc(s_w_shared, 16)
                    with sp.Fori(0, NT // 4) as j:
                        sp.wait_ge(S["x_turned"], j * 2 + 1)
                        for i in range(2):
                            sp.dma_start(x_in[i][:], xn_dram[j * 2 + i]).then_inc(S[f"x_loaded{i}"], 16)
                        sp.wait_ge(S["rows_ready"], j * 8 + 1)
                        sp.dma_start(x_rows[:], xn_dram[bass.ds(j * 4, 4)].rearrange("t p d -> p t d")).then_inc(S["rows_in"], 16)

                @block.tensor
                def _(pe):
                    pe.wait_ge(S["counted"], 2)
                    for n, what in enumerate(("before", "ones")):
                        ins = pe.matmul(p_c[:, n, :], table(what), count[:].rearrange("p t e -> p (t e)"), start=(n == 0),
                                        stop=True, skip_group_check=True)
                    ins.then_inc(S["counted"], 1)
                    pe.wait_ge(s_w_shared, 49)
                    with pe.Fori(0, NT // 4) as j:
                        shared_pe(pe, {**S, "pair": j}, j * 2)

                @block.scalar
                def _(act):
                    act.activation(gate[:], best_score[:], ACT.Sigmoid).then_inc(S["gates_ready"], 1)
                    for dst, src in ((wi, w_in), (ws, w_sw), (wo, w_out)):
                        for e in range(E):
                            act.dma_start(dst[:, e], src[e]).then_inc(s_w, 16)
                    with act.Fori(0, NT // 4) as j:
                        shared_act(act, S, j * 2)

                @block.vector
                def _(dve):
                    link = Chain(dve, S["chain"])
                    dve.tensor_tensor(count[:], picks[:, :, 0, :], picks[:, :, 1, :], ALU.add).then_inc(S["counted"], 1)
                    dve.wait_ge(S["counted"], 3)
                    link.did(dve.tensor_copy(total[:].rearrange("p t e -> p (t e)"), p_c[:, 1, :]))
                    link.wait()
                    for e in range(E):
                        link.did(dve.tensor_tensor_scan(upto[:, e, :], total[:, :, e], table("zeros_nt"), 0.0, ALU.add, ALU.add))
                    link.wait()
                    link.did(dve.tensor_scalar(padded_i[:], upto[:, :, NT - 1], float(P - 1), None, ALU.add))
                    link.wait()
                    link.did(dve.tensor_scalar(padded_i[:], padded_i[:], 7, 7, ALU.arith_shift_right, ALU.logical_shift_left))
                    link.wait()
                    link.did(dve.tensor_copy(padded[:], padded_i[:]))
                    link.wait()
                    link.did(dve.tensor_tensor_scan(end[:], padded[:], table("zeros_nt")[:, 0:E], 0.0, ALU.add, ALU.add))
                    link.wait()
                    link.did(dve.tensor_tensor(base[:], end[:], padded[:], ALU.subtract))
                    link.did(dve.tensor_tensor(place[:], upto[:].rearrange("p e t -> p t e"), total[:], ALU.subtract))
                    link.wait()
                    link.did(dve.tensor_tensor(place[:], place[:], base[:].unsqueeze(1).to_broadcast([P, NT, E]), ALU.add))
                    link.wait()
                    link.did(dve.tensor_tensor(place[:].rearrange("p t e -> p (t e)"), p_c[:, 0, :],
                                               place[:].rearrange("p t e -> p (t e)"), ALU.add))
                    link.wait()
                    for k in range(TOP):
                        link.did(dve.tensor_tensor(chosen[:, :, k, :], picks[:, :, k, :], place[:], ALU.mult))
                    link.wait()
                    link.did(dve.tensor_reduce(slot_f[:], chosen[:], AX, ALU.add))
                    link.wait()
                    link.did(dve.tensor_copy(slot_of[:], slot_f[:]))
                    link.did(dve.tensor_tensor(past[:], table("slot").unsqueeze(2).to_broadcast([P, SLOTS, E]),
                                               end[:].unsqueeze(1).to_broadcast([P, SLOTS, E]), ALU.is_ge))
                    link.wait()
                    link.did(dve.tensor_reduce(past_n[:], past[:], AX, ALU.add))
                    link.wait()
                    link.did(dve.tensor_scalar(past_n[:], past_n[:], float(E - 1), None, ALU.min))
                    link.wait()
                    link.did(dve.tensor_copy(expert_of[:], past_n[:]))
                    link.wait()
                    dve.wait_ge(S["gates_ready"], 2)
                    with dve.Fori(0, NT // 4) as j:
                        def scatter_rows(q):
                            if q == 0:
                                dve.wait_ge(S["rows_in"], j * 16 + 17)
                            dve.tensor_copy(at[q][:], slot_of[:, bass.ds(j * 4 + q * 2, 2), :]).then_inc(S["routed"], 1)
                            for t in range(2):
                                for k in range(TOP):
                                    dve.tensor_scalar(rows[q][:, t, k, :], x_rows[:, 2 * q + t, :],
                                                            gate[:, j * 4 + 2 * q + t, k:k + 1], None,
                                                            ALU.mult).then_inc(S["rows_ready"], 1)

                        scatter_rows(0)
                        hid_out(dve, S, j * 2, 0)
                        scatter_rows(1)
                        hid_out(dve, S, j * 2 + 1, 1)
                        for i in range(2):
                            shared_add(dve, S, j * 2 + i, j * 2 + i)
                        for q in range(2):
                            dve.wait_ge(s_scat[q], j * 64 + 64)

                @block.gpsimd
                def _(pool):
                    for j in range(NT // 4):
                        for q in range(2):
                            pool.wait_ge(S["routed"], j * 2 + q + 2)
                            pool.wait_ge(S["rows_ready"], j * 8 + 4 * q + 5)
                            for t in range(2):
                                for k in range(TOP):
                                    pool.indirect_dma_start(xs_dram, bass.IndirectOffsetOnAxis(at[q][:, t, k:k + 1], 0),
                                                            rows[q][:, t, k, :], None).then_inc(s_scat[q], 16)
                    for q in range(2):
                        pool.wait_ge(s_scat[q], NT // 4 * 64)

            S = {n: sem(ctx, "c2_" + n) for n in FFN + ("y_stored0", "y_stored1")}
            start_at_one()
            with nc.Block() as block:
                @block.sync
                def _(sp):
                    for i in range(2):
                        sp.dma_start(x_in[i][:], xs_dram[i * P:(i + 1) * P, :]).then_inc(S[f"x_loaded{i}"], 16)

                    def store_y(c, i):
                        sp.wait_ge(S["y_out"], c + 2)
                        sp.dma_start(ys_dram[bass.ds(c * P, P), :], y_sb[i][:]).then_inc(S[f"y_stored{i}"], 16)

                    with sp.Fori(0, SLOTS // 2) as j:
                        for i in range(2):
                            s = j * 2 + 1 + i
                            sp.wait_ge(S["x_turned"], s + 1)
                            sp.dma_start(x_in[i][:], xs_dram[bass.ds((s + 1) * P, P), :]).then_inc(S[f"x_loaded{i}"], 16)
                            store_y(s - 1, i)
                    store_y(SLOTS - 1, 0)
                    for i in range(2):
                        sp.wait_ge(S[f"y_stored{i}"], 16 * ((SLOTS + 1 - i) // 2) + 1)
                        sp.wait_ge(S[f"x_loaded{i}"], 16 * (SLOTS // 2 + 1) + 1)

                @block.tensor
                def _(pe):
                    pe.wait_ge(s_w, 16 * 3 * E + 1)

                    def expert(s):
                        return pe.value_load(expert_of[0:1, bass.ds(s, 1)], min_val=0, max_val=E - 1)

                    turn_x(pe, S, 0, 0, 0)
                    first = expert(0)
                    up_mid(pe, S, 0, 0, first)
                    up_sw(pe, S, 0, 0, first)
                    turn_x(pe, S, 1, 1, 0)
                    with pe.Fori(0, SLOTS // 2) as j:
                        for i in range(2):
                            s, now, old = j * 2 + 1 + i, (1 + i) % 2, i
                            e = expert(s)
                            up_mid(pe, S, s, now, e)
                            turn_hid(pe, S, s - 1, old)
                            up_sw(pe, S, s, now, e)
                            turn_x(pe, S, s + 1, old, j + 1)
                            down(pe, S, s - 1, old, expert(s - 1))
                    turn_hid(pe, S, SLOTS - 1, 0)
                    down(pe, S, SLOTS - 1, 0, expert(SLOTS - 1))

                @block.scalar
                def _(act):
                    xT_out(act, S, 0, 0)
                    silu_out(act, S, 0, 0)
                    xT_out(act, S, 1, 1)
                    with act.Fori(0, SLOTS // 2) as j:
                        for i in range(2):
                            s, now, old = j * 2 + 1 + i, (1 + i) % 2, i
                            silu_out(act, S, s, now)
                            hidT_out(act, S, s - 1, old)
                            xT_out(act, S, s + 1, old)
                    hidT_out(act, S, SLOTS - 1, 0)

                @block.vector
                def _(dve):
                    def y_out(c, i, pair):
                        dve.wait_ge(S["y_summed"], c + 2)
                        dve.wait_ge(S[f"y_stored{i}"], pair * 16 + 1)
                        dve.tensor_copy(y_sb[i][:], p_y[:]).then_inc(S["y_out"], 1)

                    hid_out(dve, S, 0, 0)
                    with dve.Fori(0, SLOTS // 2) as j:
                        for i in range(2):
                            s, now, old = j * 2 + 1 + i, (1 + i) % 2, i
                            hid_out(dve, S, s, now)
                            y_out(s - 1, old, j)
                    y_out(SLOTS - 1, 0, SLOTS // 2)

            S = {n: sem(ctx, "c3_" + n) for n in FFN + ("routed", "rows_used", "added", "out_ready", "stored")}
            s_gath = [ctx.enter_context(nc.semaphore(f"gathered{i}")) for i in range(2)]
            start_at_one()
            with nc.Block() as block:
                @block.sync
                def _(sp):
                    with sp.Fori(0, NT // 4) as j:
                        sp.wait_ge(S["x_turned"], j * 2 + 1)
                        for i in range(2):
                            sp.dma_start(x_in[i][:], xn_dram[HALF + j * 2 + i]).then_inc(S[f"x_loaded{i}"], 16)
                        for q in range(2):
                            sp.wait_ge(S["out_ready"], j * 2 + q + 2)
                            sp.dma_start(out[bass.ds(j * 4 + 2 * q, 2)].rearrange("t p d -> p t d"),
                                         h[:, bass.ds(j * 4 + 2 * q, 2), :]).then_inc(S["stored"], 16)
                    sp.wait_ge(S["stored"], 16 * NT // 2 + 1)

                @block.tensor
                def _(pe):
                    with pe.Fori(0, NT // 4) as j:
                        shared_pe(pe, {**S, "pair": j}, j * 2)

                @block.scalar
                def _(act):
                    with act.Fori(0, NT // 4) as j:
                        shared_act(act, S, j * 2)

                @block.vector
                def _(dve):
                    with dve.Fori(0, NT // 4) as j:
                        def route(q):
                            dve.wait_ge(S["rows_used"], j * 2 + q + 1)
                            dve.tensor_copy(at[q][:], slot_of[:, bass.ds(j * 4 + q * 2, 2), :]).then_inc(S["routed"], 1)

                        def join(q):
                            dve.wait_ge(s_gath[q], j * 64 + 64)
                            tiles = h[:, bass.ds(j * 4 + 2 * q, 2), :]
                            dve.tensor_tensor(rows[q][:, :, 0, :], rows[q][:, :, 0, :], rows[q][:, :, 1, :],
                                              ALU.add).then_inc(S["added"], 1)
                            dve.wait_ge(S["added"], j * 2 + q + 2)
                            dve.wait_ge(S["y_out"], j * 2 + 3)
                            dve.tensor_tensor(tiles, rows[q][:, :, 0, :], tiles, ALU.add).then_inc(S["out_ready"], 1)

                        for q in range(2):
                            dve.tensor_copy(at[q][:], slot_of[:, bass.ds(j * 4 + q * 2, 2), :]).then_inc(S["routed"], 1)
                        for i in range(2):
                            hid_out(dve, S, j * 2 + i, i)
                        for i in range(2):
                            shared_add(dve, S, j * 2 + i, HALF + j * 2 + i)
                        for q in range(2):
                            join(q)

                @block.gpsimd
                def _(pool):
                    for j in range(NT // 4):
                        for q in range(2):
                            if j:
                                pool.wait_ge(S["out_ready"], j * 2 + q)
                            pool.wait_ge(S["routed"], j * 2 + q + 2)
                            for t in range(2):
                                for k in range(TOP):
                                    pool.indirect_dma_start(rows[q][:, t, k, :], None, ys_dram,
                                                            bass.IndirectOffsetOnAxis(at[q][:, t, k:k + 1], 0)
                                                            ).then_inc(s_gath[q], 16)


def lay_out(a):
    k, n = a.shape
    return np.ascontiguousarray(a.reshape(k // P, P, n).transpose(1, 0, 2))


def kernel(**inputs):
    import concourse.bacc as _bacc
    from concourse.bass_utils import run_bass_kernel_spmd as _run

    x = {k: np.asarray(v) for k, v in inputs.items()}
    a, f = "L0_attn_", "L0_ffn_"
    const, where = consts()
    qkv = ("k", "q", "v")
    arrays = {
        "ids": np.ascontiguousarray(x["x"].reshape(NT, P).T),
        "emb": x["L0_tok_embeddings"],
        "wqkv": np.stack([lay_out(x[f"{a}W{n}"].T) for n in qkv], 2),
        "wbeta": lay_out(x[a + "Wbeta"].T),
        "wout": lay_out(x[a + "Wout"].T),
        "router": lay_out(x[f + "router_DE"]),
        "conv_w": np.stack([lay_out(x[f"{a}conv_{n}"]) for n in qkv], 1),
        "qkv_b": np.stack([x[f"{a}b{n}"].reshape(KH, P).T for n in qkv], 1),
        "bbeta": np.broadcast_to(x[a + "bbeta"], (P, H)),
        "bout": np.broadcast_to(x[a + "bout"], (P, D)),
        "rms": np.tile(x[a + "rms_w"], P // DH).reshape(P, 1),
        "const": const,
        "w_in": np.stack([lay_out(w) for w in (*x[f + "w_in_eDF"], x[f + "w_in_shared_FD"].T)]),
        "w_sw": np.stack([lay_out(w) for w in (*x[f + "w_swiglu_eDF"], x[f + "w_swiglu_FD"].T)]),
        "w_out": np.stack([lay_out(w) for w in (*x[f + "w_out_eFD"], x[f + "w_out_shared_DF"].T)]),
    }
    arrays = {n: np.ascontiguousarray(v) for n, v in arrays.items()}
    nc = _bacc.Bacc("TRN2", target_bir_lowering=False, num_devices=1)
    args = [nc.dram_tensor(f"in_{n}", v.shape, mybir.dt.from_np(v.dtype), kind="ExternalInput").ap()
            for n, v in arrays.items()]
    out = nc.dram_tensor("out_h", [NT, P, D], F32, kind="ExternalOutput").ap()
    build(nc, *args, out, where)
    r = _run(nc, [{f"in_{n}": v for n, v in arrays.items()}], core_ids=[0])
    return r.results[0]["out_h"].reshape(B, L, D)
```

```python
from contextlib import ExitStack

import numpy as np
import concourse.bass as bass
from concourse import mybir

P = 128
B, L, D = 8, 512, 256
H, DH = 16, 16
C = 32
TILES = L // P
NT = B * TILES
CH = P // C
KH = D // P
VOCAB = 8000
E, F = 8, 512
FK = F // P
TAPS = 4
HP = H // 2
NC_BATCH = L // C
TOP = 2
SLOTS = TOP * B * L // P + E - 1
ROW = 2 * C

F32 = mybir.dt.float32
I32 = mybir.dt.int32
U32 = mybir.dt.uint32
ALU = mybir.AluOpType
ACT = mybir.ActivationFunctionType
AX = mybir.AxisListType.X


class Chain:

    def __init__(self, eng, sem, base=0):
        self.eng, self.sem, self.base, self.n = eng, sem, base, 0

    def did(self, ins):
        ins.then_inc(self.sem, 1)
        self.n += 1
        return self.n

    def wait(self, n=None):
        self.eng.wait_ge(self.sem, self.base + (self.n if n is None else n) + 1)


def wait_apart(dve, tick, sem, value):
    dve.wait_ge(sem, value + 1)
    dve.memset(tick, 0.0)


def consts():
    tri = lambda n: n * (n + 1) / 2.0
    p = np.arange(P)
    where, parts, at = {}, [], 0

    def add(name, a):
        nonlocal at
        a = np.asarray(a, np.float64).reshape(P, -1)
        where[name] = (at, a.shape[1])
        parts.append(a)
        at += a.shape[1]

    add("ident", np.eye(P))
    add("headblock", (p[:, None] // DH) == (p[None, :] // DH))
    add("rms_eps", np.full((P, 1), 1e-6))
    add("parity", np.stack([(p // DH) % 2 == k for k in range(2)], 1))
    m = np.zeros((P, TILES, P))
    for t in range(TILES):
        i = t * P + p[None, :] + 1.0
        j = t * P + p[:, None] + 1.0
        m[:, t, :] = np.where(j <= i, (tri(i) - tri(j - 1)) / tri(i), 0.0)
    add("average", m)
    n = np.arange(TILES)[None, :] * P + p[:, None] + 1.0
    add("tri_before", tri(n - 1))
    add("minus_tri_row", np.broadcast_to(-1.0 / tri(np.arange(L) + 1.0), (P, L)))
    row = np.arange(32)
    fwd = np.zeros((P, 2, KH, 32))
    back = np.zeros((P, TILES, 2, KH, P))
    for u in range(2):
        for m in range(KH):
            fwd[:, u, m, :] = row[None, :] == (H * u + (m * P + p[:, None]) // DH)
            for t in range(TILES):
                back[:, t, u, m, :] = p[:, None] == (32 * t + H * u + (m * P + p[None, :]) // DH)
    add("to_heads", fwd)
    add("to_channels", back)
    k = np.arange(C)
    add("unit", np.broadcast_to((k[:, None, None] == k[None, None, :]) * np.ones((1, 2, 1)), (P, C, 2, C)))
    add("before", p[:, None] < p[None, :])
    add("ones", np.ones((P, P)))
    add("slot", np.broadcast_to(np.arange(SLOTS) * P, (P, SLOTS)))
    add("zeros_nt", np.zeros((P, NT)))
    add("experts", np.broadcast_to(np.arange(E), (P, E)))
    return np.concatenate(parts, 1).astype(np.float32), where


def build(nc, ids, emb, wqkv, wbeta, wout, router, conv_w, qkv_b, bbeta, bout, rms, const, w_in, w_sw, w_out, out,
          where):
    n_dram = nc.dram_tensor("chunk_gram_dram", [B, HP, L, ROW], F32, kind="Internal").ap()
    x_dram = nc.dram_tensor("chunk_inverse_dram", [B, L, H * C], F32, kind="Internal").ap()
    kT_dram = nc.dram_tensor("k_channels_dram", [B, P, KH * L], F32, kind="Internal").ap()
    qT_dram = nc.dram_tensor("q_channels_dram", [B, P, KH * L], F32, kind="Internal").ap()
    k_dram = nc.dram_tensor("k_tokens_dram", [B, P, TILES * D], F32, kind="Internal").ap()
    bv_dram = nc.dram_tensor("beta_kv_dram", [B, P, TILES * 2 * D], F32, kind="Internal").ap()
    xs_dram = nc.dram_tensor("slots_in_dram", [(SLOTS + 1) * P, D], F32, kind="Internal").ap()
    ys_dram = nc.dram_tensor("slots_out_dram", [SLOTS * P, D], F32, kind="Internal").ap()
    xn_dram = nc.dram_tensor("ffn_input_dram", [NT, P, D], F32, kind="Internal").ap()

    made = []
    with ExitStack() as top:
        def sb(ctx, name, shape, dt=F32):
            return ctx.enter_context(nc.sbuf_tensor(name, shape, dt))

        def ps(ctx, name, shape):
            return ctx.enter_context(nc.psum_tensor(name, shape, F32))

        def sem(ctx, name):
            made.append(ctx.enter_context(nc.semaphore(name)))
            return made[-1]

        def start_at_one():
            with nc.Block() as block:
                @block.sync
                def _(sp):
                    for s in made:
                        sp.sem_inc(s, 1)
            made.clear()

        h = sb(top, "h", [P, NT, D])
        picks = sb(top, "picks", [P, NT, TOP, E])
        best_score = sb(top, "best_score", [P, NT, TOP])
        cst = sb(top, "cst", [P, const.shape[1]])

        def table(name):
            a, n = where[name]
            return cst[:, a:a + n]

        ident = table("ident")
        headblock = table("headblock")

        with ExitStack() as ctx:
            ids_sb = sb(ctx, "ids_sb", [P, NT], I32)
            wqkv_sb = sb(ctx, "wqkv_sb", [P, KH, 3, D])
            wbeta_sb = sb(ctx, "wbeta_sb", [P, KH, H])
            conv_sb = sb(ctx, "conv_sb", [P, 3, KH, TAPS])
            qkvb_sb = sb(ctx, "qkvb_sb", [P, 3, KH])
            bbeta_sb = sb(ctx, "bbeta_sb", [P, H])
            xhat = sb(ctx, "xhat", [P, TILES, D])
            stats = sb(ctx, "stats", [P, NT, 6])
            mv = sb(ctx, "mv", [P, NT, 2])
            std = sb(ctx, "std", [P, NT])
            rstd = sb(ctx, "rstd", [P, NT])
            xT = sb(ctx, "xT", [P, KH, L])
            raw = sb(ctx, "raw", [P, 3, KH, L + TAPS - 1])
            cv = sb(ctx, "cv", [P, 3, KH, L])
            sq = sb(ctx, "sq", [P, 2, KH, L])
            norm = sb(ctx, "norm", [P, P])
            rnorm = sb(ctx, "rnorm", [P, P])
            th = sb(ctx, "th", [P, TILES, H])
            kT = sb(ctx, "kT", [P, KH, L])
            qT = sb(ctx, "qT", [P, KH, L])
            kM = sb(ctx, "kM", [P, KH, 2, L])
            lin = sb(ctx, "lin", [P, TILES, H])
            eta = sb(ctx, "eta", [P, TILES, H])
            neta = sb(ctx, "neta", [P, TILES, H])
            k_tok = sb(ctx, "k_tok", [P, TILES, D])
            v_tok = sb(ctx, "v_tok", [P, TILES, D])
            bv = sb(ctx, "bv", [P, TILES, H, 2, DH])
            ng = sb(ctx, "ng", [P, TILES, HP, ROW])
            nx = sb(ctx, "nx", [P, C, 2, C])
            zero = sb(ctx, "zero", [P, 8, D])
            xt = sb(ctx, "xt", [P, C, 2, C])
            prod = sb(ctx, "prod", [P, C // 2 * 2 * C // 2])

            p_t = [ps(ctx, f"p_t{i}", [P, L]) for i in range(2)]
            p_p = [ps(ctx, f"p_p{i}", [P, L]) for i in range(2)]
            p_g = [ps(ctx, f"p_g{i}", [P, TILES, 2, ROW]) for i in range(4)]
            p_n = [p_g[i][:].rearrange("p t g x -> p (t g x)") for i in range(2)]

            s_ids, s_w, s_zero = (sem(ctx, n) for n in ("ids_in", "weights_in", "h_zeroed"))
            s_emb = [ctx.enter_context(nc.semaphore(n)) for n in ("embedded_first", "embedded_rest")]
            s_pad = sem(ctx, "pad_zeroed")
            s_zero0 = sem(ctx, "zero_ready")
            s_slots = sem(ctx, "slots_zeroed")
            s_chain = sem(ctx, "vector_chain_a")
            s_sub = sem(ctx, "vector_chain_inverse")
            s_xhat = sem(ctx, "xhat_ready")
            s_xtr = sem(ctx, "x_transposed")
            s_xT = sem(ctx, "xT_ready")
            s_bps = sem(ctx, "beta_summed")
            s_lin = sem(ctx, "beta_biased")
            s_eta = sem(ctx, "eta_ready")
            s_proj = sem(ctx, "projected")
            s_raw = sem(ctx, "raw_ready")
            s_cv = sem(ctx, "convolved")
            s_sq = sem(ctx, "squared")
            s_nsum = sem(ctx, "norms_summed")
            s_var = sem(ctx, "variance_ready")
            s_std = sem(ctx, "std_ready")
            s_norm = sem(ctx, "norms_ready")
            s_rn = sem(ctx, "inverse_norms_ready")
            s_nb = sem(ctx, "inverse_norms_spread")
            s_pre = sem(ctx, "vector_chain_setup")
            to_heads = table("to_heads").rearrange("p (n r) -> p n r", r=32)
            to_channels = table("to_channels").rearrange("p (t n r) -> p t n r", t=TILES, r=P)
            s_nrm = sem(ctx, "normalized")
            s_km = sem(ctx, "k_masked")
            s_ttr = sem(ctx, "kv_transposed")
            s_kt = sem(ctx, "k_tokens_ready")
            s_vt = sem(ctx, "v_tokens_ready")
            s_bv = sem(ctx, "beta_kv_ready")
            s_gram = sem(ctx, "gram_summed")
            s_ng = sem(ctx, "gram_scaled")
            s_ngst = sem(ctx, "gram_stored")
            s_st = sem(ctx, "kv_stored")
            s_nx = sem(ctx, "gram_loaded")
            s_xst = sem(ctx, "inverse_stored")
            s_inv = sem(ctx, "inverse_ready")

            CHAIN_A = 6 * (TAPS - 1) + 1 + 2
            CHAIN_X = 2 * (C - 1)

            start_at_one()
            with nc.Block() as block:
                @block.sync
                def _(sp):
                    sp.dma_start(ids_sb[:], ids).then_inc(s_ids, 16)
                    for dst, src in ((cst[:], const), (wqkv_sb[:], wqkv), (wbeta_sb[:], wbeta), (conv_sb[:], conv_w),
                                     (qkvb_sb[:], qkv_b), (bbeta_sb[:], bbeta)):
                        sp.dma_start(dst, src).then_inc(s_w, 16)
                    sp.wait_ge(s_zero0, 2)
                    with sp.Fori(0, (SLOTS + 1) // 8) as n:
                        sp.dma_start(xs_dram[bass.ds(n * (8 * P), 8 * P), :].rearrange("(p g) d -> p g d", g=8),
                                     zero[:]).then_inc(s_slots, 16)
                    def store_inverse(b):
                        sp.wait_ge(s_inv, b + 2)
                        for g in range(HP):
                            sp.dma_start(x_dram[b, :, g * ROW:(g + 1) * ROW].rearrange("(c k) x -> c k x", k=C),
                                         xt[g * NC_BATCH:(g + 1) * NC_BATCH].rearrange("p k e i -> p k (e i)")
                                         ).then_inc(s_xst, 16)

                    def batch(b, first):
                        sp.wait_ge(s_nrm, b * 4 + 5)
                        sp.dma_start(kT_dram[b], kT[:].rearrange("p k l -> p (k l)")).then_inc(s_st, 16)
                        sp.dma_start(qT_dram[b], qT[:].rearrange("p k l -> p (k l)")).then_inc(s_st, 16)
                        sp.wait_ge(s_kt, b * 2 + 3)
                        sp.dma_start(k_dram[b], k_tok[:].rearrange("p t d -> p (t d)")).then_inc(s_st, 16)
                        sp.wait_ge(s_bv, b * 4 + 5)
                        sp.dma_start(bv_dram[b], bv[:].rearrange("p t h u d -> p (t h u d)")).then_inc(s_st, 16)
                        if not first:
                            store_inverse(b - 1)
                        sp.wait_ge(s_ng, b * 8 + 9)
                        for t in range(TILES):
                            sp.dma_start(n_dram[b, :, t * P:(t + 1) * P, :].rearrange("g p x -> p g x"),
                                         ng[:, t]).then_inc(s_ngst, 16)
                        sp.wait_ge(s_ngst, b * 64 + 65)
                        sp.dma_start(nx[:].rearrange("p i g j -> p (i g j)"),
                                     n_dram[b].rearrange("g (c i) x -> (g c) (i x)", i=C)).then_inc(s_nx, 16)

                    batch(0, True)
                    with sp.Fori(1, B) as b:
                        batch(b, False)
                    store_inverse(B - 1)
                    sp.wait_ge(s_slots, 16 * ((SLOTS + 1) // 8) + 1)
                    sp.wait_ge(s_st, 64 * B + 1)
                    sp.wait_ge(s_xst, 16 * HP * B + 1)

                @block.gpsimd
                def _(pool):
                    pool.memset(zero[:], 0.0).then_inc(s_zero0, 1)
                    pool.wait_ge(s_ids, 16 + 1)
                    for t in range(NT):
                        if t % TILES == 0:
                            pool.wait_ge(s_zero, t // TILES + 2)
                        pool.indirect_dma_start(h[:, t, :], None, emb, bass.IndirectOffsetOnAxis(ids_sb[:, t:t + 1].bitcast(U32), 0),
                                                bounds_check=VOCAB - 1, oob_is_err=False).then_inc(s_emb[t >= TILES], 16)
                    pool.wait_ge(s_emb[0], 16 * TILES)
                    pool.wait_ge(s_emb[1], 16 * (NT - TILES))

                @block.tensor
                def _(pe):
                    pe.wait_ge(s_w, 16 * 6 + 1)
                    with pe.Fori(0, B) as b:
                        for k in range(KH):
                            if k == 0:
                                pe.wait_ge(s_vt, b * 2 + 1)
                            for t in range(TILES):
                                pe.wait_ge(s_xhat, b * TILES + t + 2)
                                ins = pe.transpose(p_t[k][:, t * P:(t + 1) * P], xhat[:, t, k * P:(k + 1) * P], ident)
                            ins.then_inc(s_xtr, 1)
                        pe.wait_ge(s_xT, b * KH + KH + 1)
                        pe.wait_ge(s_ng, b * 8 + 1)
                        for t in range(TILES):
                            for k in range(KH):
                                ins = pe.matmul(p_n[0][:, t * H:(t + 1) * H], xT[:, k, t * P:(t + 1) * P],
                                                wbeta_sb[:, k, :], start=(k == 0), stop=(k == KH - 1))
                        ins.then_inc(s_bps, 1)
                        for p in range(3):
                            for m in range(KH):
                                n = p * KH + m
                                pe.wait_ge(s_raw, b * 6 + max(n - 1, 0) + 1)
                                for k in range(KH):
                                    ins = pe.matmul(p_p[n % 2][:], wqkv_sb[:, k, p, m * P:(m + 1) * P], xT[:, k, :],
                                                    start=(k == 0), stop=(k == KH - 1))
                                ins.then_inc(s_proj, 1)
                        pe.wait_ge(s_lin, b + 2)
                        pe.wait_ge(s_sq, b * 4 + 5)
                        for t in range(TILES):
                            for n in range(4):
                                ins = pe.matmul(p_n[0][32 * t:32 * t + 32, 0:P], to_heads[:, n, :],
                                                sq[:, n // KH, n % KH, t * P:(t + 1) * P], start=(n == 0), stop=(n == 3))
                        ins.then_inc(s_nsum, 1)
                        pe.wait_ge(s_rn, b + 2)
                        for n in range(4):
                            if n >= 2:
                                pe.wait_ge(s_nrm, b * 4 + n - 1 + 1)
                            for t in range(TILES):
                                ins = pe.matmul(p_n[(n + 1) % 2][:, t * P:(t + 1) * P], to_channels[:, t, n, :], rnorm[:],
                                                start=True, stop=True)
                            ins.then_inc(s_nb, 1)
                        pe.wait_ge(s_nrm, b * 4 + 3)
                        for u in range(4):
                            if u >= 2:
                                pe.wait_ge(s_cv, b * 6 + 7)
                                pe.wait_ge(s_nrm, b * 4 + 5)
                                pe.wait_ge(s_km, b * KH * 2 + KH * 2 + 1)
                                pe.wait_ge(s_kt, b * 2 + u - 1 + 1)
                                pe.wait_ge(s_bv, b * 4 + u - 1 + 1)
                            for s in range(4):
                                t, k = 2 * (u % 2) + s // 2, s % 2
                                src = kT[:, k, t * P:(t + 1) * P] if u < 2 else cv[:, 2, k, t * P:(t + 1) * P]
                                ins = pe.transpose(p_t[u % 2][:, s * P:(s + 1) * P], src, ident)
                            ins.then_inc(s_ttr, 1)
                        for t in range(TILES):
                            for c in range(CH):
                                tok = slice(t * P + c * C, t * P + (c + 1) * C)
                                for g in range(HP):
                                    r = slice(32 * (g % 4), 32 * (g % 4) + 32)
                                    ins = pe.matmul(p_g[g % 4][c * C:(c + 1) * C, t, g // 4, :],
                                                    kT[r, g // 4, tok], kM[r, g // 4, :, tok], start=True, stop=True)
                        ins.then_inc(s_gram, 1)

                @block.scalar
                def _(act):
                    act.wait_ge(s_w, 16 * 6 + 1)
                    act.wait_ge(s_var, 1 + 1)
                    act.activation(std[:, 0:TILES], std[:, 0:TILES], ACT.Sqrt).then_inc(s_std, 1)

                    def batch(b):
                        for k in range(KH):
                            act.wait_ge(s_xtr, b * KH + k + 2)
                            act.copy(xT[:, k, :], p_t[k][:]).then_inc(s_xT, 1)
                        for n in range(6):
                            act.wait_ge(s_proj, b * 6 + n + 2)
                            act.wait_ge(s_cv, b * 6 + 1)
                            act.activation(raw[:, n // KH, n % KH, TAPS - 1:], p_p[n % 2][:], ACT.Identity,
                                           bias=qkvb_sb[:, n // KH, n % KH:n % KH + 1]).then_inc(s_raw, 1)
                        for n in range(4):
                            act.wait_ge(s_cv, b * 6 + n + 2)
                            act.activation(sq[:, n // KH, n % KH, :], cv[:, n // KH, n % KH, :],
                                           ACT.Square).then_inc(s_sq, 1)
                        act.wait_ge(s_nsum, b + 2)
                        act.activation(norm[:], p_n[0][:, 0:P], ACT.Sqrt).then_inc(s_norm, 1)
                        act.wait_ge(s_lin, b + 2)
                        act.activation(th[:], lin[:], ACT.Tanh, scale=0.5).then_inc(s_eta, 1)
                        act.wait_ge(s_nrm, b * 4 + 3)
                        act.wait_ge(s_gram, b + 1)
                        for k in range(KH):
                            for e in range(2):
                                a, _n = where["parity"]
                                act.activation(kM[:, k, e, :], kT[:, k, :], ACT.Copy,
                                               scale=cst[:, a + e:a + e + 1]).then_inc(s_km, 1)
                        act.wait_ge(s_st, b * 64 + 1)
                        for u in range(2):
                            act.wait_ge(s_ttr, b * 4 + u + 2)
                            act.copy(k_tok[:, 2 * u:2 * u + 2, :].rearrange("p t d -> p (t d)"),
                                     p_t[u][:]).then_inc(s_kt, 1)
                        for u in range(2):
                            act.wait_ge(s_ttr, b * 4 + u + 4)
                            act.activation(v_tok[:, 2 * u:2 * u + 2, :].rearrange("p t d -> p (t d)"), p_t[u][:],
                                           ACT.Silu).then_inc(s_vt, 1)

                    batch(0)
                    act.wait_ge(s_var, 2 + 1)
                    act.activation(std[:, TILES:NT], std[:, TILES:NT], ACT.Sqrt).then_inc(s_std, 1)
                    with act.Fori(1, B) as b:
                        batch(b)

                @block.vector
                def _(dve):
                    for b in range(B):
                        dve.memset(h[:, b * TILES:(b + 1) * TILES, :], 0.0).then_inc(s_zero, 1)
                    dve.memset(raw[:, :, :, 0:TAPS - 1], 0.0).then_inc(s_pad, 1)
                    dve.wait_ge(s_w, 16 * 6 + 1)
                    pre = Chain(dve, s_pre)

                    def statistics(part, tiles):
                        dve.wait_ge(s_emb[part], 16 * len(tiles))
                        for t in tiles:
                            pre.did(dve.bn_stats(stats[:, t, :], h[:, t, :]))
                        before = pre.n - len(tiles)
                        for n, t in enumerate(tiles):
                            pre.wait(before + n + 1)
                            pre.did(dve.bn_aggr(mv[:, t, :], stats[:, t, :]))
                        pre.wait()
                        cols = slice(tiles[0], tiles[-1] + 1)
                        dve.tensor_scalar(std[:, cols], mv[:, cols, 1], 1e-5, None, ALU.add).then_inc(s_var, 1)
                        dve.wait_ge(s_std, part + 2)
                        pre.did(dve.reciprocal(rstd[:, cols], std[:, cols]))
                        pre.wait()

                    def substitute(b, start, end, none=False):
                        if none:
                            return
                        link = Chain(dve, s_sub, b * CHAIN_X)
                        link.n = 2 * start
                        if start == 0:
                            dve.wait_ge(s_xst, b * 16 * HP + 1)
                            link.did(dve.tensor_copy(xt[:].rearrange("p k e i -> p (k e i)"), table("unit")))
                            dve.wait_ge(s_nx, b * 16 + 17)
                        else:
                            link.n += 1
                        for i in range(start, end):
                            k, m = i + 1, C - 1 - i
                            link.wait()
                            pr = prod[:, 0:k * 2 * m].rearrange("p (k e j) -> p k e j", e=2, j=m)
                            link.did(dve.tensor_tensor(
                                pr, nx[:, k:C, :, i].rearrange("p j e -> p e j").unsqueeze(1).to_broadcast([P, k, 2, m]),
                                xt[:, 0:k, :, i:i + 1].to_broadcast([P, k, 2, m]), ALU.mult))
                            link.wait()
                            ins = dve.tensor_tensor(xt[:, 0:k, :, k:C], xt[:, 0:k, :, k:C], pr, ALU.add)
                            if i < C - 2:
                                link.did(ins)
                            else:
                                ins.then_inc(s_inv, 1)
                        if end == C - 1:
                            assert link.n == CHAIN_X, link.n

                    def batch(b, first=False):
                        link = Chain(dve, s_chain, b * CHAIN_A)
                        dve.wait_ge(s_xtr, b * KH + 1)
                        for t in range(TILES):
                            dve.tensor_scalar(xhat[:, t, :], h[:, b * TILES + t, :], mv[:, b * TILES + t, 0:1],
                                              rstd[:, bass.ds(b * TILES + t, 1)],
                                              ALU.subtract, ALU.mult).then_inc(s_xhat, 1)
                        substitute(b - 1, 0, 5, first)
                        dve.wait_ge(s_bps, b + 2)
                        dve.tensor_tensor(lin[:], p_n[0][:, 0:TILES * H].rearrange("p (t h) -> p t h", t=TILES),
                                          bbeta_sb[:].unsqueeze(1).to_broadcast([P, TILES, H]), ALU.add).then_inc(s_lin, 1)
                        for n in range(6):
                            p, m = n // KH, n % KH
                            substitute(b - 1, 5 + n, 6 + n, first)
                            if n == 0:
                                dve.wait_ge(s_ttr, b * 4 + 1)
                            dve.wait_ge(s_raw, b * 6 + n + 2)
                            for j in range(TAPS):
                                w = conv_sb[:, p, m, j:j + 1]
                                x = raw[:, p, m, j:j + L]
                                if j == 0:
                                    ins = dve.tensor_scalar(cv[:, p, m, :], x, w, None, ALU.mult)
                                else:
                                    link.wait()
                                    ins = dve.scalar_tensor_tensor(cv[:, p, m, :], x, w, cv[:, p, m, :], ALU.mult, ALU.add)
                                if j < TAPS - 1:
                                    link.did(ins)
                                else:
                                    ins.then_inc(s_cv, 1)
                        substitute(b - 1, 11, 15, first)
                        dve.wait_ge(s_norm, b + 2)
                        link.did(dve.tensor_scalar(norm[:], norm[:], 1e-6, None, ALU.add))
                        link.wait()
                        dve.reciprocal(rnorm[:], norm[:]).then_inc(s_rn, 1)
                        dve.wait_ge(s_eta, b + 2)
                        link.did(dve.tensor_scalar(eta[:], th[:], 0.5, 0.5, ALU.mult, ALU.add))
                        link.did(dve.tensor_scalar(neta[:], th[:], -0.5, -0.5, ALU.mult, ALU.add))
                        dve.wait_ge(s_st, b * 64 + 1)
                        dve.wait_ge(s_gram, b + 1)
                        substitute(b - 1, 15, 18, first)
                        for n in range(4):
                            dst = (kT, qT)[n // KH]
                            dve.wait_ge(s_nb, b * 4 + n + 2)
                            dve.tensor_tensor(dst[:, n % KH, :], cv[:, n // KH, n % KH, :], p_n[(n + 1) % 2],
                                              ALU.mult).then_inc(s_nrm, 1)
                        link.wait()
                        substitute(b - 1, 18, 21, first)
                        for u in range(4):
                            t = slice(2 * (u % 2), 2 * (u % 2) + 2)
                            dve.wait_ge(s_kt if u < 2 else s_vt, b * 2 + u % 2 + 2)
                            src = (k_tok if u < 2 else v_tok)[:, t, :].rearrange("p t (h d) -> p t h d", d=DH)
                            dve.tensor_tensor(bv[:, t, :, u // 2, :].rearrange("p t h d -> p (t h) d"),
                                              src.rearrange("p t h d -> p (t h) d"),
                                              eta[:, t, :].rearrange("p t h -> p (t h)").unsqueeze(2).to_broadcast([P, 2 * H, DH]),
                                              ALU.mult).then_inc(s_bv, 1)
                        substitute(b - 1, 21, C - 1, first)
                        dve.wait_ge(s_ngst, b * 64 + 1)
                        dve.wait_ge(s_gram, b + 2)
                        for g in range(HP):
                            dve.tensor_tensor(ng[:, :, g, :].rearrange("p t (e j) -> p t e j", e=2),
                                              p_g[g % 4][:, :, g // 4, :].rearrange("p t (e j) -> p t e j", e=2),
                                              neta[:, :, 2 * g:2 * g + 2].unsqueeze(3).to_broadcast([P, TILES, 2, C]),
                                              ALU.mult).then_inc(s_ng, 1)
                        assert link.n == CHAIN_A, link.n

                    statistics(0, range(TILES))
                    batch(0, True)
                    statistics(1, range(TILES, NT))
                    with dve.Fori(1, B) as b:
                        batch(b)
                    substitute(B - 1, 0, C - 1)

        with ExitStack() as ctx:
            def pair_of(name, shape):
                return [sb(ctx, f"{name}{q}", shape) for q in range(2)]

            wout_sb = sb(ctx, "wout_sb", [P, KH, D])
            router_sb = sb(ctx, "router_sb", [P, KH, E])
            bout_sb = sb(ctx, "bout_sb", [P, D])
            rms_sb = sb(ctx, "rms_sb", [P, 1])
            kT = pair_of("kTb", [P, KH, L])
            qT = pair_of("qTb", [P, KH, L])
            qD = pair_of("qD", [P, KH, L])
            qM = pair_of("qM", [P, KH, 2, L])
            k_tok = pair_of("k_tok_b", [P, TILES, D])
            bv = pair_of("bv_b", [P, TILES, H, 2 * DH])
            xbd = pair_of("xbd", [P, HP, 2, P])
            st = pair_of("st", [P, H, P])
            yz_ch = sb(ctx, "yz_ch", [P, H // 4, P])
            y_tok = pair_of("y_tok", [P, D])
            z_tok = [pair_of(f"z_tok{i}_", [P, D]) for i in range(2)]
            yT = [pair_of(f"yT{i}_", [P, KH, P]) for i in range(2)]
            u = pair_of("u", [P, D])
            uw = pair_of("uw", [P, D])
            w_bd = pair_of("w_bd", [P, KH, P])
            w_old = [pair_of(f"w_old{i}_", [P, KH, P]) for i in range(2)]
            d_bd = pair_of("d_bd", [P, KH, P])
            o_even = sb(ctx, "o_even", [P, KH, P])
            o = pair_of("o", [P, KH, P])
            osq = pair_of("osq", [P, D])
            orms = pair_of("orms", [P, D])
            oT = pair_of("oT", [P, KH, P])
            hb = pair_of("hb", [P, D])
            stats = pair_of("stats_b", [P, 6])
            mv = pair_of("mv_b", [P, 2])
            var = pair_of("var_b", [P, 1])
            std = pair_of("std_b", [P, 1])
            rstd = pair_of("rstd_b", [P, 1])
            xn = pair_of("xn", [P, D])
            xnT = pair_of("xnT", [P, KH, P])
            score = sb(ctx, "score", [P, 2, E])
            best = pair_of("best", [P, 8])
            best_at = pair_of("best_at", [P, 8])
            best_at = [a[:].bitcast(U32) for a in best_at]
            best_f = pair_of("best_f", [P, TOP])
            tick = sb(ctx, "tick", [P, 1])

            p_r = [ps(ctx, f"p_r{q}", [P, D]) for q in range(2)]
            p_acc = [ps(ctx, f"p_acc{q}", [P, 2, KH, P]) for q in range(2)]
            p_yz = ps(ctx, "p_yz", [P, H, 2 * DH])
            p_tr = ps(ctx, "p_tr", [P, D])
            p_st = ps(ctx, "p_st", [P, KH, 2, P])
            p_o = ps(ctx, "p_o", [P, KH, 2, P])
            p_out = p_o[:].rearrange("p k e l -> p (k e l)")

            names = ("b_weights", "bv_loaded0", "bv_loaded1", "kT_loaded0", "kT_loaded1", "qT_loaded0", "qT_loaded1",
                     "k_loaded0", "k_loaded1", "xbd_zeroed", "xbd_loaded0", "xbd_loaded1", "q_masked", "q_scaled",
                     "yz_summed", "yz_ch_ready", "yz_turned", "y_out", "z_out", "y_transposed", "yT_ready", "weights_summed", "weights_masked",
                     "r_summed", "u_ready", "w_summed", "w_ready", "uw_ready", "d_summed", "d_ready",
                     "o_summed", "o_even_ready", "o_ready", "o_squared", "squares_summed", "orms_ready", "oT_ready",
                     "out_projected",
                     "hb_ready", "h_ready", "xn_ready", "xn_stored0", "xn_stored1", "xn_transposed", "xnT_ready", "scored", "score_copied",
                     "var_ready", "std_ready", "vector_chain_b")
            S = {n: sem(ctx, "b_" + n) for n in names}
            HEAD_STEPS, NORM_STEPS, GATE_STEPS = 1, 3, 5

            def after(n):
                return 1 if isinstance(n, int) and n < 0 else n + 2

            def loads(n):
                return 16 * n + 1

            class Tile:

                def __init__(self, pair, t):
                    self.pair, self.t = pair + t // TILES, t % TILES
                    self.n = self.pair * TILES + self.t

                def at(self, q):
                    return self.n * 2 + q

                def chunk(self, c, q):
                    return (self.n * CH + c) * 2 + q

                def read(self, c, q):
                    return (self.pair * (NC_BATCH - 1) + self.t * CH + c - 1) * 2 + q

                def inner(self, q):
                    return (self.pair * (TILES - 1) + self.t) * 2 + q

                def token_tile(self, q):
                    return (self.pair * 2 + q) * TILES + self.t

            def pipeline(eng, run_pair):
                run_pair(0, True, False)
                with eng.Fori(1, B // 2 - 1) as pair:
                    run_pair(pair, False, False)
                run_pair(B // 2 - 1, False, True)

            start_at_one()
            with nc.Block() as block:
                @block.sync
                def _(sp):
                    def load_bv(pair, q):
                        sp.dma_start(bv[q][:].rearrange("p t h d -> p (t h d)"), bv_dram[pair * 2 + q]
                                     ).then_inc(S[f"bv_loaded{q}"], 16)

                    def load_kT(pair, q):
                        sp.dma_start(kT[q][:].rearrange("p k l -> p (k l)"), kT_dram[pair * 2 + q]
                                     ).then_inc(S[f"kT_loaded{q}"], 16)

                    def load_qT(pair, q):
                        sp.dma_start(qT[q][:].rearrange("p k l -> p (k l)"), qT_dram[pair * 2 + q]
                                     ).then_inc(S[f"qT_loaded{q}"], 16)

                    def load_k(pair, q):
                        sp.dma_start(k_tok[q][:].rearrange("p t d -> p (t d)"), k_dram[pair * 2 + q]
                                     ).then_inc(S[f"k_loaded{q}"], 16)

                    def load_xbd(T, q):
                        for c in range(CH):
                            sp.dma_start(xbd[q][c * C:(c + 1) * C, :, :, c * C:(c + 1) * C].rearrange("p g e i -> p (g e) i"),
                                         x_dram[T.pair * 2 + q, T.t * P + c * C:T.t * P + (c + 1) * C, :].rearrange(
                                             "p (g i) -> p g i", i=C)).then_inc(S[f"xbd_loaded{q}"], 16)

                    for dst, src in ((wout_sb[:], wout), (router_sb[:], router), (bout_sb[:], bout), (rms_sb[:], rms)):
                        sp.dma_start(dst, src).then_inc(S["b_weights"], 16)
                    for q in range(2):
                        load_bv(0, q)
                    sp.wait_ge(S["xbd_zeroed"], after(1))
                    for q in range(2):
                        load_xbd(Tile(0, 0), q)
                    for load in (load_qT, load_kT, load_k):
                        for q in range(2):
                            load(0, q)

                    def run_pair(pair, first, final):
                        for t in range(TILES):
                            T = Tile(pair, t)
                            if t < TILES - 1 or not final:
                                for q in range(2):
                                    sp.wait_ge(S["yz_summed"], after(T.at(q)))
                                    load_xbd(Tile(pair, t + 1), q)
                                    if t == TILES - 1:
                                        load_bv(pair + 1, q)
                        if not final:
                            for q in range(2):
                                sp.wait_ge(S["weights_summed"], after(T.chunk(CH - 1, q)))
                                load_kT(pair + 1, q)
                            for q in range(2):
                                sp.wait_ge(S["o_summed"], after(T.at(q)))
                                load_qT(pair + 1, q)
                                sp.wait_ge(S["w_summed"], after(T.chunk(CH - 1, q)))
                                load_k(pair + 1, q)

                    pipeline(sp, run_pair)

                @block.gpsimd
                def _(pool):
                    for q in range(2):
                        pool.memset(xbd[q][:], 0.0).then_inc(S["xbd_zeroed"], 1)
                    pool.wait_ge(S["b_weights"], loads(4))

                    def residual(T, q):
                        pool.wait_ge(S["h_ready"], after(T.at(q) - 2))
                        pool.tensor_tensor(hb[q][:], h[:, T.token_tile(q), :], bout_sb[:], ALU.add).then_inc(S["hb_ready"], 1)

                    def scale_q(pair, q):
                        a, _n = where["minus_tri_row"]
                        pool.wait_ge(S[f"qT_loaded{q}"], loads(pair + 1))
                        pool.tensor_tensor(qD[q][:], qT[q][:], cst[:, a:a + L].unsqueeze(1).to_broadcast([P, KH, L]),
                                           ALU.mult).then_inc(S["q_scaled"], 1)

                    def run_pair(pair, first, final):
                        for t in range(TILES):
                            T, before = Tile(pair, t), Tile(pair if t else pair - 1, (t - 1) % TILES)
                            for q in range(2):
                                if t or not first:
                                    residual(before, q)
                                if t == 0:
                                    scale_q(pair, q)
                            for q in range(2):
                                if t < TILES - 1:
                                    a, _n = where["tri_before"]
                                    pool.wait_ge(S["d_summed"], after(T.inner(q) - 2))
                                    pool.wait_ge(S["u_ready"], after(T.chunk(CH - 1, q)))
                                    pool.tensor_tensor(uw[q][:], u[q][:], cst[:, a + t:a + t + 1].to_broadcast([P, D]),
                                                       ALU.mult).then_inc(S["uw_ready"], 1)
                        if final:
                            for q in range(2):
                                residual(T, q)

                    pipeline(pool, run_pair)

                @block.tensor
                def _(pe):
                    pe.wait_ge(S["b_weights"], loads(4))

                    def yz(T, q):
                        pe.wait_ge(S[f"bv_loaded{q}"], loads(T.pair + 1))
                        pe.wait_ge(S[f"xbd_loaded{q}"], loads((T.n + 1) * CH))
                        pe.wait_ge(S["z_out"], after(T.at(q) - 1))
                        for hd in range(H):
                            r, hs = slice(32 * (hd % 4), 32 * (hd % 4) + 32), hd // 4 * 4
                            ins = pe.matmul(p_yz[r, hs:hs + 4, :].rearrange("p h d -> p (h d)"), bv[q][:, T.t, hd, :],
                                            xbd[q][:, hd // 2, hd % 2, :], start=True, stop=True)
                        ins.then_inc(S["yz_summed"], 1)

                    def yz_transpose(T, q):
                        pe.wait_ge(S["yz_ch_ready"], after(T.at(q)))
                        for n in range(H // 4):
                            ins = pe.transpose(p_yz[:, 4 * n:4 * n + 4, :].rearrange("p h d -> p (h d)"), yz_ch[:, n, :], ident)
                        ins.then_inc(S["yz_turned"], 1)

                    def turn(src, done):
                        for k in range(KH):
                            ins = pe.transpose(p_tr[:, k * P:(k + 1) * P], src[:, k * P:(k + 1) * P], ident)
                        ins.then_inc(S[done], 1)

                    def y_transpose(T, q):
                        pe.wait_ge(S["y_out"], after(T.at(q)))
                        pe.wait_ge(S["yT_ready"], after(T.at(q) - 1))
                        if q == 0:
                            pe.wait_ge(S["orms_ready"], after(T.at(1) - 4))
                        turn(y_tok[q], "y_transposed")

                    def weights(T, n, q):
                        if n == 0 and T.t == 0:
                            pe.wait_ge(S[f"kT_loaded{q}"], loads(T.pair + 1))
                            pe.wait_ge(S["q_masked"], after(T.pair * 8 + 4 * q + 3))
                        pe.wait_ge(S["weights_masked"], after(T.chunk(n, q) - 1))
                        r = slice(32 * n, 32 * n + 32)
                        for k in range(KH):
                            ins = pe.matmul(p_st[:, k, :, :], kT[q][r, k, T.t * P:(T.t + 1) * P],
                                            qM[q][r, k, :, T.t * P:(T.t + 1) * P], start=True, stop=True)
                        ins.then_inc(S["weights_summed"], 1)

                    def recur_r(T, c, q):
                        if T.t == 0 and c == 0:
                            return
                        pe.wait_ge(S["w_ready"], after(T.chunk(c, q) - 2))
                        if c == 0:
                            pe.wait_ge(S["yT_ready"], after(T.at(q)))
                        state = w_bd[q] if c else w_old[T.t % 2][q]
                        for k in range(KH):
                            ins = pe.matmul(p_r[q][c * C:(c + 1) * C, k * P:(k + 1) * P],
                                            yT[T.t % 2][q][:, k, c * C:(c + 1) * C], state[:, k, :], start=True, stop=True)
                        ins.then_inc(S["r_summed"], 1)

                    def recur_w(T, c, q):
                        pe.wait_ge(S["u_ready"], after(T.chunk(c, q)))
                        if c == 0:
                            if T.t:
                                pe.wait_ge(S["d_ready"], after(T.inner(q) - 2))
                            else:
                                pe.wait_ge(S[f"k_loaded{q}"], loads(T.pair + 1))
                                pe.wait_ge(S["w_ready"], after(T.chunk(0, q) - 2))
                        for k in range(KH):
                            ins = pe.matmul(p_acc[q][:, 0, k, :], k_tok[q][c * C:(c + 1) * C, T.t, k * P:(k + 1) * P],
                                            u[q][c * C:(c + 1) * C, k * P:(k + 1) * P],
                                            start=(T.t == 0 and c == 0 and k == 0), stop=False, skip_group_check=True)
                        ins.then_inc(S["w_summed"], 1)

                    def average(T, q):
                        if T.t == TILES - 1:
                            return
                        pe.wait_ge(S["uw_ready"], after(T.inner(q)))
                        pe.wait_ge(S["w_ready"], after(T.chunk(CH - 1, q)))
                        for k in range(KH):
                            ins = pe.matmul(p_acc[q][:, 1, k, :], k_tok[q][:, T.t, k * P:(k + 1) * P],
                                            uw[q][:, k * P:(k + 1) * P], start=False, stop=False, skip_group_check=True)
                        ins.then_inc(S["d_summed"], 1)

                    def old_reads(T, q):
                        pe.wait_ge(S["o_ready"], after(T.at(q) - 1))
                        if q == 0:
                            pe.wait_ge(S["h_ready"], after(T.at(1) - 2))
                        if T.t == 0:
                            return
                        pe.wait_ge(S["d_ready"], after(T.inner(q) - 2))
                        pe.wait_ge(S["q_scaled"], after(T.pair * 2 + q))
                        for reader, state in ((qT[q], w_old[T.t % 2][q]), (qD[q], d_bd[q])):
                            for k in range(KH):
                                pe.matmul(p_o[:, k, :, :], state[:, k, :],
                                          reader[:, k, T.t * P:(T.t + 1) * P].unsqueeze(1).to_broadcast([P, 2, P]),
                                          start=(k == 0 and reader is qT[q]), stop=False, skip_group_check=True)

                    def new_reads(T, q):
                        pe.wait_ge(S["weights_masked"], after(T.chunk(CH - 1, q)))
                        for g in range(HP):
                            ins = pe.matmul(p_o[32 * (g % 4):32 * (g % 4) + 32, g // 4, :, :], u[q][:, 32 * g:32 * g + 32],
                                            st[q][:, 2 * g:2 * g + 2, :], start=(T.t == 0 and g < 4), stop=(g >= 4),
                                            skip_group_check=True)
                        ins.then_inc(S["o_summed"], 1)

                    def sum_squares(T, q):
                        pe.wait_ge(S["o_squared"], after(T.at(q)))
                        if q:
                            pe.wait_ge(S["orms_ready"], after(T.at(0)))
                        else:
                            pe.wait_ge(S["xnT_ready"], after(T.at(1) - 2))
                        pe.matmul(p_tr[:], headblock, osq[q][:], start=True, stop=True).then_inc(S["squares_summed"], 1)

                    def project(T, q):
                        pe.wait_ge(S["oT_ready"], after(T.at(q)))
                        if q:
                            pe.wait_ge(S["h_ready"], after(T.at(0)))
                        else:
                            pe.wait_ge(S["o_ready"], after(T.at(1)))
                            pe.wait_ge(S["score_copied"], after(T.n - 1))
                        for k in range(KH):
                            ins = pe.matmul(p_out[:, 0:D], oT[q][:, k, :], wout_sb[:, k, :], start=(k == 0), stop=(k == KH - 1))
                        ins.then_inc(S["out_projected"], 1)

                    def xn_transpose(T, q, final):
                        pe.wait_ge(S["xn_ready"], after(T.at(q)))
                        if q:
                            pe.wait_ge(S["xnT_ready"], after(T.at(0)))
                        else:
                            pe.wait_ge(S["orms_ready"], after(T.at(1)))
                            if not final:
                                pe.wait_ge(S["yT_ready"], after(T.at(1) + 4))
                        turn(xn[q], "xn_transposed")

                    def route(T, final):
                        pe.wait_ge(S["xnT_ready"], after(T.at(1)))
                        if final:
                            pe.wait_ge(S["h_ready"], after(T.at(1)))
                        else:
                            pe.wait_ge(S["o_ready"], after(T.at(1) + 2))
                        for q in range(2):
                            for k in range(KH):
                                ins = pe.matmul(p_out[:, q * E:(q + 1) * E], xnT[q][:, k, :], router_sb[:, k, :], start=(k == 0),
                                                stop=(k == KH - 1))
                        ins.then_inc(S["scored"], 1)

                    for q in range(2):
                        yz(Tile(0, 0), q)
                        yz_transpose(Tile(0, 0), q)
                    for q in range(2):
                        y_transpose(Tile(0, 0), q)

                    def run_pair(pair, first, final):
                        for t in range(TILES):
                            T, before, nxt = Tile(pair, t), Tile(pair if t else pair - 1, (t - 1) % TILES), Tile(pair, t + 1)
                            has_before, has_next = t or not first, t < TILES - 1 or not final
                            for c in range(CH):
                                for q in range(2):
                                    recur_r(T, c, q)
                                weights(T, c, 0)
                                if has_before and c == 0:
                                    sum_squares(before, 0)
                                if has_next and c == 2:
                                    yz_transpose(nxt, 0)
                                if has_before and c == 2:
                                    project(before, 0)
                                if has_next and c == 3:
                                    y_transpose(nxt, 0)
                                for q in range(2):
                                    recur_w(T, c, q)
                                weights(T, c, 1)
                                if has_before and c == 0:
                                    sum_squares(before, 1)
                                if has_before and c == 2:
                                    project(before, 1)
                                if has_next and c in (1, 2):
                                    yz(nxt, c - 1)
                                if has_next and c == 3:
                                    yz_transpose(nxt, 1)
                            for q in range(2):
                                if has_next and q == 0:
                                    y_transpose(nxt, 1)
                                old_reads(T, q)
                                average(T, q)
                                new_reads(T, q)
                                if has_before:
                                    xn_transpose(before, q, not has_next)
                            if has_before:
                                route(before, False)
                        if final:
                            for step in (sum_squares, project):
                                for q in range(2):
                                    step(T, q)
                            for q in range(2):
                                xn_transpose(T, q, True)
                            route(T, True)

                    pipeline(pe, run_pair)

                @block.scalar
                def _(act):
                    act.wait_ge(S["b_weights"], loads(4))

                    def yz_ch_out(T, q):
                        act.wait_ge(S["yz_summed"], after(T.at(q)))
                        act.wait_ge(S["yz_turned"], after(T.at(q) - 1))
                        act.copy(yz_ch[:].rearrange("p n l -> p (n l)"), p_yz[:].rearrange("p h d -> p (h d)")
                                 ).then_inc(S["yz_ch_ready"], 1)

                    def yz_out(T, q):
                        act.wait_ge(S["yz_turned"], after(T.at(q)))
                        act.wait_ge(S["y_transposed"], after(T.at(q) - 2))
                        act.copy(y_tok[q][:].rearrange("p (h d) -> p h d", d=DH), p_yz[:, :, 0:DH]).then_inc(S["y_out"], 1)
                        act.wait_ge(S["u_ready"], after(T.chunk(-CH - 1, q)))
                        act.copy(z_tok[T.t % 2][q][:].rearrange("p (h d) -> p h d", d=DH),
                                 p_yz[:, :, DH:2 * DH]).then_inc(S["z_out"], 1)

                    def yT_out(T, q):
                        act.wait_ge(S["y_transposed"], after(T.at(q)))
                        act.wait_ge(S["u_ready"], after(T.chunk(-CH - 1, q)))
                        act.copy(yT[T.t % 2][q][:].rearrange("p k l -> p (k l)"), p_tr[:]).then_inc(S["yT_ready"], 1)

                    def mask_q(pair, q):
                        a, _n = where["parity"]
                        act.wait_ge(S[f"qT_loaded{q}"], loads(pair + 1))
                        for k in range(KH):
                            for e in range(2):
                                act.activation(qM[q][:, k, e, :], qT[q][:, k, :], ACT.Copy,
                                               scale=cst[:, a + e:a + e + 1]).then_inc(S["q_masked"], 1)

                    def square(T, q):
                        act.wait_ge(S["o_ready"], after(T.at(q)))
                        act.activation(osq[q][:], o[q][:].rearrange("p k l -> p (k l)"), ACT.Square).then_inc(S["o_squared"], 1)

                    def even_out(T, q):
                        a, _n = where["parity"]
                        act.wait_ge(S["o_summed"], after(T.at(q)))
                        act.wait_ge(S["o_ready"], after(T.at(q) - 1))
                        act.activation(o_even[:], p_o[:, :, 0, :], ACT.Copy, scale=cst[:, a:a + 1]).then_inc(S["o_even_ready"], 1)

                    def head_sqrt(T, q):
                        act.wait_ge(S["squares_summed"], after(T.at(q)))
                        act.activation(orms[q][:], p_tr[:], ACT.Sqrt, bias=table("rms_eps"), scale=1.0 / DH
                                       ).then_inc(S["orms_ready"], 1)

                    def row_sqrt(T, q):
                        act.wait_ge(S["var_ready"], after(T.at(q)))
                        act.activation(std[q][:], var[q][:], ACT.Sqrt).then_inc(S["std_ready"], 1)

                    def xnT_out(T, q):
                        act.wait_ge(S["xn_transposed"], after(T.at(q)))
                        act.copy(xnT[q][:].rearrange("p k l -> p (k l)"), p_tr[:]).then_inc(S["xnT_ready"], 1)

                    def store_xn(T, q):
                        act.wait_ge(S["xn_ready"], after(T.at(q)))
                        act.dma_start(xn_dram[T.token_tile(q)], xn[q][:]).then_inc(S[f"xn_stored{q}"], 16)

                    for q in range(2):
                        yz_ch_out(Tile(0, 0), q)
                        yz_out(Tile(0, 0), q)
                    for q in range(2):
                        yT_out(Tile(0, 0), q)

                    def run_pair(pair, first, final):
                        for t in range(TILES):
                            T, before, nxt = Tile(pair, t), Tile(pair if t else pair - 1, (t - 1) % TILES), Tile(pair, t + 1)
                            has_before, has_next = t or not first, t < TILES - 1 or not final
                            if t == 0:
                                for q in range(2):
                                    mask_q(pair, q)
                            if has_before:
                                for q in range(2):
                                    head_sqrt(before, q)
                            if has_next:
                                yz_ch_out(nxt, 0)
                                yz_out(nxt, 0)
                                yz_ch_out(nxt, 1)
                            for q in range(2):
                                if has_before:
                                    row_sqrt(before, q)
                                if has_next:
                                    if q:
                                        yz_out(nxt, 1)
                                    yT_out(nxt, q)
                            for q in range(2):
                                if has_before:
                                    store_xn(before, q)
                            for q in range(2):
                                even_out(T, q)
                                square(T, q)
                                if has_before:
                                    xnT_out(before, q)
                        if final:
                            for step in (head_sqrt, row_sqrt, store_xn, xnT_out):
                                for q in range(2):
                                    step(T, q)

                    pipeline(act, run_pair)
                    for q in range(2):
                        act.wait_ge(S[f"xn_stored{q}"], loads(NT // 2))

                @block.vector
                def _(dve):
                    dve.wait_ge(S["b_weights"], loads(4))
                    link = Chain(dve, S["vector_chain_b"])

                    def update_u(T, c, q):
                        r = slice(c * C, (c + 1) * C)
                        if c == 0:
                            dve.wait_ge(S["z_out"], after(T.at(q)))
                            dve.wait_ge(S["o_summed"], after(T.at(q) - 2))
                            dve.wait_ge(S["uw_ready"], after(T.inner(q) - 2))
                        if T.t == 0 and c == 0:
                            dve.tensor_copy(u[q][r, :], z_tok[0][q][r, :]).then_inc(S["u_ready"], 1)
                        else:
                            dve.wait_ge(S["r_summed"], after(T.read(c, q)))
                            dve.tensor_tensor(u[q][r, :], z_tok[T.t % 2][q][r, :], p_r[q][r, :],
                                              ALU.subtract).then_inc(S["u_ready"], 1)

                    def update_w(T, c, q):
                        dve.wait_ge(S["w_summed"], after(T.chunk(c, q)))
                        state = w_bd[q] if c < CH - 1 else w_old[(T.t + 1) % 2][q]
                        dve.tensor_tensor(state[:], p_acc[q][:, 0], headblock.unsqueeze(1).to_broadcast([P, KH, P]),
                                          ALU.mult).then_inc(S["w_ready"], 1)

                    def update_d(T, q):
                        if T.t == TILES - 1:
                            return
                        dve.wait_ge(S["d_summed"], after(T.inner(q)))
                        dve.tensor_tensor(d_bd[q][:], p_acc[q][:, 1], headblock.unsqueeze(1).to_broadcast([P, KH, P]),
                                          ALU.mult).then_inc(S["d_ready"], 1)

                    def mask(T, n, q):
                        dve.wait_ge(S["weights_summed"], after(T.chunk(n, q)))
                        if n == 0:
                            dve.wait_ge(S["o_summed"], after(T.at(q) - 2))
                        a, _n = where["average"]
                        dve.tensor_tensor(st[q][:].rearrange("p (k h) i -> p k h i", k=KH)[:, :, 2 * n:2 * n + 2, :],
                                          p_st[:],
                                          cst[:, a + T.t * P:a + (T.t + 1) * P].unsqueeze(1).unsqueeze(1).to_broadcast(
                                              [P, KH, 2, P]),
                                          ALU.mult).then_inc(S["weights_masked"], 1)

                    def read_out(T, q):
                        a, _n = where["parity"]
                        dve.wait_ge(S["o_even_ready"], after(T.at(q)))
                        dve.wait_ge(S["oT_ready"], after(T.at(q) - 2))
                        dve.scalar_tensor_tensor(o[q][:], p_o[:, :, 1, :], cst[:, a + 1:a + 2], o_even[:], ALU.mult, ALU.add
                                                 ).then_inc(S["o_ready"], 1)

                    def head_norm(T, q):
                        dve.wait_ge(S["orms_ready"], after(T.at(q)))
                        link.did(dve.reciprocal(orms[q][:], orms[q][:]))
                        link.wait()
                        dve.wait_ge(S["out_projected"], after(T.at(q) - 2))
                        dve.scalar_tensor_tensor(oT[q][:].rearrange("p k l -> p (k l)"), o[q][:].rearrange("p k l -> p (k l)"),
                                                 rms_sb[:, 0:1], orms[q][:], ALU.mult, ALU.mult).then_inc(S["oT_ready"], 1)

                    def residual(T, q):
                        dve.wait_ge(S["out_projected"], after(T.at(q)))
                        dve.wait_ge(S["hb_ready"], after(T.at(q)))
                        hh = h[:, T.token_tile(q), :]
                        dve.tensor_tensor(hh, p_out[:, 0:D], hb[q][:], ALU.add).then_inc(S["h_ready"], 1)
                        wait_apart(dve, tick[:], S["h_ready"], after(T.at(q)) - 1)
                        link.did(dve.bn_stats(stats[q][:], hh))
                        wait_apart(dve, tick[:], link.sem, link.base + link.n)
                        link.did(dve.bn_aggr(mv[q][:], stats[q][:]))
                        link.wait()
                        dve.tensor_scalar(var[q][:], mv[q][:, 1:2], 1e-5, None, ALU.add).then_inc(S["var_ready"], 1)

                    def norm(T, q):
                        hh = h[:, T.token_tile(q), :]
                        dve.wait_ge(S["std_ready"], after(T.at(q)))
                        link.did(dve.reciprocal(rstd[q][:], std[q][:]))
                        link.wait()
                        dve.wait_ge(S[f"xn_stored{q}"], loads(T.n))
                        dve.tensor_scalar(xn[q][:], hh, mv[q][:, 0:1], rstd[q][:, 0:1], ALU.subtract, ALU.mult
                                          ).then_inc(S["xn_ready"], 1)

                    def copy_score(T):
                        dve.wait_ge(S["scored"], after(T.n))
                        dve.tensor_copy(score[:].rearrange("p q e -> p (q e)"), p_out[:, 0:2 * E]).then_inc(S["score_copied"], 1)

                    def gate(T, q):
                        wait_apart(dve, tick[:], S["score_copied"], after(T.n) - 1)
                        link.did(dve.max(best[q][:], score[:, q, :]))
                        wait_apart(dve, tick[:], link.sem, link.base + link.n)
                        link.did(dve.max_index(best_at[q], best[q][:], score[:, q, :]))
                        link.wait()
                        link.did(dve.tensor_copy(best_f[q][:], best_at[q][:, 0:TOP]))
                        link.wait()
                        for k in range(TOP):
                            link.did(dve.tensor_scalar(picks[:, T.token_tile(q), k, :], table("experts"), best_f[q][:, k:k + 1],
                                                       None, ALU.is_equal))
                        dve.tensor_copy(best_score[:, T.token_tile(q), :], best[q][:, 0:TOP])

                    per_tile = 2 * (HEAD_STEPS + NORM_STEPS + GATE_STEPS)

                    def run_pair(pair, first, final):
                        link.base, link.n = (0 if first else pair * (TILES * per_tile) - per_tile), 0
                        for t in range(TILES):
                            T, before = Tile(pair, t), Tile(pair if t else pair - 1, (t - 1) % TILES)
                            has_before = t or not first
                            for c in range(CH):
                                for q in range(2):
                                    update_u(T, c, q)
                                mask(T, c, 0)
                                if has_before:
                                    if c == 1:
                                        head_norm(before, 0)
                                    if c == 2:
                                        residual(before, 0)
                                    if c == 3:
                                        norm(before, 0)
                                for q in range(2):
                                    update_w(T, c, q)
                                mask(T, c, 1)
                                if has_before:
                                    if c == 1:
                                        head_norm(before, 1)
                                    if c == 2:
                                        residual(before, 1)
                                    if c == 3:
                                        norm(before, 1)
                            for q in range(2):
                                update_d(T, q)
                                read_out(T, q)
                            if has_before:
                                copy_score(before)
                                for q in range(2):
                                    gate(before, q)
                        if final:
                            for step in (head_norm, residual, norm):
                                for q in range(2):
                                    step(T, q)
                            copy_score(T)
                            for q in range(2):
                                gate(T, q)
                        assert link.n == per_tile * (TILES - first + final), (link.n, per_tile)

                    pipeline(dve, run_pair)

        with ExitStack() as ctx:
            SHARED = E
            HALF = NT // 2
            wi = sb(ctx, "wi", [P, E + 1, KH, F])
            ws = sb(ctx, "ws", [P, E + 1, KH, F])
            wo = sb(ctx, "wo", [P, E + 1, FK, D])
            x_in = [sb(ctx, f"x_in{i}", [P, D]) for i in range(2)]
            xT = [sb(ctx, f"xT_c{i}", [P, KH, P]) for i in range(2)]
            silu = [sb(ctx, f"silu{i}", [P, F]) for i in range(2)]
            hid = [sb(ctx, f"hid{i}", [P, F]) for i in range(2)]
            hidT = [sb(ctx, f"hidT{i}", [P, FK, P]) for i in range(2)]
            y_sb = [sb(ctx, f"y_sb{i}", [P, D]) for i in range(2)]
            rows = [sb(ctx, f"rows{i}", [P, 2, TOP, D]) for i in range(2)]
            at = [sb(ctx, f"at{i}", [P, 2, TOP], U32) for i in range(2)]
            x_rows = sb(ctx, "x_rows", [P, 4, D])
            gate = sb(ctx, "gate", [P, NT, TOP])
            slot_of = sb(ctx, "slot_of", [P, NT, TOP], U32)
            expert_of = sb(ctx, "expert_of", [P, SLOTS], I32)
            count = sb(ctx, "count", [P, NT, E])
            total = sb(ctx, "total", [P, NT, E])
            upto = sb(ctx, "upto", [P, E, NT])
            place = sb(ctx, "place", [P, NT, E])
            chosen = sb(ctx, "chosen", [P, NT, TOP, E])
            slot_f = sb(ctx, "slot_f", [P, NT, TOP])
            padded_i = sb(ctx, "padded_i", [P, E], I32)
            padded = sb(ctx, "padded", [P, E])
            end = sb(ctx, "end", [P, E])
            base = sb(ctx, "base", [P, E])
            past = sb(ctx, "past", [P, SLOTS, E])
            past_n = sb(ctx, "past_n", [P, SLOTS])
            tick = sb(ctx, "tick_c", [P, 1])

            p_x = ps(ctx, "p_x", [P, KH, P])
            p_i = ps(ctx, "p_i", [P, F])
            p_s = ps(ctx, "p_s", [P, F])
            p_h = ps(ctx, "p_h", [P, FK, P])
            p_y = ps(ctx, "p_y", [P, D])
            p_c = ps(ctx, "p_c", [P, 2, NT * E])

            s_w = sem(ctx, "c_weights")
            s_w_shared = sem(ctx, "c_weights_shared")
            FFN = ("x_loaded0", "x_loaded1", "x_turned", "xT_ready", "mid_summed", "sw_summed", "silu_ready", "hid_ready",
                   "hid_turned", "hidT_ready", "y_summed", "y_out")

            def turn_x(pe, S, c, i, pair):
                pe.wait_ge(S[f"x_loaded{i}"], pair * 16 + 17)
                pe.wait_ge(S["xT_ready"], c + 1)
                for k in range(KH):
                    ins = pe.transpose(p_x[:, k, :], x_in[i][:, k * P:(k + 1) * P], ident)
                ins.then_inc(S["x_turned"], 1)

            def up_mid(pe, S, c, i, e):
                pe.wait_ge(S["xT_ready"], c + 2)
                pe.wait_ge(S["silu_ready"], c + 1)
                for k in range(KH):
                    ins = pe.matmul(p_i[:], xT[i][:, k, :], wi[:, e, k, :], start=(k == 0), stop=(k == KH - 1))
                ins.then_inc(S["mid_summed"], 1)

            def up_sw(pe, S, c, i, e):
                pe.wait_ge(S["hid_ready"], c + 1)
                for k in range(KH):
                    ins = pe.matmul(p_s[:], xT[i][:, k, :], ws[:, e, k, :], start=(k == 0), stop=(k == KH - 1))
                ins.then_inc(S["sw_summed"], 1)

            def turn_hid(pe, S, c, i):
                pe.wait_ge(S["hid_ready"], c + 2)
                pe.wait_ge(S["hidT_ready"], c + 1)
                for f in range(FK):
                    ins = pe.transpose(p_h[:, f, :], hid[i][:, f * P:(f + 1) * P], ident)
                ins.then_inc(S["hid_turned"], 1)

            def down(pe, S, c, i, e):
                pe.wait_ge(S["hidT_ready"], c + 2)
                pe.wait_ge(S["y_out"], c + 1)
                for f in range(FK):
                    ins = pe.matmul(p_y[:], hidT[i][:, f, :], wo[:, e, f, :], start=(f == 0), stop=(f == FK - 1))
                ins.then_inc(S["y_summed"], 1)

            def xT_out(act, S, c, i):
                act.wait_ge(S["x_turned"], c + 2)
                act.copy(xT[i][:], p_x[:]).then_inc(S["xT_ready"], 1)

            def silu_out(act, S, c, i):
                act.wait_ge(S["mid_summed"], c + 2)
                act.activation(silu[i][:], p_i[:], ACT.Silu).then_inc(S["silu_ready"], 1)

            def hidT_out(act, S, c, i):
                act.wait_ge(S["hid_turned"], c + 2)
                act.copy(hidT[i][:], p_h[:]).then_inc(S["hidT_ready"], 1)

            def hid_out(dve, S, c, i):
                dve.wait_ge(S["silu_ready"], c + 2)
                dve.wait_ge(S["sw_summed"], c + 2)
                dve.tensor_tensor(hid[i][:], p_s[:], silu[i][:], ALU.mult).then_inc(S["hid_ready"], 1)

            def shared_pe(pe, S, c):
                turn_x(pe, S, c, 0, c // 2 if isinstance(c, int) else S["pair"])
                turn_x(pe, S, c + 1, 1, S["pair"])
                up_mid(pe, S, c, 0, SHARED)
                up_sw(pe, S, c, 0, SHARED)
                up_mid(pe, S, c + 1, 1, SHARED)
                turn_hid(pe, S, c, 0)
                up_sw(pe, S, c + 1, 1, SHARED)
                down(pe, S, c, 0, SHARED)
                turn_hid(pe, S, c + 1, 1)
                down(pe, S, c + 1, 1, SHARED)

            def shared_act(act, S, c):
                xT_out(act, S, c, 0)
                xT_out(act, S, c + 1, 1)
                silu_out(act, S, c, 0)
                silu_out(act, S, c + 1, 1)
                hidT_out(act, S, c, 0)
                hidT_out(act, S, c + 1, 1)

            def shared_add(dve, S, c, t):
                dve.wait_ge(S["y_summed"], c + 2)
                dve.tensor_tensor(h[:, t, :], p_y[:], h[:, t, :], ALU.add).then_inc(S["y_out"], 1)

            S = {n: sem(ctx, "c1_" + n) for n in FFN + ("counted", "chain", "gates_ready", "rows_in", "rows_ready",
                                                        "routed")}
            s_scat = [ctx.enter_context(nc.semaphore(f"scattered{i}")) for i in range(2)]
            start_at_one()
            with nc.Block() as block:
                @block.sync
                def _(sp):
                    for dst, src in ((wi, w_in), (ws, w_sw), (wo, w_out)):
                        sp.dma_start(dst[:, SHARED], src[SHARED]).then_inc(s_w_shared, 16)
                    with sp.Fori(0, NT // 4) as j:
                        sp.wait_ge(S["x_turned"], j * 2 + 1)
                        for i in range(2):
                            sp.dma_start(x_in[i][:], xn_dram[j * 2 + i]).then_inc(S[f"x_loaded{i}"], 16)
                        sp.wait_ge(S["rows_ready"], j * 8 + 1)
                        sp.dma_start(x_rows[:], xn_dram[bass.ds(j * 4, 4)].rearrange("t p d -> p t d")).then_inc(S["rows_in"], 16)

                @block.tensor
                def _(pe):
                    pe.wait_ge(S["counted"], 2)
                    for n, what in enumerate(("before", "ones")):
                        ins = pe.matmul(p_c[:, n, :], table(what), count[:].rearrange("p t e -> p (t e)"), start=(n == 0),
                                        stop=True, skip_group_check=True)
                    ins.then_inc(S["counted"], 1)
                    pe.wait_ge(s_w_shared, 49)
                    with pe.Fori(0, NT // 4) as j:
                        shared_pe(pe, {**S, "pair": j}, j * 2)

                @block.scalar
                def _(act):
                    act.activation(gate[:], best_score[:], ACT.Sigmoid).then_inc(S["gates_ready"], 1)
                    for dst, src in ((wi, w_in), (ws, w_sw), (wo, w_out)):
                        for e in range(E):
                            act.dma_start(dst[:, e], src[e]).then_inc(s_w, 16)
                    with act.Fori(0, NT // 4) as j:
                        shared_act(act, S, j * 2)

                @block.vector
                def _(dve):
                    link = Chain(dve, S["chain"])
                    dve.tensor_tensor(count[:], picks[:, :, 0, :], picks[:, :, 1, :], ALU.add).then_inc(S["counted"], 1)
                    dve.wait_ge(S["counted"], 3)
                    link.did(dve.tensor_copy(total[:].rearrange("p t e -> p (t e)"), p_c[:, 1, :]))
                    link.wait()
                    for e in range(E):
                        link.did(dve.tensor_tensor_scan(upto[:, e, :], total[:, :, e], table("zeros_nt"), 0.0, ALU.add, ALU.add))
                    link.wait()
                    link.did(dve.tensor_scalar(padded_i[:], upto[:, :, NT - 1], float(P - 1), None, ALU.add))
                    link.wait()
                    link.did(dve.tensor_scalar(padded_i[:], padded_i[:], 7, 7, ALU.arith_shift_right, ALU.logical_shift_left))
                    link.wait()
                    link.did(dve.tensor_copy(padded[:], padded_i[:]))
                    link.wait()
                    link.did(dve.tensor_tensor_scan(end[:], padded[:], table("zeros_nt")[:, 0:E], 0.0, ALU.add, ALU.add))
                    link.wait()
                    link.did(dve.tensor_tensor(base[:], end[:], padded[:], ALU.subtract))
                    link.did(dve.tensor_tensor(place[:], upto[:].rearrange("p e t -> p t e"), total[:], ALU.subtract))
                    link.wait()
                    link.did(dve.tensor_tensor(place[:], place[:], base[:].unsqueeze(1).to_broadcast([P, NT, E]), ALU.add))
                    link.wait()
                    link.did(dve.tensor_tensor(place[:].rearrange("p t e -> p (t e)"), p_c[:, 0, :],
                                               place[:].rearrange("p t e -> p (t e)"), ALU.add))
                    link.wait()
                    for k in range(TOP):
                        link.did(dve.tensor_tensor(chosen[:, :, k, :], picks[:, :, k, :], place[:], ALU.mult))
                    link.wait()
                    link.did(dve.tensor_reduce(slot_f[:], chosen[:], AX, ALU.add))
                    link.wait()
                    link.did(dve.tensor_copy(slot_of[:], slot_f[:]))
                    link.did(dve.tensor_tensor(past[:], table("slot").unsqueeze(2).to_broadcast([P, SLOTS, E]),
                                               end[:].unsqueeze(1).to_broadcast([P, SLOTS, E]), ALU.is_ge))
                    link.wait()
                    link.did(dve.tensor_reduce(past_n[:], past[:], AX, ALU.add))
                    link.wait()
                    link.did(dve.tensor_scalar(past_n[:], past_n[:], float(E - 1), None, ALU.min))
                    link.wait()
                    link.did(dve.tensor_copy(expert_of[:], past_n[:]))
                    link.wait()
                    dve.wait_ge(S["gates_ready"], 2)
                    with dve.Fori(0, NT // 4) as j:
                        def scatter_rows(q):
                            if q == 0:
                                dve.wait_ge(S["rows_in"], j * 16 + 17)
                            dve.tensor_copy(at[q][:], slot_of[:, bass.ds(j * 4 + q * 2, 2), :]).then_inc(S["routed"], 1)
                            for t in range(2):
                                for k in range(TOP):
                                    dve.tensor_scalar(rows[q][:, t, k, :], x_rows[:, 2 * q + t, :],
                                                            gate[:, j * 4 + 2 * q + t, k:k + 1], None,
                                                            ALU.mult).then_inc(S["rows_ready"], 1)

                        scatter_rows(0)
                        hid_out(dve, S, j * 2, 0)
                        scatter_rows(1)
                        hid_out(dve, S, j * 2 + 1, 1)
                        for i in range(2):
                            shared_add(dve, S, j * 2 + i, j * 2 + i)
                        for q in range(2):
                            dve.wait_ge(s_scat[q], j * 64 + 64)

                @block.gpsimd
                def _(pool):
                    for j in range(NT // 4):
                        for q in range(2):
                            pool.wait_ge(S["routed"], j * 2 + q + 2)
                            pool.wait_ge(S["rows_ready"], j * 8 + 4 * q + 5)
                            for t in range(2):
                                for k in range(TOP):
                                    pool.indirect_dma_start(xs_dram, bass.IndirectOffsetOnAxis(at[q][:, t, k:k + 1], 0),
                                                            rows[q][:, t, k, :], None).then_inc(s_scat[q], 16)
                    for q in range(2):
                        pool.wait_ge(s_scat[q], NT // 4 * 64)

            S = {n: sem(ctx, "c2_" + n) for n in FFN + ("y_stored0", "y_stored1")}
            start_at_one()
            with nc.Block() as block:
                @block.sync
                def _(sp):
                    for i in range(2):
                        sp.dma_start(x_in[i][:], xs_dram[i * P:(i + 1) * P, :]).then_inc(S[f"x_loaded{i}"], 16)

                    def store_y(c, i):
                        sp.wait_ge(S["y_out"], c + 2)
                        sp.dma_start(ys_dram[bass.ds(c * P, P), :], y_sb[i][:]).then_inc(S[f"y_stored{i}"], 16)

                    with sp.Fori(0, SLOTS // 2) as j:
                        for i in range(2):
                            s = j * 2 + 1 + i
                            sp.wait_ge(S["x_turned"], s + 1)
                            sp.dma_start(x_in[i][:], xs_dram[bass.ds((s + 1) * P, P), :]).then_inc(S[f"x_loaded{i}"], 16)
                            store_y(s - 1, i)
                    store_y(SLOTS - 1, 0)
                    for i in range(2):
                        sp.wait_ge(S[f"y_stored{i}"], 16 * ((SLOTS + 1 - i) // 2) + 1)
                        sp.wait_ge(S[f"x_loaded{i}"], 16 * (SLOTS // 2 + 1) + 1)

                @block.tensor
                def _(pe):
                    pe.wait_ge(s_w, 16 * 3 * E + 1)

                    def expert(s):
                        return pe.value_load(expert_of[0:1, bass.ds(s, 1)], min_val=0, max_val=E - 1)

                    turn_x(pe, S, 0, 0, 0)
                    first = expert(0)
                    up_mid(pe, S, 0, 0, first)
                    up_sw(pe, S, 0, 0, first)
                    turn_x(pe, S, 1, 1, 0)
                    with pe.Fori(0, SLOTS // 2) as j:
                        for i in range(2):
                            s, now, old = j * 2 + 1 + i, (1 + i) % 2, i
                            e = expert(s)
                            up_mid(pe, S, s, now, e)
                            turn_hid(pe, S, s - 1, old)
                            up_sw(pe, S, s, now, e)
                            turn_x(pe, S, s + 1, old, j + 1)
                            down(pe, S, s - 1, old, expert(s - 1))
                    turn_hid(pe, S, SLOTS - 1, 0)
                    down(pe, S, SLOTS - 1, 0, expert(SLOTS - 1))

                @block.scalar
                def _(act):
                    xT_out(act, S, 0, 0)
                    silu_out(act, S, 0, 0)
                    xT_out(act, S, 1, 1)
                    with act.Fori(0, SLOTS // 2) as j:
                        for i in range(2):
                            s, now, old = j * 2 + 1 + i, (1 + i) % 2, i
                            silu_out(act, S, s, now)
                            hidT_out(act, S, s - 1, old)
                            xT_out(act, S, s + 1, old)
                    hidT_out(act, S, SLOTS - 1, 0)

                @block.vector
                def _(dve):
                    def y_out(c, i, pair):
                        dve.wait_ge(S["y_summed"], c + 2)
                        dve.wait_ge(S[f"y_stored{i}"], pair * 16 + 1)
                        dve.tensor_copy(y_sb[i][:], p_y[:]).then_inc(S["y_out"], 1)

                    hid_out(dve, S, 0, 0)
                    with dve.Fori(0, SLOTS // 2) as j:
                        for i in range(2):
                            s, now, old = j * 2 + 1 + i, (1 + i) % 2, i
                            hid_out(dve, S, s, now)
                            y_out(s - 1, old, j)
                    y_out(SLOTS - 1, 0, SLOTS // 2)

            S = {n: sem(ctx, "c3_" + n) for n in FFN + ("routed", "rows_used", "added", "out_ready", "stored")}
            s_gath = [ctx.enter_context(nc.semaphore(f"gathered{i}")) for i in range(2)]
            start_at_one()
            with nc.Block() as block:
                @block.sync
                def _(sp):
                    with sp.Fori(0, NT // 4) as j:
                        sp.wait_ge(S["x_turned"], j * 2 + 1)
                        for i in range(2):
                            sp.dma_start(x_in[i][:], xn_dram[HALF + j * 2 + i]).then_inc(S[f"x_loaded{i}"], 16)
                        for q in range(2):
                            sp.wait_ge(S["out_ready"], j * 2 + q + 2)
                            sp.dma_start(out[bass.ds(j * 4 + 2 * q, 2)].rearrange("t p d -> p t d"),
                                         h[:, bass.ds(j * 4 + 2 * q, 2), :]).then_inc(S["stored"], 16)
                    sp.wait_ge(S["stored"], 16 * NT // 2 + 1)

                @block.tensor
                def _(pe):
                    with pe.Fori(0, NT // 4) as j:
                        shared_pe(pe, {**S, "pair": j}, j * 2)

                @block.scalar
                def _(act):
                    with act.Fori(0, NT // 4) as j:
                        shared_act(act, S, j * 2)

                @block.vector
                def _(dve):
                    with dve.Fori(0, NT // 4) as j:
                        def route(q):
                            dve.wait_ge(S["rows_used"], j * 2 + q + 1)
                            dve.tensor_copy(at[q][:], slot_of[:, bass.ds(j * 4 + q * 2, 2), :]).then_inc(S["routed"], 1)

                        def join(q):
                            dve.wait_ge(s_gath[q], j * 64 + 64)
                            tiles = h[:, bass.ds(j * 4 + 2 * q, 2), :]
                            dve.tensor_tensor(rows[q][:, :, 0, :], rows[q][:, :, 0, :], rows[q][:, :, 1, :],
                                              ALU.add).then_inc(S["added"], 1)
                            dve.wait_ge(S["added"], j * 2 + q + 2)
                            dve.wait_ge(S["y_out"], j * 2 + 3)
                            dve.tensor_tensor(tiles, rows[q][:, :, 0, :], tiles, ALU.add).then_inc(S["out_ready"], 1)

                        for q in range(2):
                            dve.tensor_copy(at[q][:], slot_of[:, bass.ds(j * 4 + q * 2, 2), :]).then_inc(S["routed"], 1)
                        for i in range(2):
                            hid_out(dve, S, j * 2 + i, i)
                        for i in range(2):
                            shared_add(dve, S, j * 2 + i, HALF + j * 2 + i)
                        for q in range(2):
                            join(q)

                @block.gpsimd
                def _(pool):
                    for j in range(NT // 4):
                        for q in range(2):
                            if j:
                                pool.wait_ge(S["out_ready"], j * 2 + q)
                            pool.wait_ge(S["routed"], j * 2 + q + 2)
                            for t in range(2):
                                for k in range(TOP):
                                    pool.indirect_dma_start(rows[q][:, t, k, :], None, ys_dram,
                                                            bass.IndirectOffsetOnAxis(at[q][:, t, k:k + 1], 0)
                                                            ).then_inc(s_gath[q], 16)


def lay_out(a):
    k, n = a.shape
    return np.ascontiguousarray(a.reshape(k // P, P, n).transpose(1, 0, 2))


def kernel(**inputs):
    import concourse.bacc as _bacc
    from concourse.bass_utils import run_bass_kernel_spmd as _run

    x = {k: np.asarray(v) for k, v in inputs.items()}
    a, f = "L0_attn_", "L0_ffn_"
    const, where = consts()
    qkv = ("k", "q", "v")
    arrays = {
        "ids": np.ascontiguousarray(x["x"].reshape(NT, P).T),
        "emb": x["L0_tok_embeddings"],
        "wqkv": np.stack([lay_out(x[f"{a}W{n}"].T) for n in qkv], 2),
        "wbeta": lay_out(x[a + "Wbeta"].T),
        "wout": lay_out(x[a + "Wout"].T),
        "router": lay_out(x[f + "router_DE"]),
        "conv_w": np.stack([lay_out(x[f"{a}conv_{n}"]) for n in qkv], 1),
        "qkv_b": np.stack([x[f"{a}b{n}"].reshape(KH, P).T for n in qkv], 1),
        "bbeta": np.broadcast_to(x[a + "bbeta"], (P, H)),
        "bout": np.broadcast_to(x[a + "bout"], (P, D)),
        "rms": np.tile(x[a + "rms_w"], P // DH).reshape(P, 1),
        "const": const,
        "w_in": np.stack([lay_out(w) for w in (*x[f + "w_in_eDF"], x[f + "w_in_shared_FD"].T)]),
        "w_sw": np.stack([lay_out(w) for w in (*x[f + "w_swiglu_eDF"], x[f + "w_swiglu_FD"].T)]),
        "w_out": np.stack([lay_out(w) for w in (*x[f + "w_out_eFD"], x[f + "w_out_shared_DF"].T)]),
    }
    arrays = {n: np.ascontiguousarray(v) for n, v in arrays.items()}
    nc = _bacc.Bacc("TRN2", target_bir_lowering=False, num_devices=1)
    args = [nc.dram_tensor(f"in_{n}", v.shape, mybir.dt.from_np(v.dtype), kind="ExternalInput").ap()
            for n, v in arrays.items()]
    out = nc.dram_tensor("out_h", [NT, P, D], F32, kind="ExternalOutput").ap()
    build(nc, *args, out, where)
    r = _run(nc, [{f"in_{n}": v for n, v in arrays.items()}], core_ids=[0])
    return r.results[0]["out_h"].reshape(B, L, D)
```
